# Optimizing a Trainium2 kernel written in Bass

```python
import numpy as np
import jax
import jax.numpy as jnp

def _softmax(x, axis=-1):
    return jax.nn.softmax(x, axis=axis)

def _gelu(x):
    return jax.nn.gelu(x, approximate=True)

def _silu(x):
    return jax.nn.silu(x)

def _sigmoid(x):
    return jax.nn.sigmoid(x)

def _layernorm(x, axis=-1, eps=1e-05):
    m = jnp.mean(x, axis=axis, keepdims=True)
    v = jnp.var(x, axis=axis, keepdims=True)
    return (x - m) / jnp.sqrt(v + eps)

def _scatter_add(tgt, idx, src, axis=0):
    return tgt.at[idx].add(src)

def _segment_sum(src, seg, n):
    return jax.ops.segment_sum(src, seg, n)
kernel_name = 'mk_adaln_d2_jaxref_r8_0ae4ef'

def setup_inputs(seed: int=0):
    np.random.seed(seed)
    _w = jnp.asarray

    def _L0_attn_setup():
        import jax, jax.numpy as jnp
        import numpy as np
        D_MODEL, D_STATE, DT_RANK = (128, 16, 64)
        B, L = (4, 1024)
        key = jax.random.key(seed)
        ks = jax.random.split(key, 8)
        s = 0.02
        return {'x': jax.random.normal(ks[0], (B, L, D_MODEL), dtype=jnp.float32), 'Wxproj': jax.random.normal(ks[1], (DT_RANK + 2 * D_STATE, D_MODEL), dtype=jnp.float32) * s, 'Wdt': jax.random.normal(ks[2], (1, DT_RANK), dtype=jnp.float32) * s, 'bdt': jax.random.normal(ks[3], (1,), dtype=jnp.float32) * s, 'Wxs': jax.random.normal(ks[4], (D_STATE, D_MODEL), dtype=jnp.float32) * s, 'A_log': jnp.arange(1, D_STATE + 1, dtype=jnp.float32)[None, :], 'Wout': jax.random.normal(ks[5], (D_MODEL, D_STATE), dtype=jnp.float32) * s, 'Dp': jnp.ones((D_MODEL,), dtype=jnp.float32)}
    _L0_attn_in = _L0_attn_setup()

    def _L0_ffn_setup():
        import jax, jax.numpy as jnp
        import numpy as np
        TOPK = 4
        N_GROUPS = 4
        TOPK_GROUPS = 2
        ROUTE_SCALE = 2.5

        def _gate(x2, Wg):
            T = x2.shape[0]
            E = Wg.shape[0]
            scores = x2 @ Wg.T
            s = jax.nn.sigmoid(scores)
            g = s.reshape(T, N_GROUPS, E // N_GROUPS)
            group_scores = g.max(axis=-1)
            _, gidx = jax.lax.top_k(group_scores, TOPK_GROUPS)
            group_mask = jnp.any(jax.nn.one_hot(gidx, N_GROUPS, dtype=jnp.bool_), axis=1)
            masked = jnp.where(group_mask[:, :, None], g, -jnp.inf).reshape(T, E)
            _, idx = jax.lax.top_k(masked, TOPK)
            w = jnp.take_along_axis(s, idx, axis=1)
            w = w / jnp.sum(w, axis=-1, keepdims=True)
            w = w * ROUTE_SCALE
            return (w.astype(x2.dtype), idx)
        key = jax.random.key(seed)
        ks = jax.random.split(key, 6)
        B, S, D, I, E = (2, 256, 128, 128, 16)
        scale = 0.02
        return {'x': jax.random.normal(ks[0], (B, S, D), dtype=jnp.float32), 'Wg': jax.random.normal(ks[1], (E, D), dtype=jnp.float32) * scale, 'W1': jax.random.normal(ks[2], (E, I, D), dtype=jnp.float32) * scale, 'b1': jnp.zeros((E, I), dtype=jnp.float32), 'W2': jax.random.normal(ks[3], (E, D, I), dtype=jnp.float32) * scale, 'b2': jnp.zeros((E, D), dtype=jnp.float32), 'W3': jax.random.normal(ks[4], (E, I, D), dtype=jnp.float32) * scale, 'b3': jnp.zeros((E, I), dtype=jnp.float32)}
    _L0_ffn_in = _L0_ffn_setup()
    _L0_c = _w((lambda *s: np.random.randn(*s).astype(np.float32) * 0.05)(4, 128))
    _L0_wmod = _w((lambda *s: np.random.randn(*s).astype(np.float32) * 0.05)(128, 6 * 128) * 128 ** (-0.5))

    def _L1_attn_setup():
        import math
        import jax, jax.numpy as jnp
        import numpy as np
        B, T, D, NH = (4, 256, 128, 16)
        HS = D // NH
        N_BUCKETS = 32
        MAX_DIST = 128

        def _relative_position_bucket(rp):
            nb = N_BUCKETS // 2
            buckets = (rp > 0).astype(jnp.int32) * nb
            rp = jnp.abs(rp)
            max_exact = nb // 2
            is_small = rp < max_exact
            me = max_exact - 1
            nbm = nb - 1
            rp_safe = jnp.maximum(rp, 1).astype(jnp.float32)
            rp_large = me + (jnp.log(rp_safe / me) / math.log(MAX_DIST / me) * (nbm - me)).astype(jnp.int32)
            rp_large = jnp.minimum(rp_large, nbm)
            buckets = buckets + jnp.where(is_small, rp, rp_large)
            return buckets

        def compute_bias(rel_emb, qT, kT):
            ctx = jnp.arange(qT, dtype=jnp.int32)[:, None]
            mem = jnp.arange(kT, dtype=jnp.int32)[None, :]
            bucket = _relative_position_bucket(mem - ctx)
            values = rel_emb[bucket]
            return jnp.transpose(values, (2, 0, 1))[None]
        key = jax.random.key(seed)
        ks = jax.random.split(key, 6)
        s = 0.02
        return {'queries': jax.random.normal(ks[0], (B, T, D), jnp.float32), 'Wq': jax.random.normal(ks[1], (D, D), jnp.float32) * s, 'Wk': jax.random.normal(ks[2], (D, D), jnp.float32) * s, 'Wv': jax.random.normal(ks[3], (D, D), jnp.float32) * s, 'Wo': jax.random.normal(ks[4], (D, D), jnp.float32) * s, 'rel_emb': jax.random.normal(ks[5], (N_BUCKETS, NH), jnp.float32) * s}
    _L1_attn_in = _L1_attn_setup()

    def _L1_ffn_setup():
        import math
        import jax, jax.numpy as jnp
        import numpy as np
        B, S, D, H, E, F = (2, 128, 128, 16, 16, 512)
        HEAD = D // H
        MOE_TOKEN_DROPOUT = 0.2
        EPS = 1e-05

        def layer_norm(x, w, b):
            mu = x.mean(-1, keepdims=True)
            var = ((x - mu) ** 2).mean(-1, keepdims=True)
            return (x - mu) * jax.lax.rsqrt(var + EPS) * w + b
        key = jax.random.key(seed)
        ks = jax.random.split(key, 16)
        w = lambda k, shape: jax.random.normal(k, shape, jnp.float32) * 0.02
        return {'hidden_states': jax.random.normal(ks[0], (B, S, D), jnp.float32), 'ln1_w': jnp.ones((D,), jnp.float32), 'ln1_b': jnp.zeros((D,), jnp.float32), 'q_w': w(ks[1], (D, D)), 'q_b': jnp.zeros((D,), jnp.float32), 'k_w': w(ks[2], (D, D)), 'k_b': jnp.zeros((D,), jnp.float32), 'v_w': w(ks[3], (D, D)), 'v_b': jnp.zeros((D,), jnp.float32), 'o_w': w(ks[4], (D, D)), 'o_b': jnp.zeros((D,), jnp.float32), 'ln2_w': jnp.ones((D,), jnp.float32), 'ln2_b': jnp.zeros((D,), jnp.float32), 'router_w': w(ks[5], (D, E)), 'fc1_w': w(ks[6], (E, D, F)), 'fc1_b': jnp.zeros((E, F), jnp.float32), 'fc2_w': w(ks[7], (E, F, D)), 'fc2_b': jnp.zeros((E, D), jnp.float32)}
    _L1_ffn_in = _L1_ffn_setup()
    _L1_c = _w((lambda *s: np.random.randn(*s).astype(np.float32) * 0.05)(4, 128))
    _L1_wmod = _w((lambda *s: np.random.randn(*s).astype(np.float32) * 0.05)(128, 6 * 128) * 128 ** (-0.5))
    _d = {'L0_attn_x': _L0_attn_in['x'], 'L0_attn_Wxproj': _L0_attn_in['Wxproj'], 'L0_attn_Wdt': _L0_attn_in['Wdt'], 'L0_attn_bdt': _L0_attn_in['bdt'], 'L0_attn_Wxs': _L0_attn_in['Wxs'], 'L0_attn_A_log': _L0_attn_in['A_log'], 'L0_attn_Wout': _L0_attn_in['Wout'], 'L0_attn_Dp': _L0_attn_in['Dp'], 'L0_ffn_Wg': _L0_ffn_in['Wg'], 'L0_ffn_W1': _L0_ffn_in['W1'], 'L0_ffn_b1': _L0_ffn_in['b1'], 'L0_ffn_W2': _L0_ffn_in['W2'], 'L0_ffn_b2': _L0_ffn_in['b2'], 'L0_ffn_W3': _L0_ffn_in['W3'], 'L0_ffn_b3': _L0_ffn_in['b3'], 'L0_c': _L0_c, 'L0_wmod': _L0_wmod, 'L1_attn_Wq': _L1_attn_in['Wq'], 'L1_attn_Wk': _L1_attn_in['Wk'], 'L1_attn_Wv': _L1_attn_in['Wv'], 'L1_attn_Wo': _L1_attn_in['Wo'], 'L1_attn_rel_emb': _L1_attn_in['rel_emb'], 'L1_ffn_ln1_w': _L1_ffn_in['ln1_w'], 'L1_ffn_ln1_b': _L1_ffn_in['ln1_b'], 'L1_ffn_q_w': _L1_ffn_in['q_w'], 'L1_ffn_q_b': _L1_ffn_in['q_b'], 'L1_ffn_k_w': _L1_ffn_in['k_w'], 'L1_ffn_k_b': _L1_ffn_in['k_b'], 'L1_ffn_v_w': _L1_ffn_in['v_w'], 'L1_ffn_v_b': _L1_ffn_in['v_b'], 'L1_ffn_o_w': _L1_ffn_in['o_w'], 'L1_ffn_o_b': _L1_ffn_in['o_b'], 'L1_ffn_ln2_w': _L1_ffn_in['ln2_w'], 'L1_ffn_ln2_b': _L1_ffn_in['ln2_b'], 'L1_ffn_router_w': _L1_ffn_in['router_w'], 'L1_ffn_fc1_w': _L1_ffn_in['fc1_w'], 'L1_ffn_fc1_b': _L1_ffn_in['fc1_b'], 'L1_ffn_fc2_w': _L1_ffn_in['fc2_w'], 'L1_ffn_fc2_b': _L1_ffn_in['fc2_b'], 'L1_c': _L1_c, 'L1_wmod': _L1_wmod}
    _x0 = _d['L0_attn_x']
    _d['L0_attn_x'] = jax.random.normal(jax.random.fold_in(jax.random.key(seed), 1), (4, 1024, 128), dtype=_x0.dtype)
    del _x0
    return _d

def reference(L0_attn_x, L0_attn_Wxproj, L0_attn_Wdt, L0_attn_bdt, L0_attn_Wxs, L0_attn_A_log, L0_attn_Wout, L0_attn_Dp, L0_ffn_Wg, L0_ffn_W1, L0_ffn_b1, L0_ffn_W2, L0_ffn_b2, L0_ffn_W3, L0_ffn_b3, L0_c, L0_wmod, L1_attn_Wq, L1_attn_Wk, L1_attn_Wv, L1_attn_Wo, L1_attn_rel_emb, L1_ffn_ln1_w, L1_ffn_ln1_b, L1_ffn_q_w, L1_ffn_q_b, L1_ffn_k_w, L1_ffn_k_b, L1_ffn_v_w, L1_ffn_v_b, L1_ffn_o_w, L1_ffn_o_b, L1_ffn_ln2_w, L1_ffn_ln2_b, L1_ffn_router_w, L1_ffn_fc1_w, L1_ffn_fc1_b, L1_ffn_fc2_w, L1_ffn_fc2_b, L1_c, L1_wmod):

    def _L0_attn_ref(x, Wxproj, Wdt, bdt, Wxs, A_log, Wout, Dp):
        import jax, jax.numpy as jnp
        import numpy as np
        D_MODEL, D_STATE, DT_RANK = (128, 16, 64)
        B, L = (4, 1024)
        dt_rank = Wdt.shape[1]
        N = A_log.shape[1]
        Bsz = x.shape[0]
        proj = jnp.einsum('bld,pd->blp', x, Wxproj)
        dt_part = proj[..., :dt_rank]
        B_part = proj[..., dt_rank:dt_rank + N]
        C_part = proj[..., dt_rank + N:]
        dt = jax.nn.softplus(jnp.einsum('blr,or->blo', dt_part, Wdt) + bdt)
        A = -jnp.exp(A_log)
        A_bar = jnp.exp(dt * A)
        Bx = dt * B_part * jnp.einsum('bld,nd->bln', x, Wxs)

        def step(h, inp):
            a_t, bx_t = inp
            h = a_t * h + bx_t
            return (h, h)
        h0 = jnp.zeros((Bsz, N), dtype=x.dtype)
        _, hs = jax.lax.scan(step, h0, (jnp.swapaxes(A_bar, 0, 1), jnp.swapaxes(Bx, 0, 1)))
        hc = hs * jnp.swapaxes(C_part, 0, 1)
        y = jnp.einsum('lbn,dn->bld', hc, Wout)
        return y + Dp * x

    def _L0_ffn_ref(x, Wg, W1, b1, W2, b2, W3, b3):
        import jax, jax.numpy as jnp
        import numpy as np
        TOPK = 4
        N_GROUPS = 4
        TOPK_GROUPS = 2
        ROUTE_SCALE = 2.5

        def _gate(x2, Wg):
            T = x2.shape[0]
            E = Wg.shape[0]
            scores = x2 @ Wg.T
            s = jax.nn.sigmoid(scores)
            g = s.reshape(T, N_GROUPS, E // N_GROUPS)
            group_scores = g.max(axis=-1)
            _, gidx = jax.lax.top_k(group_scores, TOPK_GROUPS)
            group_mask = jnp.any(jax.nn.one_hot(gidx, N_GROUPS, dtype=jnp.bool_), axis=1)
            masked = jnp.where(group_mask[:, :, None], g, -jnp.inf).reshape(T, E)
            _, idx = jax.lax.top_k(masked, TOPK)
            w = jnp.take_along_axis(s, idx, axis=1)
            w = w / jnp.sum(w, axis=-1, keepdims=True)
            w = w * ROUTE_SCALE
            return (w.astype(x2.dtype), idx)
        shape = x.shape
        D = shape[-1]
        x2 = x.reshape(-1, D)
        weights, indices = _gate(x2, Wg)
        E = Wg.shape[0]
        y = jnp.zeros_like(x2)
        for e in range(E):
            we = jnp.sum(weights * (indices == e), axis=-1)
            h = jax.nn.silu(x2 @ W1[e].T + b1[e]) * (x2 @ W3[e].T + b3[e])
            y = y + (h @ W2[e].T + b2[e]) * we[:, None]
        return y.reshape(shape)

    def _L1_attn_ref(queries, Wq, Wk, Wv, Wo, rel_emb):
        import math
        import jax, jax.numpy as jnp
        import numpy as np
        B, T, D, NH = (4, 256, 128, 16)
        HS = D // NH
        N_BUCKETS = 32
        MAX_DIST = 128

        def _relative_position_bucket(rp):
            nb = N_BUCKETS // 2
            buckets = (rp > 0).astype(jnp.int32) * nb
            rp = jnp.abs(rp)
            max_exact = nb // 2
            is_small = rp < max_exact
            me = max_exact - 1
            nbm = nb - 1
            rp_safe = jnp.maximum(rp, 1).astype(jnp.float32)
            rp_large = me + (jnp.log(rp_safe / me) / math.log(MAX_DIST / me) * (nbm - me)).astype(jnp.int32)
            rp_large = jnp.minimum(rp_large, nbm)
            buckets = buckets + jnp.where(is_small, rp, rp_large)
            return buckets

        def compute_bias(rel_emb, qT, kT):
            ctx = jnp.arange(qT, dtype=jnp.int32)[:, None]
            mem = jnp.arange(kT, dtype=jnp.int32)[None, :]
            bucket = _relative_position_bucket(mem - ctx)
            values = rel_emb[bucket]
            return jnp.transpose(values, (2, 0, 1))[None]
        b, t, d = queries.shape

        def split_heads(x):
            return jnp.transpose(x.reshape(b, t, NH, HS), (0, 2, 1, 3))
        q = split_heads(queries @ Wq.T)
        k = split_heads(queries @ Wk.T)
        v = split_heads(queries @ Wv.T)
        att = jnp.einsum('bhqd,bhkd->bhqk', q, k) * (1.0 / math.sqrt(HS))
        att = att + compute_bias(rel_emb, t, t)
        att = jax.nn.softmax(att, axis=-1)
        o = jnp.einsum('bhqk,bhkd->bhqd', att, v)
        o = jnp.transpose(o, (0, 2, 1, 3)).reshape(b, t, d)
        return o @ Wo.T

    def _L1_ffn_ref(hidden_states, ln1_w, ln1_b, q_w, q_b, k_w, k_b, v_w, v_b, o_w, o_b, ln2_w, ln2_b, router_w, fc1_w, fc1_b, fc2_w, fc2_b):
        import math
        import jax, jax.numpy as jnp
        import numpy as np
        B, S, D, H, E, F = (2, 128, 128, 16, 16, 512)
        HEAD = D // H
        MOE_TOKEN_DROPOUT = 0.2
        EPS = 1e-05

        def layer_norm(x, w, b):
            mu = x.mean(-1, keepdims=True)
            var = ((x - mu) ** 2).mean(-1, keepdims=True)
            return (x - mu) * jax.lax.rsqrt(var + EPS) * w + b
        b, s, _ = hidden_states.shape
        T = b * s
        neg = jnp.finfo(jnp.float32).min
        resid = hidden_states
        x = layer_norm(hidden_states, ln1_w, ln1_b)
        q = (x @ q_w + q_b) / math.sqrt(HEAD)
        k = x @ k_w + k_b
        v = x @ v_w + v_b
        split = lambda t: t.reshape(b, s, H, HEAD).transpose(0, 2, 1, 3)
        q, k, v = (split(q), split(k), split(v))
        scores = jnp.einsum('bhqd,bhkd->bhqk', q, k)
        causal = jnp.tril(jnp.ones((s, s), bool))
        scores = jnp.where(causal, scores, neg)
        attn = jax.nn.softmax(scores, axis=-1)
        ctx = jnp.einsum('bhqk,bhkd->bhqd', attn, v)
        ctx = ctx.transpose(0, 2, 1, 3).reshape(b, s, D)
        hidden = resid + (ctx @ o_w + o_b)
        resid = hidden
        xt = layer_norm(hidden, ln2_w, ln2_b).reshape(T, D)
        logits = xt @ router_w
        probs = jax.nn.softmax(logits, axis=-1)
        top1 = jnp.argmax(probs, axis=-1)
        m1 = jax.nn.one_hot(top1, E, dtype=jnp.float32)
        logits_no1 = jnp.where(m1 > 0, -jnp.inf, logits)
        top2 = jnp.argmax(logits_no1, axis=-1)
        m2 = jax.nn.one_hot(top2, E, dtype=jnp.float32)
        loc1 = jnp.cumsum(m1, axis=0) - 1.0
        loc2 = jnp.cumsum(m2, axis=0) - 1.0 + m1.sum(axis=0, keepdims=True)
        C = 2 * math.ceil(T / E)
        m1 = m1 * (loc1 < C)
        m2 = m2 * (loc2 < C)
        g1 = (probs * m1).sum(-1)
        g2 = (probs * m2).sum(-1)
        denom = jnp.maximum(g1 + g2, jnp.finfo(jnp.float32).eps)
        g1, g2 = (g1 / denom, g2 / denom)
        slot1 = (loc1 * m1).sum(-1).astype(jnp.int32)
        slot2 = (loc2 * m2).sum(-1).astype(jnp.int32)
        d1 = m1[:, :, None] * jax.nn.one_hot(slot1, C, dtype=jnp.float32)[:, None, :]
        d2 = m2[:, :, None] * jax.nn.one_hot(slot2, C, dtype=jnp.float32)[:, None, :]
        dispatch = d1 + d2
        combine = g1[:, None, None] * d1 + g2[:, None, None] * d2
        xin = jnp.einsum('tec,td->ecd', dispatch, xt)
        h = jnp.einsum('ecd,edf->ecf', xin, fc1_w) + fc1_b[:, None, :]
        h = jax.nn.gelu(h, approximate=False)
        eout = jnp.einsum('ecf,efd->ecd', h, fc2_w) + fc2_b[:, None, :]
        eout = eout * (1.0 - MOE_TOKEN_DROPOUT)
        moe_out = jnp.einsum('tec,ecd->td', combine, eout).reshape(b, s, D)
        return resid + moe_out
    x = L0_attn_x
    mod = (_silu(L0_c) @ L0_wmod).reshape(L0_c.shape[0], 6, 1, -1)
    sa, ca, ga, sb, cb, gb = (mod[:, 0], mod[:, 1], mod[:, 2], mod[:, 3], mod[:, 4], mod[:, 5])
    ga = (2 * (ga >= 0) - 1) * jnp.maximum(jnp.abs(ga), 0.25)
    gb = (2 * (gb >= 0) - 1) * jnp.maximum(jnp.abs(gb), 0.25)
    h = _layernorm(x, axis=-1) * (1 + ca) + sa
    x = x + ga * _L0_attn_ref(h, L0_attn_Wxproj, L0_attn_Wdt, L0_attn_bdt, L0_attn_Wxs, L0_attn_A_log, L0_attn_Wout, L0_attn_Dp)
    h = _layernorm(x, axis=-1) * (1 + cb) + sb
    x = x + gb * _L0_ffn_ref(h, L0_ffn_Wg, L0_ffn_W1, L0_ffn_b1, L0_ffn_W2, L0_ffn_b2, L0_ffn_W3, L0_ffn_b3)
    mod = (_silu(L1_c) @ L1_wmod).reshape(L1_c.shape[0], 6, 1, -1)
    sa, ca, ga, sb, cb, gb = (mod[:, 0], mod[:, 1], mod[:, 2], mod[:, 3], mod[:, 4], mod[:, 5])
    ga = (2 * (ga >= 0) - 1) * jnp.maximum(jnp.abs(ga), 0.25)
    gb = (2 * (gb >= 0) - 1) * jnp.maximum(jnp.abs(gb), 0.25)
    h = _layernorm(x, axis=-1) * (1 + ca) + sa
    x = x + ga * _L1_attn_ref(h, L1_attn_Wq, L1_attn_Wk, L1_attn_Wv, L1_attn_Wo, L1_attn_rel_emb)
    h = _layernorm(x, axis=-1) * (1 + cb) + sb
    x = x + gb * _L1_ffn_ref(h, L1_ffn_ln1_w, L1_ffn_ln1_b, L1_ffn_q_w, L1_ffn_q_b, L1_ffn_k_w, L1_ffn_k_b, L1_ffn_v_w, L1_ffn_v_b, L1_ffn_o_w, L1_ffn_o_b, L1_ffn_ln2_w, L1_ffn_ln2_b, L1_ffn_router_w, L1_ffn_fc1_w, L1_ffn_fc1_b, L1_ffn_fc2_w, L1_ffn_fc2_b)
    return x

_drawn_inputs = setup_inputs


def setup_inputs(seed=0):
    import zlib

    import numpy as np

    out = dict(_drawn_inputs(seed))
    spreads = {'L0_attn_Dp': (1.0, 0.2),
     'L0_ffn_b1': (0.0, 0.8),
     'L0_ffn_b2': (0.0, 0.1),
     'L0_ffn_b3': (0.0, 0.8),
     'L1_ffn_ln1_w': (1.0, 0.6),
     'L1_ffn_ln1_b': (0.0, 0.8),
     'L1_ffn_q_b': (0.0, 0.8),
     'L1_ffn_k_b': (0.0, 2.0),
     'L1_ffn_v_b': (0.0, 0.8),
     'L1_ffn_o_b': (0.0, 0.339),
     'L1_ffn_ln2_w': (1.0, 0.6),
     'L1_ffn_ln2_b': (0.0, 0.8),
     'L1_ffn_fc1_b': (0.0, 0.8),
     'L1_ffn_fc2_b': (0.0, 0.522)}
    factors = {'L0_attn_Wxproj': 8.0,
     'L0_attn_Wdt': 8.0,
     'L0_attn_Wxs': 8.0,
     'L0_attn_A_log': 47.957,
     'L0_attn_Wout': 8.0,
     'L0_ffn_W1': 8.0,
     'L0_ffn_W2': 8.0,
     'L0_ffn_W3': 8.0,
     'L1_attn_Wq': 8.0,
     'L1_attn_Wk': 8.0,
     'L1_attn_Wv': 8.0,
     'L1_attn_Wo': 8.0,
     'L1_attn_rel_emb': 8.0,
     'L1_ffn_q_w': 8.0,
     'L1_ffn_k_w': 8.0,
     'L1_ffn_v_w': 8.0,
     'L1_ffn_o_w': 8.0,
     'L1_ffn_router_w': 3.367,
     'L1_ffn_fc1_w': 6.736,
     'L1_ffn_fc2_w': 6.109}
    for name, (base, spread) in spreads.items():
        noise = np.random.default_rng([zlib.crc32(name.encode()), seed]).standard_normal(out[name].shape)
        drawn = base * np.exp(spread * noise) if base else spread * noise
        out[name] = jnp.asarray(drawn.astype(out[name].dtype))
    for name, factor in factors.items():
        out[name] = (out[name] * factor).astype(out[name].dtype)
    return out
```

```python
from contextlib import ExitStack

import concourse.bass as bass
from concourse import mybir

F32 = mybir.dt.float32
BF16 = mybir.dt.bfloat16
I32 = mybir.dt.int32
ALU = mybir.AluOpType
ACT = mybir.ActivationFunctionType
AX = mybir.AxisListType

P = 128
B, L, D = 4, 1024, 128
TOK = B * L
NT = TOK // P
TB = L // P
CH = 512
NCH = TOK // CH
EPS = 1e-5

NST = 16
RANK = 64
SP = 32
E = 16
H, HD = 16, 8
HG = 4
NG = H // HG
VA = HD + 1
NBK = 32
STRIP = 512
NEAR = 3 * P
FF = 512
CAP = 2 * (TOK // E)
KEEP = 1.0 - 0.2
NEG = -1.0e30

C_ID, C_TRI, C_MA, C_MB = 0, 128, 256, 384
C_FIRST, C_SLOT, C_SEL, C_OH = 512, 528, 544, 560
C_FLIP = C_OH + STRIP
C_W = C_FLIP + P

SA, CA, GA, SB, CB, GB = range(6)


class Chain:

    def __init__(self, eng, sem):
        self.eng, self.sem, self.at, self.base = eng, sem, 0, 0

    def link(self, ins):
        ins.then_inc(self.sem, 1)
        self.at += 1
        self.eng.wait_ge(self.sem, self.base + self.at)


def col(tensor, t):
    return tensor[:, bass.ds(t, 1)]


class Core:
    pass


def load_and_modulate(nc, k, m):
    with ExitStack() as c:
        cT = c.enter_context(nc.sbuf_tensor("cT", [P, 2, B], F32))
        cS = c.enter_context(nc.sbuf_tensor("cS", [P, 2, B], F32))
        wm = c.enter_context(nc.sbuf_tensor("wm", [P, 2, 6 * D], F32))
        diag = c.enter_context(nc.sbuf_tensor("diag", [P, 5, B, D], F32))
        t0 = c.enter_context(nc.sbuf_tensor("modt0", [P, 2, 2, B], F32))
        t1 = c.enter_context(nc.sbuf_tensor("modt1", [P, 2, 2, B], F32))
        t2 = c.enter_context(nc.sbuf_tensor("modt2", [P, 2, 2, B], F32))
        loaded = nc.alloc_semaphore("loaded")
        xloaded = nc.alloc_semaphore("xloaded")
        silu_done = nc.alloc_semaphore("silu_done")
        mod_ready = nc.alloc_semaphore("mod_ready")
        ones_ready = nc.alloc_semaphore("ones_ready")
        chain = nc.alloc_semaphore("mod_chain")
        diag_ready = nc.alloc_semaphore("diag_ready")
        rows_ready = nc.alloc_semaphore("rows_ready")
        rows_kept = nc.alloc_semaphore("rows_kept")
        pm = k.ps[:, 7, 0:2 * 6 * B].rearrange("p (l r b) -> p l r b", l=2, r=6)
        with nc.Block() as block:
            @block.sync
            def _(sp):
                sp.dma_start(cT[:, 0, :], m["c0T"]).then_inc(loaded, 16)
                sp.dma_start(cT[:, 1, :], m["c1T"]).then_inc(loaded, 16)
                sp.dma_start(k.cst[:], m["consts"]).then_inc(loaded, 16)
                sp.dma_start(wm[:, 0, :], m["L0_wmod"]).then_inc(loaded, 16)
                sp.dma_start(wm[:, 1, :], m["L1_wmod"]).then_inc(loaded, 16)
                sp.dma_start(k.x[:], m["x"].rearrange("b (t p) d -> p (b t) d", p=P)).then_inc(xloaded, 16)
                sp.wait_ge(xloaded, 16)

            @block.scalar
            def _(act):
                act.wait_ge(loaded, 5 * 16)
                nc.scalar.activation(cS[:], cT[:], ACT.Silu).then_inc(silu_done, 1)
                for i in range(5):
                    act.wait_ge(rows_ready, i + 1)
                    nc.scalar.copy(k.row[:, i, :, :].rearrange("p b d -> p (b d)"), k.ps[:, i, :]).then_inc(rows_kept, 1)

            @block.tensor
            def _(pe):
                pe.wait_ge(silu_done, 1)
                for l in range(2):
                    for r in range(6):
                        ins = nc.tensor.matmul(pm[:, l, r, :], wm[:, l, r * D:(r + 1) * D], cS[:, l, :],
                                               start=True, stop=True)
                ins.then_inc(mod_ready, 1)
                pe.wait_ge(ones_ready, 1)
                for i in range(5):
                    pe.wait_ge(diag_ready, 4 * (i + 1))
                    nc.tensor.matmul(k.ps[:, i, :], k.ones[:], diag[:, i, :, :].rearrange("p b d -> p (b d)"),
                                     start=True, stop=True).then_inc(rows_ready, 1)

            @block.vector
            def _(dve):
                ch = Chain(dve, chain)
                nc.vector.memset(k.ones[:], 1.0).then_inc(ones_ready, 1)
                dve.wait_ge(mod_ready, 1)
                ch.link(nc.vector.tensor_copy(k.mod[:], pm))
                ch.link(nc.vector.tensor_scalar(k.mod[:, :, CA::3, :], k.mod[:, :, CA::3, :], 1.0, None, ALU.add))
                g = k.mod[:, :, GA::3, :]
                ch.link(nc.vector.tensor_scalar(t0[:], g, 0.0, None, ALU.is_ge))
                ch.link(nc.vector.tensor_scalar(t1[:], g, 0.25, None, ALU.max))
                ch.link(nc.vector.tensor_tensor(t1[:], t1[:], t0[:], ALU.mult))
                ch.link(nc.vector.tensor_scalar(t0[:], g, 0.0, None, ALU.is_lt))
                ch.link(nc.vector.tensor_scalar(t2[:], g, -0.25, None, ALU.min))
                ch.link(nc.vector.tensor_tensor(t2[:], t2[:], t0[:], ALU.mult))
                ch.link(nc.vector.tensor_tensor(g, t1[:], t2[:], ALU.add))
                for i, (l, r) in enumerate(k.row_of):
                    for b in range(B):
                        nc.vector.tensor_scalar(diag[:, i, b, :], k.cst[:, C_ID:C_ID + D], k.mod[:, l, r, b:b + 1],
                                                None, ALU.mult).then_inc(diag_ready, 1)
                nc.vector.tensor_copy(k.cstb[:], k.cst[:, 0:C_FIRST])
                nc.vector.tensor_copy(k.selb[:], k.cst[0:3 * E, C_SEL:C_SEL + E].unsqueeze(2).broadcast_to([3 * E, E, P]))


def statistics(nc, dve, ch, src, stats, mean, var, dif, counted, var_ready):
    with dve.Fori(0, NT // 4) as i:
        for j in range(4):
            nc.vector.bn_stats(stats[:, 4 * i + j, :], src[:, 4 * i + j, :]).then_inc(counted, 1)
    dve.wait_ge(counted, NT)
    me, mo, qe, qo = (stats[:, :, j] for j in (1, 4, 2, 5))
    ch.link(nc.vector.tensor_tensor(mean[:], me, mo, ALU.add))
    ch.link(nc.vector.tensor_tensor(dif[:], me, mo, ALU.subtract))
    ch.link(nc.vector.tensor_tensor(var[:], qe, qo, ALU.add))
    ch.link(nc.vector.tensor_scalar(mean[:], mean[:], 0.5, None, ALU.mult))
    ch.link(nc.vector.tensor_tensor(dif[:], dif[:], dif[:], ALU.mult))
    ch.link(nc.vector.tensor_scalar(dif[:], dif[:], 0.25, EPS, ALU.mult, ALU.add))
    nc.vector.scalar_tensor_tensor(var[:], var[:], 1.0 / D, dif[:], ALU.mult, ALU.add).then_inc(var_ready, 1)


def normalise(nc, k, tag, src, dst, scale_of, shift_of):
    QT = CH // P
    with ExitStack() as c:
        def sb(name, shape, dt=F32):
            return c.enter_context(nc.sbuf_tensor(tag + name, shape, dt))

        stats = sb("stats", [P, NT, 6])
        mean, var, rstd, dif = (sb(n, [P, NT]) for n in ("mean", "var", "rstd", "dif"))
        xn = sb("xn", [P, 2, QT, D])
        counted, var_ready, sd_ready, chain, xn_ready, turned, kept = (
            nc.alloc_semaphore(tag + n) for n in ("counted", "var_r", "sd", "chain", "xn_r", "turned", "kept"))
        with nc.Block() as block:
            @block.vector
            def _(dve):
                ch = Chain(dve, chain)
                statistics(nc, dve, ch, src, stats, mean, var, dif, counted, var_ready)
                dve.wait_ge(sd_ready, 1)
                ch.link(nc.vector.reciprocal(rstd[:], var[:]))

                def chunk(at, slot):
                    for j in range(QT):
                        t = at * QT + j
                        nc.vector.tensor_scalar(xn[:, slot, j, :], src[:, t, :], col(mean, t), col(rstd, t),
                                                ALU.subtract, ALU.mult).then_inc(xn_ready, 1)

                chunk(0, 0)
                chunk(1, 1)
                with dve.Fori(1, NCH // 2) as i:
                    for s in range(2):
                        dve.wait_ge(turned, 2 * i + s - 1)
                        chunk(2 * i + s, s)

            @block.scalar
            def _(act):
                act.wait_ge(var_ready, 1)
                nc.scalar.activation(var[:], var[:], ACT.Sqrt).then_inc(sd_ready, 1)
                for i in range(NCH):
                    act.wait_ge(turned, i + 1)
                    b = i * CH // L
                    nc.scalar.activation(dst[:, i * CH:(i + 1) * CH], k.ps[:, i % 2, :], ACT.Identity,
                                         bias=shift_of(b), scale=scale_of(b)).then_inc(kept, 1)

            @block.tensor
            def _(pe):
                def chunk(at, slot):
                    for j in range(QT):
                        pe.wait_ge(xn_ready, at * QT + j + 1)
                        ins = nc.tensor.transpose(k.ps[:, slot, j * P:(j + 1) * P], xn[:, slot, j, :],
                                                  k.cst[:, C_ID:C_ID + P])
                    ins.then_inc(turned, 1)

                chunk(0, 0)
                chunk(1, 1)
                with pe.Fori(1, NCH // 2) as i:
                    for s in range(2):
                        pe.wait_ge(kept, 2 * i + s - 1)
                        chunk(2 * i + s, s)


def selective_scan(nc, k, m):
    with ExitStack() as c:
        def sb(name, shape, dt=F32):
            return c.enter_context(nc.sbuf_tensor("ss_" + name, shape, dt))

        wp = sb("wp", [P, 3, SP])
        wx = sb("wx", [RANK, D])
        wdt = sb("wdt", [RANK, SP])
        wdtx = sb("wdtx", [P, SP])
        col = sb("col", [P, 3])
        aneg = sb("aneg", [P, 1])
        wout = sb("wout", [P, D])
        dpg = sb("dpg", [P, B, D])
        z, e1, dt, abar, bx, hs = (sb(n, [P, L]) for n in ("z", "e1", "dt", "abar", "bx", "hs"))
        loaded, dtw, dtw_kept, proj, chain, act_done, y_ready, y_added, aready = (
            nc.alloc_semaphore("ss_" + n) for n in
            ("loaded", "dtw", "dtw_kept", "proj", "chain", "act_done", "y_ready", "y_added", "aready"))
        hs_ready, w_ready, z_ready = (nc.alloc_semaphore("ss_" + n) for n in ("hs_ready", "w_ready", "z_ready"))

        def q(i):
            return k.ps[:, 2 * i:2 * i + 2, :].rearrange("p h n -> p (h n)")

        with nc.Block() as block:
            @block.sync
            def _(sp):
                sp.dma_start(wp[:], m["ssm_wp"]).then_inc(loaded, 16)
                sp.dma_start(wx[:], m["ssm_wx"]).then_inc(loaded, 16)
                sp.dma_start(wdt[:], m["ssm_wdt"]).then_inc(loaded, 16)
                sp.dma_start(col[:], m["ssm_col"]).then_inc(loaded, 16)
                sp.dma_start(wout[:], m["ssm_wout"]).then_inc(loaded, 16)

            @block.tensor
            def _(pe):
                pe.wait_ge(loaded, 5 * 16)
                nc.tensor.matmul(k.ps[:, 0, 0:SP], wx[:], wdt[:], start=True, stop=True).then_inc(dtw, 1)
                pe.wait_ge(dtw_kept, 1)
                for i in range(4):
                    for half in range(2):
                        for b in range(B):
                            w = wdtx[:] if i == 0 else wp[:, i - 1, :]
                            at = b * L + half * CH
                            ins = nc.tensor.matmul(k.ps[SP * b:SP * b + SP, 2 * i + half, :], w, k.hT[:, at:at + CH],
                                                   start=True, stop=True)
                    ins.then_inc(proj, 1)
                pe.wait_ge(hs_ready, 1)
                pe.wait_ge(w_ready, 1)
                for t in range(NT):
                    b, bank = t // TB, t // 4
                    o = k.ps[:, bank, (t % 4) * P:(t % 4 + 1) * P]
                    nc.tensor.matmul(o, hs[SP * b:SP * b + SP, (t % TB) * P:(t % TB + 1) * P],
                                     wout[SP * b:SP * b + SP, :], start=True, stop=False)
                    ins = nc.tensor.matmul(o, k.hT[:, t * P:(t + 1) * P], dpg[:, b, :], start=False, stop=True)
                    if t % 4 == 3:
                        ins.then_inc(y_ready, 1)

            @block.scalar
            def _(act):
                act.wait_ge(w_ready, 2)
                nc.scalar.activation(aneg[:], col[:, 0:1], ACT.Exp).then_inc(act_done, 1)
                act.wait_ge(z_ready, 1)
                nc.scalar.activation(e1[:], z[:], ACT.Abs).then_inc(act_done, 1)
                act.wait_ge(act_done, 2)
                nc.scalar.activation(e1[:], e1[:], ACT.Exp, scale=-1.0).then_inc(act_done, 1)
                act.wait_ge(act_done, 3)
                nc.scalar.activation(e1[:], e1[:], ACT.Ln, bias=1.0).then_inc(act_done, 1)
                act.wait_ge(aready, 3)
                nc.scalar.activation(abar[:], z[:], ACT.Exp).then_inc(act_done, 1)

            @block.vector
            def _(dve):
                ch = Chain(dve, chain)
                dve.wait_ge(loaded, 5 * 16)
                for b in range(B):
                    r = slice(SP * b, SP * b + SP)
                    nc.vector.tensor_tensor(wout[r, :], wout[r, :], k.row[r, 0, b, :], ALU.mult)
                    ins = nc.vector.tensor_scalar(dpg[:, b, :], k.cst[:, C_ID:C_ID + D], col[:, 2:3],
                                                  k.mod[:, 0, GA, b:b + 1], ALU.mult, ALU.mult)
                ins.then_inc(w_ready, 1)
                nc.vector.tensor_scalar(col[:, 0:1], col[:, 0:1], 88.0, None, ALU.min).then_inc(w_ready, 1)
                dve.wait_ge(dtw, 1)
                nc.vector.tensor_copy(wdtx[:], k.ps[:, 0, 0:SP]).then_inc(dtw_kept, 1)
                dve.wait_ge(act_done, 1)
                nc.vector.tensor_scalar(aneg[:], aneg[:], -1.0, None, ALU.mult).then_inc(aready, 1)
                dve.wait_ge(proj, 1)
                nc.vector.tensor_scalar(z[:], q(0), col[:, 1:2], None, ALU.add).then_inc(z_ready, 1)
                dve.wait_ge(z_ready, 1)
                dve.wait_ge(act_done, 4)
                nc.vector.scalar_tensor_tensor(dt[:], z[:], 0.0, e1[:], ALU.max, ALU.add).then_inc(aready, 1)
                dve.wait_ge(aready, 2)
                nc.vector.tensor_scalar(z[:], dt[:], aneg[:], -104.0, ALU.mult, ALU.max).then_inc(aready, 1)
                dve.wait_ge(proj, 4)
                ch.link(nc.vector.tensor_tensor(bx[:], q(1), dt[:], ALU.mult))
                ch.link(nc.vector.tensor_tensor(bx[:], q(3), bx[:], ALU.mult))
                dve.wait_ge(act_done, 5)
                ch.link(nc.vector.tensor_tensor_scan(hs[:], abar[:], bx[:], 0.0, ALU.mult, ALU.add))
                nc.vector.tensor_tensor(hs[:], q(2), hs[:], ALU.mult).then_inc(hs_ready, 1)
                for i in range(NCH):
                    dve.wait_ge(y_ready, i + 1)
                    xs = k.x[:, 4 * i:4 * i + 4, :].rearrange("p t d -> p (t d)")
                    nc.vector.tensor_tensor(xs, xs, k.ps[:, i, :], ALU.add)


def rank(nc, ch, v, n, before):
    for j in range(n):
        vj = v[:, :, j:j + 1]
        if j + 1 < n:
            ins = nc.vector.tensor_tensor(before[:, :, j + 1:n, j], vj.broadcast_to([P, NT, n - j - 1]),
                                          v[:, :, j + 1:n], ALU.is_ge)
        if j:
            ins = nc.vector.tensor_tensor(before[:, :, 0:j, j], vj.broadcast_to([P, NT, j]), v[:, :, 0:j], ALU.is_gt)
        ins.then_inc(ch.sem, 1)
        ch.at += 1
    ch.eng.wait_ge(ch.sem, ch.base + ch.at)


def gate_experts(nc, k, m, g):
    GR, PER, TOPG, TOPK, ROUTE = 4, E // 4, 2, 4, 2.5
    with ExitStack() as c:
        def sb(name, shape, dt=F32):
            return c.enter_context(nc.sbuf_tensor("ga_" + name, shape, dt))

        wg = sb("wg", [P, E])
        s, v, w, rest = (sb(n, [P, NT, E]) for n in ("s", "v", "w", "rest"))
        w3 = sb("w3", [P, NT, 3, E], BF16)
        gmax, gcnt = (sb(n, [P, NT, GR]) for n in ("gmax", "gcnt"))
        gbef = sb("gbef", [P, NT, GR, GR])
        bef = sb("bef", [P, NT, E, E])
        total = sb("total", [P, NT])
        loaded, logits, sig, chain, split, turned, kept = (
            nc.alloc_semaphore("ga_" + n) for n in ("loaded", "logits", "sig", "chain", "split", "turned", "kept"))
        lg = k.ps[:, 0, :]
        b16 = k.ps[:, 4:8, :].rearrange("p a n -> p (a n)").bitcast(BF16)
        with nc.Block() as block:
            @block.sync
            def _(sp):
                sp.dma_start(wg[:], m["gate_w"]).then_inc(loaded, 16)
                for n in ("w1", "w3", "w2"):
                    sp.dma_start(g.weights[n][:], m["ffn_" + n]).then_inc(g.loaded, 16)
                sp.dma_start(g.bias[:], m["ffn_bias"]).then_inc(g.loaded, 16)
                sp.dma_start(g.b2[:], m["ffn_b2"]).then_inc(g.loaded, 16)

            @block.tensor
            def _(pe):
                pe.wait_ge(loaded, 16)
                for t in range(NT):
                    ins = nc.tensor.matmul(lg[:, t * E:(t + 1) * E], k.hT[:, t * P:(t + 1) * P], wg[:], start=True, stop=True)
                ins.then_inc(logits, 1)
                pe.wait_ge(split, 1)
                for t in range(NT):
                    ins = nc.tensor.transpose(b16[0:3 * E, t * P:(t + 1) * P], w3[:, t, :, :].rearrange("p a e -> p (a e)"),
                                              k.cstb[:, C_ID:C_ID + P])
                ins.then_inc(turned, 1)
                for half in range(2):
                    pe.wait_ge(kept, half)
                    for j in range(NT // 2):
                        t = half * NT // 2 + j
                        ins = nc.tensor.transpose(k.ps[0:E, j // 4, (j % 4) * P:(j % 4 + 1) * P], w[:, t, :],
                                                  k.cst[:, C_ID:C_ID + P])
                    ins.then_inc(turned, 1)

            @block.scalar
            def _(act):
                act.wait_ge(logits, 1)
                nc.scalar.activation(s[:].rearrange("p t e -> p (t e)"), lg, ACT.Sigmoid).then_inc(sig, 1)
                act.wait_ge(turned, 1)
                nc.scalar.copy(g.w3T[:], b16[0:3 * E, :])
                for half in range(2):
                    act.wait_ge(turned, half + 2)
                    nc.scalar.copy(g.wT[:, half * (TOK // 2):(half + 1) * (TOK // 2)],
                                   k.ps[0:E, 0:4, :].rearrange("p a n -> p (a n)")).then_inc(kept, 1)

            @block.vector
            def _(dve):
                ch = Chain(dve, chain)
                nc.vector.memset(gbef[:], 0.0).then_inc(chain, 1)
                nc.vector.memset(bef[:], 0.0).then_inc(chain, 1)
                ch.at = 2
                dve.wait_ge(chain, 2)
                dve.wait_ge(sig, 1)
                ch.link(nc.vector.tensor_reduce(gmax[:], s[:].rearrange("p t (g e) -> p t g e", g=GR), AX.X, ALU.max))
                rank(nc, ch, gmax, GR, gbef)
                ch.link(nc.vector.tensor_reduce(gcnt[:], gbef[:], AX.X, ALU.add))
                ch.link(nc.vector.tensor_scalar(gcnt[:], gcnt[:], float(TOPG), -4.0, ALU.is_ge, ALU.mult))
                ch.link(nc.vector.tensor_tensor(v[:].rearrange("p t (g e) -> p t g e", g=GR),
                                                s[:].rearrange("p t (g e) -> p t g e", g=GR),
                                                gcnt[:].unsqueeze(3).broadcast_to([P, NT, GR, PER]), ALU.add))
                rank(nc, ch, v, E, bef)
                ch.link(nc.vector.tensor_reduce(w[:], bef[:], AX.X, ALU.add))
                ch.link(nc.vector.scalar_tensor_tensor(w[:], w[:], float(TOPK), s[:], ALU.is_lt, ALU.mult))
                ch.link(nc.vector.tensor_reduce(total[:], w[:], AX.X, ALU.add))
                ch.link(nc.vector.reciprocal(total[:], total[:]))
                ch.link(nc.vector.tensor_scalar(total[:], total[:], ROUTE, None, ALU.mult))
                ch.link(nc.vector.tensor_tensor(w[:], w[:], total[:].unsqueeze(2).broadcast_to([P, NT, E]), ALU.mult))
                ch.link(nc.vector.tensor_copy(w3[:, :, 0, :], w[:]))
                ch.link(nc.vector.tensor_tensor(rest[:], w[:], w3[:, :, 0, :], ALU.subtract))
                ch.link(nc.vector.tensor_copy(w3[:, :, 1, :], rest[:]))
                ch.link(nc.vector.tensor_tensor(rest[:], rest[:], w3[:, :, 1, :], ALU.subtract))
                nc.vector.tensor_copy(w3[:, :, 2, :], rest[:]).then_inc(split, 1)


def gated_mixture(nc, k, g):
    with ExitStack() as c:
        def sb(name, shape, dt=F32):
            return c.enter_context(nc.sbuf_tensor("gm_" + name, shape, dt))

        sg = sb("sg", [P, 2, CH])
        hc = sb("hc", [P, 2, CH])
        hw = sb("hw", [P, 2, CH])
        y = sb("y", [P, CH])
        up, spread, silu, prod, scaled, down, summed, y_kept, y_turned, added = (
            nc.alloc_semaphore("gm_" + n) for n in
            ("up", "spread", "silu", "prod", "scaled", "down", "summed", "y_kept", "y_turned", "added"))
        w1, w3, w2 = (g.weights[n] for n in ("w1", "w3", "w2"))
        A, C, W, Y, YT = 0, 2, 4, 6, 7

        with nc.Block() as block:
            @block.tensor
            def _(pe):
                pe.wait_ge(g.loaded, 5 * 16)

                def lower(n, e):
                    pe.wait_ge(scaled, n + 1)
                    nc.tensor.matmul(k.ps[:, Y, :], w2[:, e, :], hw[:, e % 2, :], start=(e == 0), stop=False).then_inc(down, 1)

                with pe.Fori(0, B) as b:
                    with pe.Fori(0, 2) as half:
                        chunk = 2 * b + half
                        n0 = chunk * E
                        tok = bass.ds(chunk * CH, CH)
                        for e in range(E):
                            pe.wait_ge(scaled, n0 + e - 1 if e else n0)
                            nc.tensor.matmul(k.ps[:, A + e % 2, :], w1[:, e, :], k.hT[:, tok], start=True, stop=True)
                            nc.tensor.matmul(k.ps[:, C + e % 2, :], w3[:, e, :], k.hT[:, tok], start=True, stop=True).then_inc(up, 1)
                            nc.tensor.matmul(k.ps[:, W + e % 2, :], k.selb[:, e, :], g.w3T[:, tok], start=True, stop=True).then_inc(spread, 1)
                            if e == 1:
                                pe.wait_ge(y_kept, chunk)
                            if e:
                                lower(n0 + e - 1, e - 1)
                        lower(n0 + E - 1, E - 1)
                        nc.tensor.matmul(k.ps[:, Y, :], g.b2[:], g.wT[:, tok], start=False, stop=True).then_inc(summed, 1)
                        pe.wait_ge(y_kept, chunk + 1)
                        pe.wait_ge(added, chunk)
                        for j in range(4):
                            ins = nc.tensor.transpose(k.ps[:, YT, j * P:(j + 1) * P], y[:, j * P:(j + 1) * P],
                                                      k.cst[:, C_ID:C_ID + P])
                        ins.then_inc(y_turned, 1)

            @block.scalar
            def _(act):
                with act.Fori(0, B) as b:
                    with act.Fori(0, 2) as half:
                        chunk = 2 * b + half
                        for e in range(E):
                            n = chunk * E + e
                            act.wait_ge(up, n + 1)
                            act.wait_ge(prod, n - 1 if e else n)
                            nc.scalar.activation(sg[:, e % 2, :], k.ps[:, A + e % 2, :], ACT.Silu,
                                                 bias=g.bias[:, 0, e:e + 1]).then_inc(silu, 1)
                        act.wait_ge(summed, chunk + 1)
                        act.wait_ge(y_turned, chunk)
                        nc.scalar.activation(y[:], k.ps[:, Y, :], ACT.Copy, scale=k.mod[:, 0, GB, bass.ds(b, 1)]).then_inc(y_kept, 1)

            @block.vector
            def _(dve):
                with dve.Fori(0, B) as b:
                    with dve.Fori(0, 2) as half:
                        chunk = 2 * b + half
                        for e in range(E):
                            n = chunk * E + e
                            dve.wait_ge(silu, n + 1)
                            nc.vector.scalar_tensor_tensor(hc[:, e % 2, :], k.ps[:, C + e % 2, :], g.bias[:, 1, e:e + 1],
                                                           sg[:, e % 2, :], ALU.add, ALU.mult).then_inc(prod, 1)
                            dve.wait_ge(prod, n + 1)
                            dve.wait_ge(spread, n + 1)
                            dve.wait_ge(down, n - 1 if e else n)
                            nc.vector.tensor_tensor(hw[:, e % 2, :], k.ps[:, W + e % 2, :], hc[:, e % 2, :],
                                                    ALU.mult).then_inc(scaled, 1)
                        dve.wait_ge(y_turned, chunk + 1)
                        xs = k.x[:, bass.ds(chunk * 4, 4), :]
                        nc.vector.tensor_tensor(xs, xs, k.ps[:, YT, :].rearrange("p (t d) -> p t d", t=4),
                                                ALU.add).then_inc(added, 1)


def first_mixture(nc, k, m):
    g = Core()
    with ExitStack() as c:
        g.weights = {n: c.enter_context(nc.sbuf_tensor("ffn_" + n, [P, E, D], F32)) for n in ("w1", "w3", "w2")}
        g.bias = c.enter_context(nc.sbuf_tensor("ffn_bias", [P, 2, E], F32))
        g.b2 = c.enter_context(nc.sbuf_tensor("ffn_b2", [E, D], F32))
        g.wT = c.enter_context(nc.sbuf_tensor("ffn_wT", [E, TOK], F32))
        g.w3T = c.enter_context(nc.sbuf_tensor("ffn_w3T", [3 * E, TOK], BF16))
        g.loaded = nc.alloc_semaphore("ffn_loaded")
        gate_experts(nc, k, m, g)
        gated_mixture(nc, k, g)


def project(nc, k, m, a):
    tag = a.tag + "pr_"
    with ExitStack() as c:
        def sb(name, shape, dt=F32):
            return c.enter_context(nc.sbuf_tensor(tag + name, shape, dt))

        w = sb("w", [P, 3, D])
        bias = sb("bias", [P, 2])
        vb = sb("vb", [P, D])
        full = sb("full", [P, 2, 2, CH])
        rest = sb("rest", [P, 2, 2, CH])
        parts = sb("parts", [P, 2, 2, 3, CH], BF16)
        loaded, done, v_done, v_kept, ones_set = (
            nc.alloc_semaphore(tag + n) for n in ("loaded", "done", "v_done", "v_kept", "ones"))
        stored = [nc.alloc_semaphore(tag + f"stored{s}") for s in range(2)]
        whole, part1, rest1, part2, rest2 = (
            [nc.alloc_semaphore(tag + f"{n}{o}") for o in "qk"] for n in ("whole", "part1_", "rest1_", "part2_", "rest2_"))
        scale = (HD ** -0.5, 1.0)

        with nc.Block() as block:
            @block.sync
            def _(sp):
                sp.dma_start(w[:], m[a.tag + "w"]).then_inc(loaded, 16)
                sp.dma_start(bias[:], m[a.tag + "bias"]).then_inc(loaded, 16)
                sp.dma_start(vb[:], m[a.tag + "vb"].broadcast_to([P, D])).then_inc(loaded, 16)
                for i in range(NCH):
                    for o in range(2):
                        sp.wait_ge(rest2[o], i + 1)
                        for part in range(3):
                            sp.dma_start(a.qk[o, :, part if o else 2 - part, :, i * CH:(i + 1) * CH],
                                         parts[:, i % 2, o, part, :]).then_inc(stored[i % 2], 16)
                for s in range(2):
                    sp.wait_ge(stored[s], NCH // 2 * 6 * 16)

            @block.tensor
            def _(pe):
                pe.wait_ge(loaded, 3 * 16)
                for i in range(NCH):
                    if i >= 2:
                        for o in range(2):
                            pe.wait_ge(whole[o], i - 1)
                        pe.wait_ge(v_kept, i - 1)
                    for o in range(2):
                        ins = nc.tensor.matmul(k.ps[:, 2 * o + i % 2, :], w[:, o, :], k.hT[:, i * CH:(i + 1) * CH],
                                               start=True, stop=True)
                        ins.then_inc(done, 1)
                    for j in range(4):
                        t = 4 * i + j
                        ins = nc.tensor.matmul(k.ps[:, 4 + i % 2, j * P:(j + 1) * P], k.hT[:, t * P:(t + 1) * P],
                                               w[:, 2, :], start=True, stop=True)
                    ins.then_inc(v_done, 1)

            def split(eng, o, i):
                s = i % 2
                eng.wait_ge(part1[o], i + 1)
                eng.tensor_tensor(rest[:, s, o, :], full[:, s, o, :], parts[:, s, o, 0, :], ALU.subtract).then_inc(rest1[o], 1)
                eng.wait_ge(part2[o], i + 1)
                eng.tensor_tensor(parts[:, s, o, 2, :], rest[:, s, o, :], parts[:, s, o, 1, :], ALU.subtract).then_inc(rest2[o], 1)

            @block.scalar
            def _(act):
                for i in range(NCH):
                    for o in range(2):
                        act.wait_ge(whole[o], i + 1)
                        if i >= 2:
                            act.wait_ge(stored[i % 2], i // 2 * 6 * 16)
                        nc.scalar.copy(parts[:, i % 2, o, 0, :], full[:, i % 2, o, :]).then_inc(part1[o], 1)
                    for o in range(2):
                        act.wait_ge(rest1[o], i + 1)
                        nc.scalar.copy(parts[:, i % 2, o, 1, :], rest[:, i % 2, o, :]).then_inc(part2[o], 1)

            @block.gpsimd
            def _(pool):
                for i in range(NCH):
                    split(nc.gpsimd, 1, i)

            @block.vector
            def _(dve):
                nc.vector.memset(a.v[:, :, :, HD:VA], 1.0)
                dve.wait_ge(loaded, 3 * 16)
                for i in range(NCH):
                    for o in range(2):
                        dve.wait_ge(done, 2 * i + o + 1)
                        if i >= 2:
                            dve.wait_ge(rest1[o], i - 1)
                        nc.vector.tensor_scalar(full[:, i % 2, o, :], k.ps[:, 2 * o + i % 2, :], bias[:, o:o + 1], scale[o],
                                                ALU.add, ALU.mult).then_inc(whole[o], 1)
                    dve.wait_ge(v_done, i + 1)
                    out = a.v[:, 4 * i:4 * i + 4, :, 0:HD].rearrange("p t h d -> p (t h) d")
                    src = k.ps[:, 4 + i % 2, :].rearrange("p (x d) -> p x d", d=HD)
                    nc.vector.tensor_copy(out, src).then_inc(v_kept, 1)
                    split(nc.vector, 0, i)
                if a.causal:
                    dve.wait_ge(v_kept, NCH)
                    for t in range(NT):
                        out = a.v[:, t, :, 0:HD]
                        nc.vector.tensor_tensor(out, out, vb[:].rearrange("p (h d) -> p h d", d=HD), ALU.add)


def relative_bias(nc, k, m, a):
    with ExitStack() as c:
        rel = c.enter_context(nc.sbuf_tensor("rb_rel", [NBK, H], F32))
        top = c.enter_context(nc.sbuf_tensor("rb_top", [H, 1], F32))
        strip = c.enter_context(nc.sbuf_tensor("rb_strip", [H, STRIP], F32))
        skew = c.enter_context(nc.sbuf_tensor("rb_skew", [P, H * NEAR], F32))
        loaded, picked, top_ready, strip_ready, stored, skewed, spread, flipped, near_kept = (
            nc.alloc_semaphore("rb_" + n) for n in ("loaded", "picked", "top", "strip_r", "stored", "skewed", "spread",
                                                    "flipped", "near_kept"))
        near = a.near[:].rearrange("p h q -> p (h q)")
        BANKS = H * NEAR // CH
        with nc.Block() as block:
            @block.sync
            def _(sp):
                sp.dma_start(rel[:], m["rel_emb"]).then_inc(loaded, 16)
                sp.wait_ge(strip_ready, 1)
                sp.dma_start(a.strip, strip[:]).then_inc(stored, 16)
                sp.wait_ge(stored, 16)
                sp.dma_start(skew[:].rearrange("p (h q) -> p h q", h=H),
                             bass.AP(a.strip.tensor, 0, [[1, P], [STRIP, H], [1, NEAR]])).then_inc(skewed, 16)
                sp.dma_start(a.left[:], bass.AP(a.strip.tensor, STRIP - 1, [[0, P], [STRIP, H]]),
                             allow_slow_non_contiguous=True).then_inc(spread, 16)
                sp.dma_start(a.right[:], bass.AP(a.strip.tensor, 0, [[0, P], [STRIP, H]]),
                             allow_slow_non_contiguous=True).then_inc(spread, 16)
                sp.wait_ge(spread, 32)

            @block.tensor
            def _(pe):
                pe.wait_ge(loaded, 16)
                nc.tensor.matmul(k.ps[0:H, 0, :], rel[:], k.cst[0:NBK, C_OH:C_OH + STRIP], start=True, stop=True).then_inc(picked, 1)
                pe.wait_ge(skewed, 16)
                pe.wait_ge(strip_ready, 1)
                for i in range(BANKS):
                    if i >= 8:
                        pe.wait_ge(near_kept, i - 7)
                    nc.tensor.matmul(k.ps[:, i % 8, :], k.cst[:, C_FLIP:C_FLIP + P], skew[:, i * CH:(i + 1) * CH],
                                     start=True, stop=True).then_inc(flipped, 1)

            @block.vector
            def _(dve):
                dve.wait_ge(picked, 1)
                nc.vector.tensor_reduce(top[:], k.ps[0:H, 0, :], AX.X, ALU.max, negate=True).then_inc(top_ready, 1)
                for i in range(BANKS):
                    dve.wait_ge(flipped, i + 1)
                    nc.vector.tensor_copy(near[:, i * CH:(i + 1) * CH], k.ps[:, i % 8, :]).then_inc(near_kept, 1)

            @block.scalar
            def _(act):
                act.wait_ge(top_ready, 1)
                nc.scalar.activation(strip[:], k.ps[0:H, 0, :], ACT.Exp, bias=top[:]).then_inc(strip_ready, 1)


def attend(nc, k, a):
    causal, tag = a.causal, a.tag + "at_"
    TERMS, ROWS = 6, 6 * HD
    RING = 16
    LAG = 2
    NV = 1 if causal else 3
    HALF = CH // P

    def pieces():
        out = []
        for i in range(TB):
            for half in range(2):
                q0, q1 = half * CH, (half + 1) * CH
                if causal:
                    q0 = max(q0, i * P)
                if q0 < q1:
                    out.append((i, half, q0, q1))
        return out

    PIECES = pieces()
    NP_ = len(PIECES)
    NB_ = NP_ * HG
    NA_ = HG * TB + 1
    last_of = {half: max(n for n, p in enumerate(PIECES) if p[1] == half) for half in range(2)}

    def near(n):
        i, half, q0, q1 = PIECES[n]
        lo, hi = max(q0, (i - 1) * P), min(q1, (i + 2) * P)
        return (lo, hi) if lo < hi and not causal else None

    def segments(n):
        i, half, q0, q1 = PIECES[n]
        if causal:
            return [(0, q0, q1)]
        cuts = [(2, q0, min(q1, (i - 1) * P)), (0, max(q0, (i - 1) * P), min(q1, (i + 2) * P)), (1, max(q0, (i + 2) * P), q1)]
        return [s for s in cuts if s[1] < s[2]]

    NEARS = [n for n in range(NP_) if near(n)]

    with ExitStack() as c:
        def sb(name, shape, dt=F32):
            return c.enter_context(nc.sbuf_tensor(tag + name, shape, dt))

        def sem(name):
            return nc.alloc_semaphore(tag + name)

        qop = sb("qop", [P, NG, 2, L], BF16)
        kop = sb("kop", [P, NG, HG, L], BF16)
        row1 = sb("row1", [1, L], BF16)
        row0 = sb("row0", [1, L], BF16)
        top = sb("top", [P, HG * TB])
        negm = sb("negm", [HG * TB, P], BF16)
        ring = sb("ring", [P, RING, CH])
        vs = sb("vs", [P, 2, NV, TB, HG, 32])
        osb = sb("osb", [P, L])
        loads = [sem(f"loads{g}") for g in range(NG)]
        mrow = [sem(f"mrow{g}") for g in range(NG)]
        stored = sem("stored")
        (cleared, ones_in, a_filled, a_read, b_filled, exped, scaled, pv_done, o_copied,
         vs_zero, vs_ready) = (sem(n) for n in
                               ("cleared", "ones_in", "a_filled", "a_read", "b_filled", "exped", "scaled",
                                "pv_done", "o_copied", "vs_zero", "vs_ready"))
        NLOAD = 14 * 16
        A_BANK, B_BANK, O_BANK = 0, 4, 6

        def place(j):
            return 64 * (j % 2), j // 2

        def unit(b, g):
            return b * NG + g

        with nc.Block() as block:
            @block.sync
            def _(sp):
                def loads_of(b, g):
                    for base in range(2):
                        last = 64 * base + ROWS
                        sp.dma_start(qop[last:last + 1, g, :, :], row0[:].unsqueeze(1).broadcast_to([1, 2, L])).then_inc(loads[g], 16)
                        for o in range(2):
                            row = 64 * base
                            for n in (3, 2, 1):
                                start = a.qk[o, g * HG + base, 3 - n if o == 0 else 0, :, bass.ds(b * L, L)]
                                rows = bass.AP(start.tensor, start.offset, [[TOK, n * HD], [2 * 3 * HD * TOK, 2], [1, L]])
                                slot = qop[row:row + n * HD, g, :, :] if o == 0 else kop[row:row + n * HD, g, base::2, :]
                                sp.dma_start(slot, rows).then_inc(loads[g], 16)
                                row += n * HD

                def largest(b, g):
                    sp.wait_ge(a_read, (unit(b, g) + 1) * NA_)
                    for j in range(HG):
                        base, pair = place(j)
                        sp.dma_start(qop[base + ROWS:base + ROWS + 1, g, pair, :],
                                     negm[j * TB:(j + 1) * TB, :]).then_inc(mrow[g], 16)

                def store(b, g):
                    u = unit(b, g)
                    sp.wait_ge(o_copied, u + 1)
                    for j in range(HG):
                        sp.dma_start(a.o[b, g * HG + j, :, :], osb[32 * j:32 * j + VA, :]).then_inc(stored, 16)

                def steps(b, end=False):
                    for g in range(NG):
                        if not (end and g >= 2):
                            nb, ng = (b, g + 2) if g < 2 else (b + 1, g - 2)
                            sp.wait_ge(pv_done, unit(b, g) * NP_)
                            loads_of(nb, ng)
                        if g < NG - 1:
                            largest(b, g + 1)
                        elif not end:
                            largest(b + 1, 0)
                        store(b, g)

                sp.wait_ge(cleared, 4)
                for base in range(2):
                    last = 64 * base + ROWS
                    for g in range(NG):
                        sp.dma_start(kop[last:last + 1, g, base::2, :], row1[:].unsqueeze(1).broadcast_to([1, 2, L])).then_inc(ones_in, 16)
                loads_of(0, 0)
                loads_of(0, 1)
                largest(0, 0)
                with sp.Fori(0, B - 1) as b:
                    steps(b)
                steps(B - 1, True)
                sp.wait_ge(stored, B * NG * HG * 16)

            @block.tensor
            def _(pe):
                def top_turn(b, g, n):
                    turn = unit(b, g) * NA_ + n
                    slot = A_BANK + 2 * ((g * NA_ + n) % 2)
                    if n == 0:
                        pe.wait_ge(loads[g], (b + 1) * NLOAD)
                    if not (isinstance(turn, int) and turn < 2):
                        pe.wait_ge(a_read, turn - 1)
                    if n == NA_ - 1:
                        pe.wait_ge(a_read, turn)
                        nc.tensor.transpose(k.ps[0:HG * TB, slot, 0:P], top[:], k.cst[:, C_ID:C_ID + P]).then_inc(a_filled, 1)
                        return
                    j, i = n // TB, n % TB
                    pair = j // 2
                    keys = (i + 1) * P if causal else L
                    for half in range(2):
                        k0, k1 = half * CH, min(keys, (half + 1) * CH)
                        if k0 >= k1:
                            continue
                        diag = causal and k0 <= i * P < k1
                        ins = nc.tensor.matmul(k.ps[:, slot + half, 0:k1 - k0], qop[:, g, pair, i * P:(i + 1) * P],
                                               kop[:, g, j, k0:k1], start=True, stop=not diag)
                        if diag:
                            ins = nc.tensor.matmul(k.ps[:, slot + half, i * P - k0:(i + 1) * P - k0], k.cstb[:, C_ID:C_ID + P],
                                                   k.cstb[:, C_MA:C_MA + P], start=False, stop=True)
                    ins.then_inc(a_filled, 1)

                def score_turn(b, g, t):
                    n, j = t // HG, t % HG
                    i, half, q0, q1 = PIECES[n]
                    pair = j // 2
                    u = unit(b, g)
                    if t == 0:
                        pe.wait_ge(mrow[g], (b + 1) * HG * 16)
                        pe.wait_ge(ones_in, 2 * NG * 16)
                    pe.wait_ge(exped, u * NB_ + (t - 1 if t else 0))
                    bank = B_BANK + t % 2
                    diag = causal and q0 == i * P
                    ins = nc.tensor.matmul(k.ps[:, bank, 0:q1 - q0], kop[:, g, j, i * P:(i + 1) * P],
                                           qop[:, g, pair, q0:q1], start=True, stop=not diag)
                    if diag:
                        ins = nc.tensor.matmul(k.ps[:, bank, 0:P], k.cstb[:, C_ID:C_ID + P], k.cstb[:, C_MB:C_MB + P],
                                               start=False, stop=True)
                    ins.then_inc(b_filled, 1)

                def value_turn(b, g, n):
                    i, half, q0, q1 = PIECES[n]
                    u = unit(b, g)
                    if n == 0:
                        pe.wait_ge(vs_ready, u + 1)
                        pe.wait_ge(o_copied, u)
                    pe.wait_ge(exped, u * NB_ + (n + 1) * HG)
                    if n in NEARS:
                        pe.wait_ge(scaled, u * len(NEARS) + NEARS.index(n) + 1)
                    for x, (var, s0, s1) in enumerate(segments(n)):
                        for j in range(HG):
                            ins = nc.tensor.matmul(k.ps[32 * j:32 * j + 32, O_BANK + half, s0 - half * CH:s1 - half * CH],
                                                   vs[:, g % 2, var, i, j, :], ring[:, (n % (RING // HG)) * HG + j, s0 - q0:s1 - q0],
                                                   start=(i == 0 and x == 0), stop=(n == last_of[half] and x == len(segments(n)) - 1),
                                                   skip_group_check=True)
                    ins.then_inc(pv_done, 1)

                def run(b, g, ahead):
                    done = 0
                    for n in range(NP_ + LAG):
                        if n < NP_:
                            for j in range(HG):
                                t = n * HG + j
                                score_turn(b, g, t)
                                while ahead and done < NA_ and (done + 1) * NB_ * 0.86 / NA_ <= t + 1:
                                    top_turn(*ahead, done)
                                    done += 1
                        if n >= LAG:
                            value_turn(b, g, n - LAG)
                    while ahead and done < NA_:
                        top_turn(*ahead, done)
                        done += 1

                for n in range(NA_):
                    top_turn(0, 0, n)
                with pe.Fori(0, B - 1) as b:
                    for g in range(NG):
                        run(b, g, (b, g + 1) if g < NG - 1 else (b + 1, 0))
                for g in range(NG):
                    run(B - 1, g, (B - 1, g + 1) if g < NG - 1 else None)

            @block.vector
            def _(dve):
                def tops(b, g):
                    for n in range(NA_):
                        turn = unit(b, g) * NA_ + n
                        slot = A_BANK + 2 * ((g * NA_ + n) % 2)
                        dve.wait_ge(a_filled, turn + 1)
                        if n == NA_ - 1:
                            if not (isinstance(b, int) and b == 0 and g == 0):
                                pb, pg = (b, g - 1) if g else (b - 1, NG - 1)
                                dve.wait_ge(mrow[pg], (pb + 1) * HG * 16)
                            nc.vector.tensor_scalar(negm[:], k.ps[0:HG * TB, slot, 0:P], -1.0, None, ALU.mult).then_inc(a_read, 1)
                        else:
                            i = n % TB
                            keys = (i + 1) * P if causal else L
                            src = k.ps[:, slot:slot + 2, :].rearrange("p a n -> p (a n)")[:, 0:keys]
                            nc.vector.tensor_reduce(top[:, n:n + 1], src, AX.X, ALU.max).then_inc(a_read, 1)

                nc.vector.memset(row1[:], 1.0).then_inc(cleared, 1)
                nc.vector.memset(row0[:], 0.0).then_inc(cleared, 1)
                nc.vector.memset(kop[:].rearrange("p g a n -> p (g a n)").bitcast(I32), 0).then_inc(cleared, 1)
                nc.vector.memset(vs[:], 0.0).then_inc(vs_zero, 1)
                tops(0, 0)
                with dve.Fori(0, B - 1) as b:
                    for g in range(NG):
                        tops(*((b, g + 1) if g < NG - 1 else (b + 1, 0)))
                for g in range(1, NG):
                    tops(B - 1, g)

            @block.scalar
            def _(act):
                def copy_out(b, g):
                    act.wait_ge(stored, unit(b, g) * HG * 16)
                    act.wait_ge(pv_done, (unit(b, g) + 1) * NP_)
                    nc.scalar.copy(osb[:], k.ps[:, O_BANK:O_BANK + 2, :].rearrange("p a n -> p (a n)")).then_inc(o_copied, 1)

                def exps(b, g):
                    u = unit(b, g)
                    for t in range(NB_):
                        n = t // HG
                        i, half, q0, q1 = PIECES[n]
                        act.wait_ge(b_filled, u * NB_ + t + 1)
                        if n >= RING // HG and t % HG == 0:
                            act.wait_ge(pv_done, u * NP_ + n + 1 - RING // HG)
                        nc.scalar.activation(ring[:, t % RING, 0:q1 - q0], k.ps[:, B_BANK + t % 2, 0:q1 - q0],
                                             ACT.Exp).then_inc(exped, 1)

                with act.Fori(0, B) as b:
                    for g in range(NG):
                        exps(b, g)
                        copy_out(b, g)

            @block.gpsimd
            def _(pool):
                def values(b, g):
                    s = g % 2
                    src = a.v[:, bass.ds(b * TB, TB), g * HG:(g + 1) * HG, :]
                    ins = nc.gpsimd.tensor_copy(vs[:, s, 0, :, :, 0:VA], src)
                    if not causal:
                        for var, f in ((1, a.left), (2, a.right)):
                            by = f[:, g * HG:(g + 1) * HG].unsqueeze(1).unsqueeze(3).broadcast_to([P, TB, HG, VA])
                            ins = nc.gpsimd.tensor_tensor(vs[:, s, var, :, :, 0:VA], src, by, ALU.mult)
                    ins.then_inc(vs_ready, 1)

                def bias(b, g):
                    u = unit(b, g)
                    for n in NEARS:
                        i, half, q0, q1 = PIECES[n]
                        lo, hi = near(n)
                        for j in range(HG):
                            pool.wait_ge(exped, u * NB_ + n * HG + j + 1)
                            w = ring[:, (n * HG + j) % RING, lo - q0:hi - q0]
                            ins = nc.gpsimd.tensor_tensor(w, w, a.near[:, g * HG + j, lo - (i - 1) * P:hi - (i - 1) * P], ALU.mult)
                        ins.then_inc(scaled, 1)

                nc.gpsimd.memset(qop[:].rearrange("p g a n -> p (g a n)").bitcast(I32), 0).then_inc(cleared, 1)
                pool.wait_ge(vs_zero, 1)
                values(0, 0)
                def steps(b, end=False):
                    for g in range(NG):
                        if not (end and g == NG - 1):
                            pool.wait_ge(pv_done, unit(b, g) * NP_)
                            values(*((b, g + 1) if g < NG - 1 else (b + 1, 0)))
                        bias(b, g)

                with pool.Fori(0, B - 1) as b:
                    steps(b)
                steps(B - 1, True)


def join_heads(nc, k, m, a, dst, wo):
    tag = a.tag + "jo_"
    with ExitStack() as c:
        num = c.enter_context(nc.sbuf_tensor(tag + "num", [P, B, L], F32))
        den = c.enter_context(nc.sbuf_tensor(tag + "den", [P, B, L], F32))
        loaded = [nc.alloc_semaphore(tag + f"loaded{b}") for b in range(B)]
        inv, ready, y_ready = (nc.alloc_semaphore(tag + n) for n in ("inv", "ready", "y_ready"))
        with nc.Block() as block:
            @block.sync
            def _(sp):
                for b in range(B):
                    o = a.o[b]
                    sp.dma_start(num[:, b, :], bass.AP(o.tensor, o.offset, [[VA * L, H], [L, HD], [1, L]])).then_inc(loaded[b], 16)
                    sp.dma_start(den[:, b, :], bass.AP(o.tensor, o.offset + HD * L, [[VA * L, H], [0, HD], [1, L]])).then_inc(loaded[b], 16)

            @block.vector
            def _(dve):
                for b in range(B):
                    dve.wait_ge(loaded[b], 32)
                    nc.vector.reciprocal(den[:, b, :], den[:, b, :]).then_inc(inv, 1)
                    dve.wait_ge(inv, b + 1)
                    nc.vector.tensor_tensor(num[:, b, :], num[:, b, :], den[:, b, :], ALU.mult).then_inc(ready, 1)
                    for i in (2 * b, 2 * b + 1):
                        dve.wait_ge(y_ready, i + 1)
                        xs = dst[:, 4 * i:4 * i + 4, :].rearrange("p t d -> p (t d)")
                        nc.vector.tensor_tensor(xs, xs, k.ps[:, i, :], ALU.add)

            @block.tensor
            def _(pe):
                for t in range(NT):
                    b = t // TB
                    if t % TB == 0:
                        pe.wait_ge(ready, b + 1)
                    ins = nc.tensor.matmul(k.ps[:, t // 4, (t % 4) * P:(t % 4 + 1) * P], num[:, b, (t % TB) * P:(t % TB + 1) * P],
                                           wo[:, b, :], start=True, stop=True)
                    if t % 4 == 3:
                        ins.then_inc(y_ready, 1)


def biased_attention(nc, k, m):
    a = Core()
    a.tag, a.causal = "ba_", False
    with ExitStack() as c:
        def sb(name, shape, dt=F32):
            return c.enter_context(nc.sbuf_tensor("ba_" + name, shape, dt))

        a.v = sb("v", [P, NT, H, VA])
        a.near = sb("near", [P, H, NEAR])
        a.left = sb("left", [P, H])
        a.right = sb("right", [P, H])
        a.qk, a.o, a.strip = k.qk_dram, k.o_dram, k.strip_dram
        project(nc, k, m, a)
        relative_bias(nc, k, m, a)
        attend(nc, k, a)
    with ExitStack() as c:
        wo = c.enter_context(nc.sbuf_tensor("ba_wo", [P, B, D], F32))
        wo_in, wo_ready = nc.alloc_semaphore("ba_wo_in"), nc.alloc_semaphore("ba_wo_ready")
        with nc.Block() as block:
            @block.sync
            def _(sp):
                sp.dma_start(wo[:], m["ba_wo"].unsqueeze(1).broadcast_to([P, B, D])).then_inc(wo_in, 16)

            @block.vector
            def _(dve):
                dve.wait_ge(wo_in, 16)
                nc.vector.tensor_tensor(wo[:], wo[:], k.row[:, 1, :, :], ALU.mult)
        join_heads(nc, k, m, a, k.x, wo)


def modulate(nc, k, tag, src, dst, row_scale, row_shift, nb):
    with ExitStack() as c:
        def sb(name, shape, dt=F32):
            return c.enter_context(nc.sbuf_tensor(tag + name, shape, dt))

        stats = sb("stats", [P, NT, 6])
        mean, var, rstd, dif = (sb(n, [P, NT]) for n in ("mean", "var", "rstd", "dif"))
        counted, var_ready, sd_ready, chain, plain, scaled = (
            nc.alloc_semaphore(tag + n) for n in ("counted", "var_r", "sd", "chain", "plain", "scaled"))
        with nc.Block() as block:
            @block.vector
            def _(dve):
                ch = Chain(dve, chain)
                statistics(nc, dve, ch, src, stats, mean, var, dif, counted, var_ready)
                dve.wait_ge(sd_ready, 1)
                ch.link(nc.vector.reciprocal(rstd[:], var[:]))
                with dve.Fori(0, NT // 4) as i:
                    for j in range(4):
                        t = 4 * i + j
                        nc.vector.tensor_scalar(dst[:, t, :], src[:, t, :], col(mean, t), col(rstd, t),
                                                ALU.subtract, ALU.mult).then_inc(plain, 1)
                for b in range(B):
                    dve.wait_ge(plain, TB * (b + 1))
                    d = dst[:, b * TB:(b + 1) * TB, :]
                    r = b if nb > 1 else 0
                    nc.vector.tensor_tensor(d, d, row_scale[:, r:r + 1, :].broadcast_to([P, TB, D]), ALU.mult).then_inc(scaled, 1)
                    dve.wait_ge(scaled, b + 1)
                    nc.vector.tensor_tensor(d, d, row_shift[:, r:r + 1, :].broadcast_to([P, TB, D]), ALU.add)

            @block.scalar
            def _(act):
                act.wait_ge(var_ready, 1)
                nc.scalar.activation(var[:], var[:], ACT.Sqrt).then_inc(sd_ready, 1)


def route(nc, k, m, r):
    with ExitStack() as c:
        def sb(name, shape, dt=F32):
            return c.enter_context(nc.sbuf_tensor("ro_" + name, shape, dt))

        wr = sb("wr", [P, E])
        lg, ex, l2, c1, slot = (sb(n, [P, NT, E]) for n in ("lg", "ex", "l2", "c1", "slot"))
        pick = sb("pick", [P, 2, NT, E])
        pickb = sb("pickb", [P, 2, NT, E], BF16)
        tot = sb("tot", [P, 2, E, NT])
        inc = sb("inc", [P, 2, E, NT])
        keep1 = sb("keep1", [P, E, NT])
        col1, col2 = (sb(n, [P, NT]) for n in ("col1", "col2"))
        kept = sb("kept", [P, 2, NT])
        row = sb("row", [P, 2, NT])
        trash = sb("trash", [P, 2, NT])
        onesb = sb("onesb", [P, P], BF16)
        loaded, logits, e_ready, chain, ch_ready, counts, turned, moved = (
            nc.alloc_semaphore("ro_" + n) for n in
            ("loaded", "logits", "e_ready", "chain", "ch_ready", "counts", "turned", "moved"))
        ex_go = nc.alloc_semaphore("ro_ex_go")

        def v(t):
            return t[:].unsqueeze(2).broadcast_to([P, NT, E])

        def const(at):
            return k.cst[:, at:at + E].unsqueeze(1).broadcast_to([P, NT, E])

        with nc.Block() as block:
            @block.sync
            def _(sp):
                sp.dma_start(wr[:], m["router_w"]).then_inc(loaded, 16)
                sp.dma_start(trash[:], m["trash_rows"]).then_inc(loaded, 16)

            @block.tensor
            def _(pe):
                for t in range(NT):
                    if t >= 8 and t % 4 == 0:
                        pe.wait_ge(moved, t // 4 - 1)
                    ins = nc.tensor.transpose(k.ps[:, (t // 4) % 2, (t % 4) * P:(t % 4 + 1) * P], r.xt[:, t, :], k.cst[:, C_ID:C_ID + P])
                    if t % 4 == 3:
                        ins.then_inc(turned, 1)
                pe.wait_ge(loaded, 32)
                for t in range(NT):
                    if t % 4 == 0:
                        pe.wait_ge(moved, t // 4 + 1)
                    ins = nc.tensor.matmul(k.ps[:, 2, t * E:(t + 1) * E], k.hT[:, t * P:(t + 1) * P], wr[:], start=True, stop=True)
                ins.then_inc(logits, 1)
                pe.wait_ge(ch_ready, 1)
                for i in range(2):
                    one = pickb[:, i, :, :].rearrange("p t e -> p (t e)")
                    nc.tensor.matmul(k.ps[:, 3 + i, :], k.cstb[:, C_TRI:C_TRI + P], one, start=True, stop=True)
                    ins = nc.tensor.matmul(k.ps[:, 5 + i, :], onesb[:], one, start=True, stop=True)
                ins.then_inc(counts, 1)

            @block.scalar
            def _(act):
                for i in range(NCH):
                    act.wait_ge(turned, i + 1)
                    nc.scalar.copy(k.hT[:, i * CH:(i + 1) * CH], k.ps[:, i % 2, :]).then_inc(moved, 1)
                act.wait_ge(ex_go, 1)
                nc.scalar.activation(ex[:], lg[:], ACT.Exp).then_inc(e_ready, 1)

            @block.vector
            def _(dve):
                ch = Chain(dve, chain)
                L_, vec = ch.link, nc.vector
                L_(vec.memset(onesb[:], 1.0))
                L_(vec.memset(keep1[:], 1.0))
                L_(vec.memset(keep1[:, :, 0:1], 0.0))
                dve.wait_ge(loaded, 32)
                dve.wait_ge(logits, 1)
                raw = k.ps[:, 2, :].rearrange("p (t e) -> p t e", e=E)
                L_(vec.tensor_reduce(col1[:], raw, AX.X, ALU.max))
                vec.tensor_tensor(lg[:], raw, v(col1), ALU.subtract).then_inc(ex_go, 1)
                dve.wait_ge(e_ready, 1)
                L_(vec.tensor_reduce(col1[:], ex[:], AX.X, ALU.add))
                L_(vec.reciprocal(col1[:], col1[:]))
                L_(vec.tensor_tensor(ex[:], ex[:], v(col1), ALU.mult))

                def first_of(values, i):
                    L_(vec.tensor_reduce(col1[:], values, AX.X, ALU.max))
                    L_(vec.tensor_tensor(c1[:], values, v(col1), ALU.is_equal))
                    L_(vec.tensor_tensor(c1[:], c1[:], const(C_FIRST), ALU.mult))
                    L_(vec.tensor_reduce(col1[:], c1[:], AX.X, ALU.max))
                    L_(vec.tensor_tensor(pick[:, i, :, :], c1[:], v(col1), ALU.is_equal))

                first_of(ex[:], 0)
                L_(vec.scalar_tensor_tensor(l2[:].rearrange("p t e -> p (t e)"), pick[:, 0, :, :].rearrange("p t e -> p (t e)"),
                                            NEG, lg[:].rearrange("p t e -> p (t e)"), ALU.mult, ALU.add))
                first_of(l2[:], 1)
                vec.tensor_copy(pickb[:], pick[:]).then_inc(ch_ready, 1)
                dve.wait_ge(counts, 1)
                for i in range(2):
                    L_(vec.tensor_copy(tot[:, i, :, :], k.ps[:, 5 + i, :].rearrange("p (t e) -> p e t", e=E)))
                    L_(vec.tensor_tensor_scan(inc[:, i, :, :].rearrange("p e t -> p (e t)"), keep1[:].rearrange("p e t -> p (e t)"),
                                              tot[:, i, :, :].rearrange("p e t -> p (e t)"), 0.0, ALU.mult, ALU.add))
                for i in range(2):
                    L_(vec.tensor_tensor(c1[:], inc[:, i, :, :].rearrange("p e t -> p t e"), tot[:, i, :, :].rearrange("p e t -> p t e"), ALU.subtract))
                    L_(vec.tensor_tensor(c1[:], c1[:], k.ps[:, 3 + i, :].rearrange("p (t e) -> p t e", e=E), ALU.add))
                    if i:
                        L_(vec.tensor_tensor(c1[:], c1[:], inc[:, 0, :, NT - 1:NT].rearrange("p e a -> p a e").broadcast_to([P, NT, E]), ALU.add))
                    L_(vec.tensor_scalar(c1[:], c1[:], -1.0, None, ALU.add))
                    L_(vec.tensor_scalar(l2[:], c1[:], float(CAP), None, ALU.is_lt))
                    L_(vec.tensor_tensor(l2[:], l2[:], pick[:, i, :, :], ALU.mult))
                    L_(vec.tensor_tensor(slot[:], c1[:], const(C_SLOT), ALU.add))
                    L_(vec.tensor_tensor(slot[:], slot[:], l2[:], ALU.mult))
                    L_(vec.tensor_reduce(row[:, i, :], slot[:], AX.X, ALU.add))
                    L_(vec.tensor_reduce(kept[:, i, :], l2[:], AX.X, ALU.add))
                    L_(vec.tensor_tensor(slot[:], ex[:], l2[:], ALU.mult))
                    L_(vec.tensor_reduce(r.g[:, i, :], slot[:], AX.X, ALU.add))
                L_(vec.tensor_copy(r.frm[:], row[:]))
                L_(vec.tensor_scalar(kept[:], kept[:], -1.0, 1.0, ALU.mult, ALU.add))
                L_(vec.tensor_tensor(kept[:], kept[:], trash[:], ALU.mult))
                L_(vec.tensor_tensor(row[:], row[:], kept[:], ALU.add))
                L_(vec.tensor_copy(r.to[:], row[:]))
                L_(vec.tensor_tensor(col1[:], r.g[:, 0, :], r.g[:, 1, :], ALU.add))
                L_(vec.tensor_scalar(col1[:], col1[:], 1.1920929e-07, None, ALU.max))
                L_(vec.reciprocal(col2[:], col1[:]))
                L_(vec.tensor_scalar(col2[:], col2[:], KEEP, None, ALU.mult))
                vec.tensor_tensor(r.g[:], r.g[:], col2[:].unsqueeze(1).broadcast_to([P, 2, NT]), ALU.mult)


def experts(nc, k, m, r):
    QT, FB = CAP // P, FF // P
    with ExitStack() as c:
        def sb(name, shape, dt=F32):
            return c.enter_context(nc.sbuf_tensor("ex_" + name, shape, dt))

        fc1, fc2 = sb("fc1", [P, 2, FF]), sb("fc2", [P, 2, FB, D])
        b1, b2 = sb("b1", [P, E, FB]), sb("b2", [P, E, D])
        xi = sb("xi", [P, 2, QT, D])
        xT = sb("xT", [P, 2, CAP])
        hh = sb("hh", [P, 2, FB, CAP])
        eo = sb("eo", [P, 2, QT, D])
        back = sb("back", [P, 2, 4, 4, D])
        sent, consts_in, turned, xT_ready, up, act_done, down, eo_ready = (
            nc.alloc_semaphore("ex_" + n) for n in
            ("sent", "consts_in", "turned", "xT_ready", "up", "act_done", "down", "eo_ready"))
        w_in = [nc.alloc_semaphore(f"ex_w_in{s}") for s in range(2)]
        x_in = [nc.alloc_semaphore(f"ex_x_in{s}") for s in range(2)]
        eo_out = [nc.alloc_semaphore(f"ex_eo_out{s}") for s in range(2)]
        got = [nc.alloc_semaphore(f"ex_got{s}") for s in range(4)]
        half_sum, summed = nc.alloc_semaphore("ex_half_sum"), nc.alloc_semaphore("ex_summed")
        chain = nc.alloc_semaphore("ex_chain")

        def rounds(eng, body):
            body(0, 0)
            with eng.Fori(0, (E - 2) // 2) as i:
                body(2 * i + 1, 1)
                body(2 * i + 2, 0)
            body(E - 1, 1)

        with nc.Block() as block:
            @block.gpsimd
            def _(pool):
                pool.wait_ge(r.cleared, 16)
                for t in range(NT):
                    for i in range(2):
                        nc.gpsimd.indirect_dma_start(k.rows_in, bass.IndirectOffsetOnAxis(ap=r.to[:, i, t:t + 1], axis=0),
                                                     r.xt[:, t, :], None).then_inc(sent, 16)
                for s in range(2):
                    pool.wait_ge(eo_out[s], E // 2 * 16)
                for n in range(NT // 4):
                    if n >= 4:
                        pool.wait_ge(summed, 4 * (n - 3))
                    for j in range(4):
                        for i in range(2):
                            nc.gpsimd.indirect_dma_start(back[:, i, n % 4, j, :], None, k.rows_out,
                                                         bass.IndirectOffsetOnAxis(ap=r.frm[:, i, 4 * n + j:4 * n + j + 1], axis=0)
                                                         ).then_inc(got[n % 4], 16)

            @block.sync
            def _(sp):
                sp.dma_start(b1[:], m["fc1_b"]).then_inc(consts_in, 16)
                sp.dma_start(b2[:], m["fc2_b"].broadcast_to([P, E, D])).then_inc(consts_in, 16)

                def load(e, s):
                    if not (isinstance(e, int) and e == 0):
                        if not (isinstance(e, int) and e < 2):
                            sp.wait_ge(down, e - 1)
                    sp.dma_start(fc1[:, s, :], m["fc1_w"][e]).then_inc(w_in[s], 16)
                    sp.dma_start(fc2[:, s, :, :], m["fc2_w"][e]).then_inc(w_in[s], 16)

                def rows(e, s):
                    sp.dma_start(xi[:, s, :, :], k.rows_in[bass.ds(e * CAP, CAP), :].rearrange("(q p) d -> p q d", p=P)).then_inc(x_in[s], 16)

                def keep(e, s):
                    sp.wait_ge(eo_ready, e + 1)
                    sp.dma_start(k.rows_out[bass.ds(e * CAP, CAP), :].rearrange("(q p) d -> p q d", p=P), eo[:, s, :, :]).then_inc(eo_out[s], 16)

                load(0, 0)
                load(1, 1)
                sp.wait_ge(sent, NT * 2 * 16)
                rows(0, 0)
                rows(1, 1)

                def step(e, s, more=True):
                    keep(e, s)
                    if more:
                        load(e + 2, s)
                        rows(e + 2, s)

                with sp.Fori(0, (E - 2) // 2) as i:
                    step(2 * i, 0)
                    step(2 * i + 1, 1)
                step(E - 2, 0, False)
                step(E - 1, 1, False)
                for s in range(2):
                    sp.wait_ge(eo_out[s], E // 2 * 16)

            def nth(e, s):
                return (e - s) // 2 + 1 if isinstance(e, int) else None

            @block.tensor
            def _(pe):
                def turn(e, s, n):
                    pe.wait_ge(x_in[s], 16 * n)
                    if not (isinstance(e, int) and e < 2):
                        pe.wait_ge(xT_ready, e - 1)
                    for q in range(QT):
                        ins = nc.tensor.transpose(k.ps[:, s, q * P:(q + 1) * P], xi[:, s, q, :], k.cst[:, C_ID:C_ID + P])
                    ins.then_inc(turned, 1)

                def upper(e, s, n):
                    pe.wait_ge(w_in[s], 32 * n)
                    pe.wait_ge(xT_ready, e + 1)
                    for f in range(FB):
                        pe.wait_ge(act_done, e * FB + f - (FB - 1)) if not (isinstance(e, int) and e == 0) else None
                        nc.tensor.matmul(k.ps[:, 2 + f, :], fc1[:, s, f * P:(f + 1) * P], xT[:, s, :], start=True, stop=True).then_inc(up, 1)

                def lower(e, s):
                    pe.wait_ge(act_done, (e + 1) * FB)
                    if not (isinstance(e, int) and e < 2):
                        pe.wait_ge(eo_ready, e - 1)
                    for q in range(QT):
                        for f in range(FB):
                            ins = nc.tensor.matmul(k.ps[:, 6 + s, q * P:(q + 1) * P], hh[:, s, f, q * P:(q + 1) * P], fc2[:, s, f, :],
                                                   start=(f == 0), stop=(f == FB - 1))
                    ins.then_inc(down, 1)

                turn(0, 0, 1)
                upper(0, 0, 1)
                turn(1, 1, 1)
                lower(0, 0)
                upper(1, 1, 1)
                with pe.Fori(1, E // 2) as i:
                    turn(2 * i, 0, i + 1)
                    lower(2 * i - 1, 1)
                    upper(2 * i, 0, i + 1)
                    turn(2 * i + 1, 1, i + 1)
                    lower(2 * i, 0)
                    upper(2 * i + 1, 1, i + 1)
                lower(E - 1, 1)

            @block.scalar
            def _(act):
                act.wait_ge(consts_in, 32)

                def gelus(e, s, first=False):
                    for f in range(FB):
                        act.wait_ge(up, e * FB + f + 1)
                        if f == 0 and not first:
                            act.wait_ge(down, e - 1)
                        bias = b1[:, e, f:f + 1] if isinstance(e, int) else b1[:, bass.ds(e, 1), f]
                        nc.scalar.activation(hh[:, s, f, :], k.ps[:, 2 + f, :], ACT.Gelu, bias=bias).then_inc(act_done, 1)

                gelus(0, 0, True)
                gelus(1, 1, True)
                with act.Fori(1, E // 2) as i:
                    gelus(2 * i, 0)
                    gelus(2 * i + 1, 1)

            @block.vector
            def _(dve):
                dve.wait_ge(consts_in, 32)

                def turned_in(e, s):
                    dve.wait_ge(turned, e + 1)
                    if not (isinstance(e, int) and e < 2):
                        dve.wait_ge(up, (e - 1) * FB)
                    nc.vector.tensor_copy(xT[:, s, :], k.ps[:, s, :]).then_inc(xT_ready, 1)

                def out(e, s, n):
                    dve.wait_ge(down, e + 1)
                    dve.wait_ge(eo_out[s], 16 * n)
                    row = b2[:, bass.ds(e, 1), :].broadcast_to([P, QT, D])
                    nc.vector.tensor_tensor(eo[:, s, :, :], k.ps[:, 6 + s, :].rearrange("p (q d) -> p q d", d=D), row, ALU.add).then_inc(eo_ready, 1)

                turned_in(0, 0)
                turned_in(1, 1)
                out(0, 0, 0)
                with dve.Fori(1, E // 2) as i:
                    turned_in(2 * i, 0)
                    out(2 * i - 1, 1, i - 1)
                    turned_in(2 * i + 1, 1)
                    out(2 * i, 0, i)
                out(E - 1, 1, E // 2 - 1)
                for t in range(NT):
                    n, j = t // 4, t % 4
                    if j == 0:
                        dve.wait_ge(got[n % 4], (n // 4 + 1) * 8 * 16)
                    h = r.hidden[:, t, :]
                    nc.vector.scalar_tensor_tensor(h, back[:, 0, n % 4, j, :], r.g[:, 0, t:t + 1], h, ALU.mult, ALU.add).then_inc(half_sum, 1)
                    dve.wait_ge(half_sum, t + 1)
                    nc.vector.scalar_tensor_tensor(h, back[:, 1, n % 4, j, :], r.g[:, 1, t:t + 1], h, ALU.mult, ALU.add).then_inc(summed, 1)
                for b in range(B):
                    h = r.hidden[:, b * TB:(b + 1) * TB, :]
                    xs = k.x[:, b * TB:(b + 1) * TB, :]
                    dve.wait_ge(summed, (b + 1) * TB)
                    nc.vector.tensor_tensor(h, h, k.row[:, 2, b:b + 1, :].broadcast_to([P, TB, D]), ALU.mult).then_inc(chain, 1)
                    dve.wait_ge(chain, b + 1)
                    nc.vector.tensor_tensor(xs, xs, h, ALU.add)


def causal_sublayer(nc, k, m):
    a = Core()
    a.tag, a.causal = "ca_", True
    r = Core()
    with ExitStack() as c:
        def sb(name, shape, dt=F32):
            return c.enter_context(nc.sbuf_tensor("cs_" + name, shape, dt))

        h = sb("h", [P, NT, D])
        ln1 = sb("ln1", [P, 2])
        ln2 = sb("ln2", [P, 2, 1, D])
        wo = sb("wo", [P, B, D])
        ob = sb("ob", [P, 1, D])
        zero = sb("zero", [P, CH])
        loaded, zero_set = (nc.alloc_semaphore("cs_" + n) for n in ("loaded", "zero_set"))
        r.cleared = nc.alloc_semaphore("cs_cleared")
        modulate(nc, k, "m3", k.x, h, k.row[:, 3], k.row[:, 4], B)
        with nc.Block() as block:
            @block.sync
            def _(sp):
                sp.dma_start(ln1[:], m["ln1"]).then_inc(loaded, 16)
                sp.dma_start(ln2[:].rearrange("p a b d -> p (a b d)"), m["ln2"].broadcast_to([P, 2 * D])).then_inc(loaded, 16)
                sp.dma_start(wo[:], m["ca_wo"].unsqueeze(1).broadcast_to([P, B, D])).then_inc(loaded, 16)
                sp.dma_start(ob[:].rearrange("p b d -> p (b d)"), m["ca_ob"].broadcast_to([P, D])).then_inc(loaded, 16)
                sp.wait_ge(zero_set, 1)
                sp.dma_start(k.rows_in[0:E * CAP, :].rearrange("(a p q) d -> p a (q d)", p=P, q=CH // D),
                             zero[:].unsqueeze(1).broadcast_to([P, E * CAP // (P * CH // D), CH])).then_inc(r.cleared, 16)
                sp.wait_ge(loaded, 64)

            @block.gpsimd
            def _(pool):
                nc.gpsimd.memset(zero[:], 0.0).then_inc(zero_set, 1)
        normalise(nc, k, "n4", h, k.hT, lambda b: ln1[:, 0:1], lambda b: ln1[:, 1:2])
        with ExitStack() as c2:
            a.v = c2.enter_context(nc.sbuf_tensor("ca_v", [P, NT, H, VA], F32))
            a.qk, a.o = k.qk_dram, k.o_dram
            project(nc, k, m, a)
            attend(nc, k, a)
        with nc.Block() as block:
            @block.vector
            def _(dve):
                nc.vector.tensor_tensor(h[:], h[:], ob[:].broadcast_to([P, NT, D]), ALU.add)
        join_heads(nc, k, m, a, h, wo)
        r.hidden = h
        r.xt = sb("xt", [P, NT, D])
        r.to, r.frm = sb("to", [P, 2, NT], I32), sb("frm", [P, 2, NT], I32)
        r.g = sb("g", [P, 2, NT])
        modulate(nc, k, "m5", h, r.xt, ln2[:, 0], ln2[:, 1], 1)
        route(nc, k, m, r)
        experts(nc, k, m, r)



def store(nc, k, m):
    stored = nc.alloc_semaphore("stored")
    with nc.Block() as block:
        @block.sync
        def _(sp):
            sp.dma_start(m["out"].rearrange("b (t p) d -> p (b t) d", p=P), k.x[:]).then_inc(stored, 16)
            sp.wait_ge(stored, 16)


def program(nc, m, stop):
    with ExitStack() as c:
        def sb(name, shape, dt=F32):
            return c.enter_context(nc.sbuf_tensor(name, shape, dt))

        k = Core()
        k.ps = c.enter_context(nc.psum_tensor("ps", [P, 8, CH], F32))
        k.x = sb("x_tok", [P, NT, D])
        k.hT = sb("hT", [P, TOK])
        k.cst = sb("cst", [P, C_W])
        k.cstb = sb("cstb", [P, C_FIRST], BF16)
        k.selb = sb("selb", [3 * E, E, P], BF16)
        k.ones = sb("ones", [P, P])
        k.mod = sb("mod", [P, 2, 6, B])
        k.row_of = [(0, GA), (1, GA), (1, GB), (1, CB), (1, SB)]
        k.row = sb("row", [P, 5, B, D])
        k.qk_dram = nc.dram_tensor("qk_parts", (2, H, 3, HD, TOK), BF16).ap()
        k.o_dram = nc.dram_tensor("head_sums", (B, H, VA, L), F32).ap()
        k.strip_dram = nc.dram_tensor("bias_strip", (H, STRIP), F32).ap()
        k.rows_in = nc.dram_tensor("expert_rows_in", (E * CAP + 2 * TOK, D), F32).ap()
        k.rows_out = nc.dram_tensor("expert_rows_out", (E * CAP, D), F32).ap()
        load_and_modulate(nc, k, m)
        normalise(nc, k, "n0", k.x, k.hT, lambda b: k.mod[:, 0, CA, b:b + 1], lambda b: k.mod[:, 0, SA, b:b + 1])
        selective_scan(nc, k, m)
        def mods(layer, row):
            return lambda b: k.mod[:, layer, row, b:b + 1]

        normalise(nc, k, "n1", k.x, k.hT, mods(0, CB), mods(0, SB))
        first_mixture(nc, k, m)
        with nc.cleanup_on_exit():
            normalise(nc, k, "n2", k.x, k.hT, mods(1, CA), mods(1, SA))
            biased_attention(nc, k, m)
        with nc.cleanup_on_exit():
            causal_sublayer(nc, k, m)
        store(nc, k, m)


def constants():
    import numpy as np

    a = np.zeros((P, C_W), np.float32)
    i = np.arange(P)
    a[i, C_ID + i] = 1.0
    a[i, C_FLIP + P - 1 - i] = 1.0
    a[:, C_TRI:C_TRI + P] = i[:, None] <= i[None, :]
    a[:, C_MA:C_MA + P] = np.where(i[None, :] > i[:, None], NEG, 0.0)
    a[:, C_MB:C_MB + P] = np.where(i[None, :] < i[:, None], NEG, 0.0)
    a[:, C_FIRST:C_FIRST + E] = E - np.arange(E)
    a[:, C_SLOT:C_SLOT + E] = CAP * np.arange(E)
    a[:, C_SEL:C_SEL + E] = (i[:, None] % E) == np.arange(E)[None, :]
    edges = np.array([1, 2, 3, 4, 5, 6, 7, 11, 15, 21, 30, 44, 62, 90, 128])
    rel = 255 - np.arange(STRIP)
    bucket = (np.abs(rel)[:, None] >= edges[None, :]).sum(1) + 16 * (rel > 0)
    a[bucket, C_OH + np.arange(STRIP)] = 1.0
    return a


def layouts(i):
    import numpy as np

    def c(a):
        return np.ascontiguousarray(a)

    i = {n: np.asarray(a) for n, a in i.items()}
    d = {"consts": constants(), "x": c(i["L0_attn_x"]), "c0T": c(i["L0_c"].T), "c1T": c(i["L1_c"].T),
         "L0_wmod": c(i["L0_wmod"]), "L1_wmod": c(i["L1_wmod"])}
    wx = i["L0_attn_Wxproj"]
    wp = np.zeros((D, 3, SP), np.float32)
    wp[:, 0, :NST] = wx[RANK:RANK + NST].T
    wp[:, 1, :NST] = wx[RANK + NST:].T
    wp[:, 2, :NST] = i["L0_attn_Wxs"].T
    d["ssm_wp"], d["ssm_wx"] = wp, c(wx[:RANK])
    d["ssm_wdt"] = c(np.repeat(i["L0_attn_Wdt"].T, SP, axis=1))
    col = np.zeros((P, 3), np.float32)
    wout = np.zeros((P, D), np.float32)
    for b in range(B):
        col[SP * b:SP * b + NST, 0] = i["L0_attn_A_log"][0]
        wout[SP * b:SP * b + NST] = i["L0_attn_Wout"].T
    col[:, 1] = i["L0_attn_bdt"][0]
    col[:, 2] = i["L0_attn_Dp"]
    d["ssm_col"], d["ssm_wout"] = col, wout
    d["gate_w"] = c(i["L0_ffn_Wg"].T)
    d["ffn_w1"] = c(i["L0_ffn_W1"].transpose(2, 0, 1))
    d["ffn_w3"] = c(i["L0_ffn_W3"].transpose(2, 0, 1))
    d["ffn_w2"] = c(i["L0_ffn_W2"].transpose(2, 0, 1))
    d["ffn_bias"] = c(np.stack([i["L0_ffn_b1"].T, i["L0_ffn_b3"].T], axis=1))
    d["ffn_b2"] = c(i["L0_ffn_b2"])
    d["ba_w"] = c(np.stack([i["L1_attn_W" + n].T for n in "qkv"], axis=1))
    d["ba_bias"] = np.zeros((P, 2), np.float32)
    d["ba_vb"] = np.zeros((1, D), np.float32)
    d["ba_wo"] = c(i["L1_attn_Wo"].T)
    d["rel_emb"] = c(i["L1_attn_rel_emb"])
    d["ln1"] = c(np.stack([i["L1_ffn_ln1_w"], i["L1_ffn_ln1_b"]], axis=1))
    d["ln2"] = c(np.stack([i["L1_ffn_ln2_w"], i["L1_ffn_ln2_b"]])).reshape(1, 2 * D)
    d["ca_w"] = c(np.stack([i["L1_ffn_" + n + "_w"] for n in "qkv"], axis=1))
    d["ca_bias"] = c(np.stack([i["L1_ffn_q_b"], i["L1_ffn_k_b"]], axis=1))
    d["ca_vb"] = c(i["L1_ffn_v_b"]).reshape(1, D)
    d["ca_wo"] = c(i["L1_ffn_o_w"])
    d["ca_ob"] = c(i["L1_ffn_o_b"]).reshape(1, D)
    d["router_w"] = c(i["L1_ffn_router_w"])
    d["trash_rows"] = (E * CAP + np.arange(2)[None, :, None] * TOK + np.arange(NT)[None, None, :] * P
                       + np.arange(P)[:, None, None]).astype(np.float32)
    d["fc1_w"] = c(i["L1_ffn_fc1_w"])
    d["fc2_w"] = c(i["L1_ffn_fc2_w"].reshape(E, FF // P, P, D).transpose(0, 2, 1, 3))
    d["fc1_b"] = c(i["L1_ffn_fc1_b"].reshape(E, FF // P, P).transpose(2, 0, 1))
    d["fc2_b"] = c(i["L1_ffn_fc2_b"]).reshape(1, E, D)
    return d


def kernel(**inputs):
    import concourse.bacc as _bacc
    from concourse import mybir as _mybir
    from concourse.bass_utils import run_bass_kernel_spmd as _run

    nc = _bacc.Bacc("TRN2", target_bir_lowering=False, num_devices=1)
    arrays = layouts(inputs)
    m = {n: nc.dram_tensor("in_" + n, a.shape, _mybir.dt.from_np(a.dtype), kind="ExternalInput").ap()
         for n, a in arrays.items()}
    m["out"] = nc.dram_tensor("out_x", (B, L, D), F32, kind="ExternalOutput").ap()
    program(nc, m, None)
    r = _run(nc, [{"in_" + n: a for n, a in arrays.items()}], core_ids=[0])
    return r.results[0]["out_x"]
```

```python
from contextlib import ExitStack

import concourse.bass as bass
from concourse import mybir

F32 = mybir.dt.float32
BF16 = mybir.dt.bfloat16
I32 = mybir.dt.int32
ALU = mybir.AluOpType
ACT = mybir.ActivationFunctionType
AX = mybir.AxisListType

P = 128
B, L, D = 4, 1024, 128
TOK = B * L
NT = TOK // P
TB = L // P
CH = 512
NCH = TOK // CH
EPS = 1e-5

NST = 16
RANK = 64
SP = 32
E = 16
H, HD = 16, 8
HG = 4
NG = H // HG
VA = HD + 1
NBK = 32
STRIP = 512
NEAR = 3 * P
FF = 512
CAP = 2 * (TOK // E)
KEEP = 1.0 - 0.2
NEG = -1.0e30

C_ID, C_TRI, C_MA, C_MB = 0, 128, 256, 384
C_FIRST, C_SLOT, C_OH = 512, 528, 544
C_FLIP = C_OH + STRIP
C_W = C_FLIP + P

SA, CA, GA, SB, CB, GB = range(6)


class Chain:

    def __init__(self, eng, sem):
        self.eng, self.sem, self.at, self.base = eng, sem, 0, 0

    def link(self, ins):
        ins.then_inc(self.sem, 1)
        self.at += 1
        self.eng.wait_ge(self.sem, self.base + self.at)


def col(tensor, t):
    return tensor[:, bass.ds(t, 1)]


class Core:
    pass


def load_and_modulate(nc, k, m):
    with ExitStack() as c:
        cT = c.enter_context(nc.sbuf_tensor("cT", [P, 2, B], F32))
        cS = c.enter_context(nc.sbuf_tensor("cS", [P, 2, B], F32))
        wm = c.enter_context(nc.sbuf_tensor("wm", [P, 2, 6 * D], F32))
        diag = c.enter_context(nc.sbuf_tensor("diag", [P, len(k.row_of), B, D], F32))
        t0 = c.enter_context(nc.sbuf_tensor("modt0", [P, 2, 2, B], F32))
        t1 = c.enter_context(nc.sbuf_tensor("modt1", [P, 2, 2, B], F32))
        t2 = c.enter_context(nc.sbuf_tensor("modt2", [P, 2, 2, B], F32))
        loaded = nc.alloc_semaphore("loaded")
        xloaded = nc.alloc_semaphore("xloaded")
        silu_done = nc.alloc_semaphore("silu_done")
        mod_ready = nc.alloc_semaphore("mod_ready")
        ones_ready = nc.alloc_semaphore("ones_ready")
        chain = nc.alloc_semaphore("mod_chain")
        diag_ready = nc.alloc_semaphore("diag_ready")
        rows_ready = nc.alloc_semaphore("rows_ready")
        rows_kept = nc.alloc_semaphore("rows_kept")
        pm = k.ps[:, 7, 0:2 * 6 * B].rearrange("p (l r b) -> p l r b", l=2, r=6)
        with nc.Block() as block:
            @block.sync
            def _(sp):
                sp.dma_start(cT[:, 0, :], m["c0T"]).then_inc(loaded, 16)
                sp.dma_start(cT[:, 1, :], m["c1T"]).then_inc(loaded, 16)
                sp.dma_start(k.cst[:], m["consts"]).then_inc(loaded, 16)
                sp.dma_start(wm[:, 0, :], m["L0_wmod"]).then_inc(loaded, 16)
                sp.dma_start(wm[:, 1, :], m["L1_wmod"]).then_inc(loaded, 16)
                sp.dma_start(k.x[:], m["x"].rearrange("b (t p) d -> p (b t) d", p=P)).then_inc(xloaded, 16)
                sp.wait_ge(xloaded, 16)

            @block.scalar
            def _(act):
                act.wait_ge(loaded, 5 * 16)
                nc.scalar.activation(cS[:], cT[:], ACT.Silu).then_inc(silu_done, 1)
                for i in range(len(k.row_of)):
                    act.wait_ge(rows_ready, i + 1)
                    nc.scalar.copy(k.row[:, i, :, :].rearrange("p b d -> p (b d)"), k.ps[:, i, :]).then_inc(rows_kept, 1)

            @block.tensor
            def _(pe):
                pe.wait_ge(silu_done, 1)
                for l in range(2):
                    for r in range(6):
                        ins = nc.tensor.matmul(pm[:, l, r, :], wm[:, l, r * D:(r + 1) * D], cS[:, l, :],
                                               start=True, stop=True)
                ins.then_inc(mod_ready, 1)
                pe.wait_ge(ones_ready, 1)
                for i in range(len(k.row_of)):
                    pe.wait_ge(diag_ready, 4 * (i + 1))
                    nc.tensor.matmul(k.ps[:, i, :], k.ones[:], diag[:, i, :, :].rearrange("p b d -> p (b d)"),
                                     start=True, stop=True).then_inc(rows_ready, 1)

            @block.vector
            def _(dve):
                ch = Chain(dve, chain)
                nc.vector.memset(k.ones[:], 1.0).then_inc(ones_ready, 1)
                dve.wait_ge(mod_ready, 1)
                ch.link(nc.vector.tensor_copy(k.mod[:], pm))
                ch.link(nc.vector.tensor_scalar(k.mod[:, :, CA::3, :], k.mod[:, :, CA::3, :], 1.0, None, ALU.add))
                g = k.mod[:, :, GA::3, :]
                ch.link(nc.vector.tensor_scalar(t0[:], g, 0.0, None, ALU.is_ge))
                ch.link(nc.vector.tensor_scalar(t1[:], g, 0.25, None, ALU.max))
                ch.link(nc.vector.tensor_tensor(t1[:], t1[:], t0[:], ALU.mult))
                ch.link(nc.vector.tensor_scalar(t0[:], g, 0.0, None, ALU.is_lt))
                ch.link(nc.vector.tensor_scalar(t2[:], g, -0.25, None, ALU.min))
                ch.link(nc.vector.tensor_tensor(t2[:], t2[:], t0[:], ALU.mult))
                ch.link(nc.vector.tensor_tensor(g, t1[:], t2[:], ALU.add))
                for i, (l, r) in enumerate(k.row_of):
                    for b in range(B):
                        nc.vector.tensor_scalar(diag[:, i, b, :], k.cst[:, C_ID:C_ID + D], k.mod[:, l, r, b:b + 1],
                                                None, ALU.mult).then_inc(diag_ready, 1)
                nc.vector.tensor_copy(k.cstb[:], k.cst[:, 0:C_FIRST])


def statistics(nc, dve, ch, src, stats, mean, var, dif, counted, var_ready):
    for t in range(NT):
        nc.vector.bn_stats(stats[:, t, :], src[:, t, :]).then_inc(counted, 1)
    dve.wait_ge(counted, NT)
    me, mo, qe, qo = (stats[:, :, j] for j in (1, 4, 2, 5))
    ch.link(nc.vector.tensor_tensor(mean[:], me, mo, ALU.add))
    ch.link(nc.vector.tensor_tensor(dif[:], me, mo, ALU.subtract))
    ch.link(nc.vector.tensor_tensor(var[:], qe, qo, ALU.add))
    ch.link(nc.vector.tensor_scalar(mean[:], mean[:], 0.5, None, ALU.mult))
    ch.link(nc.vector.tensor_tensor(dif[:], dif[:], dif[:], ALU.mult))
    ch.link(nc.vector.tensor_scalar(dif[:], dif[:], 0.25, EPS, ALU.mult, ALU.add))
    nc.vector.scalar_tensor_tensor(var[:], var[:], 1.0 / D, dif[:], ALU.mult, ALU.add).then_inc(var_ready, 1)


def scales(nc, dve, ch, var, mean, rstd, shift, sd_ready, rstd_ready):
    dve.wait_ge(sd_ready, 1)
    ch.link(nc.vector.reciprocal(rstd[:], var[:]))
    nc.vector.scalar_tensor_tensor(shift[:], mean[:], -1.0, rstd[:], ALU.mult, ALU.mult).then_inc(rstd_ready, 1)


def normalise(nc, k, tag, src, dst, scale_of, shift_of, loads):
    QT = CH // P
    SLOTS = 4
    with ExitStack() as c:
        def sb(name, shape, dt=F32):
            return c.enter_context(nc.sbuf_tensor(tag + name, shape, dt))

        stats = sb("stats", [P, NT, 6])
        mean, var, rstd, dif, shift = (sb(n, [P, NT]) for n in ("mean", "var", "rstd", "dif", "shift"))
        xn = sb("xn", [P, SLOTS, QT, D])
        counted, var_ready, sd_ready, chain, rstd_ready, dve_xn, pool_xn, turned, kept = (
            nc.alloc_semaphore(tag + n) for n in ("counted", "var_r", "sd", "chain", "rstd", "dve_xn", "pool_xn", "turned", "kept"))
        with nc.Block() as block:
            block.sync(loads)

            @block.vector
            def _(dve):
                ch = Chain(dve, chain)
                statistics(nc, dve, ch, src, stats, mean, var, dif, counted, var_ready)
                scales(nc, dve, ch, var, mean, rstd, shift, sd_ready, rstd_ready)
                for i in range(NCH):
                    if i >= SLOTS:
                        dve.wait_ge(turned, i - SLOTS + 1)
                    for j in range(QT - 1):
                        t = i * QT + j
                        nc.vector.tensor_scalar(xn[:, i % SLOTS, j, :], src[:, t, :], col(mean, t), col(rstd, t),
                                                ALU.subtract, ALU.mult).then_inc(dve_xn, 1)

            @block.gpsimd
            def _(pool):
                pool.wait_ge(rstd_ready, 1)
                for i in range(NCH):
                    if i >= SLOTS:
                        pool.wait_ge(turned, i - SLOTS + 1)
                    t = i * QT + QT - 1
                    nc.gpsimd.tensor_scalar(xn[:, i % SLOTS, QT - 1, :], src[:, t, :], col(mean, t), col(rstd, t),
                                            ALU.subtract, ALU.mult).then_inc(pool_xn, 1)

            @block.scalar
            def _(act):
                act.wait_ge(var_ready, 1)
                nc.scalar.activation(var[:], var[:], ACT.Sqrt).then_inc(sd_ready, 1)
                for i in range(NCH):
                    act.wait_ge(turned, i + 1)
                    b = i * CH // L
                    nc.scalar.activation(dst[:, i * CH:(i + 1) * CH], k.ps[:, i % SLOTS, :], ACT.Identity,
                                         bias=shift_of(b), scale=scale_of(b)).then_inc(kept, 1)

            @block.tensor
            def _(pe):
                for i in range(NCH):
                    if i >= SLOTS:
                        pe.wait_ge(kept, i - SLOTS + 1)
                    for j in range(QT):
                        if j < QT - 1:
                            pe.wait_ge(dve_xn, i * (QT - 1) + j + 1)
                        else:
                            pe.wait_ge(pool_xn, i + 1)
                        ins = nc.tensor.transpose(k.ps[:, i % SLOTS, j * P:(j + 1) * P], xn[:, i % SLOTS, j, :],
                                                  k.cst[:, C_ID:C_ID + P])
                    ins.then_inc(turned, 1)


def scan_sublayer(nc, k, m):
    with ExitStack() as c:
        def sb(name, shape, dt=F32):
            return c.enter_context(nc.sbuf_tensor("ss_" + name, shape, dt))

        wp = sb("wp", [P, 3, SP])
        wx = sb("wx", [RANK, D])
        wdt = sb("wdt", [RANK, SP])
        wdtx = sb("wdtx", [P, SP])
        col = sb("col", [P, 3])
        aneg = sb("aneg", [P, 1])
        wout = sb("wout", [P, B, D])
        dpg = sb("dpg", [P, B, D])
        z, e1, dt, abar, bx, hs = (sb(n, [P, L]) for n in ("z", "e1", "dt", "abar", "bx", "hs"))
        loaded, dtw, dtw_kept, proj, chain, act_done, y_ready, y_added, aready = (
            nc.alloc_semaphore("ss_" + n) for n in
            ("loaded", "dtw", "dtw_kept", "proj", "chain", "act_done", "y_ready", "y_added", "aready"))
        hs_ready, w_ready, z_ready = (nc.alloc_semaphore("ss_" + n) for n in ("hs_ready", "w_ready", "z_ready"))

        def q(i):
            return k.ps[:, 2 * i:2 * i + 2, :].rearrange("p h n -> p (h n)")

        def loads(sp):
            sp.dma_start(wp[:], m["ssm_wp"]).then_inc(loaded, 16)
            sp.dma_start(wx[:], m["ssm_wx"]).then_inc(loaded, 16)
            sp.dma_start(wdt[:], m["ssm_wdt"]).then_inc(loaded, 16)
            sp.dma_start(col[:], m["ssm_col"]).then_inc(loaded, 16)
            sp.dma_start(wout[:], m["ssm_wout"]).then_inc(loaded, 16)

        normalise(nc, k, "n0", k.x, k.hT, lambda b: k.mod[:, 0, CA, b:b + 1], lambda b: k.mod[:, 0, SA, b:b + 1], loads)
        with nc.Block() as block:
            @block.tensor
            def _(pe):
                pe.wait_ge(loaded, 5 * 16)
                nc.tensor.matmul(k.ps[:, 0, 0:SP], wx[:], wdt[:], start=True, stop=True).then_inc(dtw, 1)
                pe.wait_ge(dtw_kept, 1)
                for i in range(4):
                    for half in range(2):
                        for b in range(B):
                            w = wdtx[:] if i == 0 else wp[:, i - 1, :]
                            at = b * L + half * CH
                            ins = nc.tensor.matmul(k.ps[SP * b:SP * b + SP, 2 * i + half, :], w, k.hT[:, at:at + CH],
                                                   start=True, stop=True)
                    ins.then_inc(proj, 1)
                pe.wait_ge(hs_ready, 1)
                pe.wait_ge(w_ready, 1)
                for t in range(NT):
                    b, bank = t // TB, t // 4
                    o = k.ps[:, bank, (t % 4) * P:(t % 4 + 1) * P]
                    nc.tensor.matmul(o, hs[:, (t % TB) * P:(t % TB + 1) * P], wout[:, b, :], start=True, stop=False)
                    ins = nc.tensor.matmul(o, k.hT[:, t * P:(t + 1) * P], dpg[:, b, :], start=False, stop=True)
                    if t % 4 == 3:
                        ins.then_inc(y_ready, 1)

            @block.scalar
            def _(act):
                act.wait_ge(w_ready, 2)
                nc.scalar.activation(aneg[:], col[:, 0:1], ACT.Exp).then_inc(act_done, 1)
                act.wait_ge(z_ready, 1)
                nc.scalar.activation(e1[:], z[:], ACT.Abs).then_inc(act_done, 1)
                act.wait_ge(act_done, 2)
                nc.scalar.activation(e1[:], e1[:], ACT.Exp, scale=-1.0).then_inc(act_done, 1)
                act.wait_ge(act_done, 3)
                nc.scalar.activation(e1[:], e1[:], ACT.Ln, bias=1.0).then_inc(act_done, 1)
                act.wait_ge(aready, 3)
                nc.scalar.activation(abar[:], z[:], ACT.Exp).then_inc(act_done, 1)

            @block.vector
            def _(dve):
                ch = Chain(dve, chain)
                dve.wait_ge(loaded, 5 * 16)
                for b in range(B):
                    nc.vector.tensor_tensor(wout[:, b, :], wout[:, b, :], k.row[:, 0, b, :], ALU.mult)
                    ins = nc.vector.tensor_scalar(dpg[:, b, :], k.cst[:, C_ID:C_ID + D], col[:, 2:3],
                                                  k.mod[:, 0, GA, b:b + 1], ALU.mult, ALU.mult)
                ins.then_inc(w_ready, 1)
                nc.vector.tensor_scalar(col[:, 0:1], col[:, 0:1], 88.0, None, ALU.min).then_inc(w_ready, 1)
                dve.wait_ge(dtw, 1)
                nc.vector.tensor_copy(wdtx[:], k.ps[:, 0, 0:SP]).then_inc(dtw_kept, 1)
                dve.wait_ge(act_done, 1)
                nc.vector.tensor_scalar(aneg[:], aneg[:], -1.0, None, ALU.mult).then_inc(aready, 1)
                dve.wait_ge(proj, 1)
                nc.vector.tensor_scalar(z[:], q(0), col[:, 1:2], None, ALU.add).then_inc(z_ready, 1)
                dve.wait_ge(z_ready, 1)
                dve.wait_ge(act_done, 4)
                nc.vector.scalar_tensor_tensor(dt[:], z[:], 0.0, e1[:], ALU.max, ALU.add).then_inc(aready, 1)
                dve.wait_ge(aready, 2)
                nc.vector.tensor_scalar(z[:], dt[:], aneg[:], -104.0, ALU.mult, ALU.max).then_inc(aready, 1)
                dve.wait_ge(proj, 4)
                ch.link(nc.vector.tensor_tensor(bx[:], q(1), dt[:], ALU.mult))
                ch.link(nc.vector.tensor_tensor(bx[:], q(3), bx[:], ALU.mult))
                dve.wait_ge(act_done, 5)
                ch.link(nc.vector.tensor_tensor_scan(hs[:], abar[:], bx[:], 0.0, ALU.mult, ALU.add))
                nc.vector.tensor_tensor(hs[:], q(2), hs[:], ALU.mult).then_inc(hs_ready, 1)
                for i in range(NCH):
                    dve.wait_ge(y_ready, i + 1)
                    xs = k.x[:, 4 * i:4 * i + 4, :].rearrange("p t d -> p (t d)")
                    nc.vector.tensor_tensor(xs, xs, k.ps[:, i, :], ALU.add)


CT = CH // P


def rank(nc, ch, v, n, before, js):
    for j in js:
        vj = v[:, :, j:j + 1]
        if j + 1 < n:
            ins = nc.vector.tensor_tensor(before[:, :, j + 1:n, j], vj.broadcast_to([P, CT, n - j - 1]),
                                          v[:, :, j + 1:n], ALU.is_ge)
        if j:
            ins = nc.vector.tensor_tensor(before[:, :, 0:j, j], vj.broadcast_to([P, CT, j]), v[:, :, 0:j], ALU.is_gt)
        ins.then_inc(ch.sem, 1)
        ch.at += 1
    ch.eng.wait_ge(ch.sem, ch.base + ch.at)


def first_mixture(nc, k, m, by_distance):
    GR, PER, TOPG, TOPK, ROUTE = 4, E // 4, 2, 4, 2.5
    with ExitStack() as c:
        def sb(name, shape, dt=F32):
            return c.enter_context(nc.sbuf_tensor("gm_" + name, shape, dt))

        w1, w3, w2 = (sb(n, [P, E, D]) for n in ("w1", "w3", "w2"))
        bias, b2, wg = sb("bias", [P, 2, E]), sb("b2", [E, D]), sb("wg", [P, E])
        sg, hc = sb("sg", [P, 2, CH]), sb("hc", [P, 2, CH])
        y = sb("y", [P, NT, D])
        gated = sb("gated", [P, CT, D])
        s, w = sb("s", [P, NT, E]), sb("w", [P, NT, E])
        wc = sb("wc", [P, CT, E])
        wT = sb("wT", [E, CH])
        v, cnt = sb("v", [P, CT, E]), sb("cnt", [P, CT, E])
        gmax, gcnt = sb("gmax", [P, CT, GR]), sb("gcnt", [P, CT, GR])
        gbef, bef = sb("gbef", [P, CT, GR, GR]), sb("bef", [P, CT, E, E])
        total = sb("total", [P, CT])
        zero = sb("zero", [P, CH])
        row1 = sb("row1", [1, L], BF16)
        zero_set, cleared = nc.alloc_semaphore("gm_zero_set"), nc.alloc_semaphore("gm_cleared")
        (gate_in, loaded, logits, sig, chain, w_ready, w_turned, wT_ready, b2_done, y_begun, up, silu, prod, down,
         added, gated_step) = (
            nc.alloc_semaphore("gm_" + n) for n in
            ("gate_in", "loaded", "logits", "sig", "chain", "w_ready", "w_turned", "wT_ready", "b2_done", "y_begun",
             "up", "silu", "prod", "down", "added", "gated_step"))
        A, C, O, G, WT = 0, 2, 4, 6, 7

        def chunks(eng, body):
            with eng.Fori(0, NCH - 1) as ci:
                body(ci, True)
            body(NCH - 1, False)

        def loads(sp):
            by_distance.load(sp, m)
            sp.dma_start(wg[:], m["gate_w"]).then_inc(gate_in, 16)
            for t, name in ((w1, "w1"), (w3, "w3"), (w2, "w2"), (bias, "bias"), (b2, "b2")):
                sp.dma_start(t[:], m["ffn_" + name]).then_inc(loaded, 16)

        normalise(nc, k, "n1", k.x, k.hT, lambda b: k.mod[:, 0, CB, b:b + 1], lambda b: k.mod[:, 0, SB, b:b + 1], loads)
        with nc.Block() as block:
            @block.sync
            def _(sp):
                by_distance.spread_out(sp)
                sp.wait_ge(zero_set, 4)
                sp.dma_start(k.rows_in[0:E * CAP, 0:D].rearrange("(p a) d -> p a d", p=P),
                             zero[:, 0:D].unsqueeze(1).broadcast_to([P, E * CAP // P, D])).then_inc(cleared, 16)
                sp.dma_start(k.rows_in[0:E * CAP, D:D + 1].bitcast(I32).rearrange("(p a) b -> p (a b)", p=P), m["unused_rows"],
                             allow_slow_non_contiguous=True).then_inc(cleared, 16)
                sp.dma_start(k.rows_out[0:2 * TOK, :].rearrange("(a p q) d -> p a (q d)", p=P, q=CH // D),
                             zero[:].unsqueeze(1).broadcast_to([P, 2 * TOK // (P * CH // D), CH])).then_inc(cleared, 16)
                for base in range(2):
                    last = 64 * base + ROWS
                    for g in range(NG):
                        sp.dma_start(k.kop[last:last + 1, g, base::2, :], row1[:].unsqueeze(1).broadcast_to([1, 2, L])).then_inc(cleared, 16)
                sp.wait_ge(cleared, (3 + 2 * NG) * 16)

            @block.tensor
            def _(pe):
                def upper(n, e, chunk):
                    pe.wait_ge(prod, n + 1)
                    tok = bass.ds(chunk * CH, CH)
                    nc.tensor.matmul(k.ps[:, A + e % 2, :], w1[:, e, :], k.hT[:, tok], start=True, stop=True)
                    nc.tensor.matmul(k.ps[:, C + e % 2, :], w3[:, e, :], k.hT[:, tok], start=True, stop=True).then_inc(up, 1)

                def lower(n, e):
                    pe.wait_ge(prod, n + 3)
                    pe.wait_ge(added, n + 1)
                    for j in range(CT):
                        ins = nc.tensor.matmul(k.ps[:, O + e % 2, j * P:(j + 1) * P], hc[:, e % 2, j * P:(j + 1) * P],
                                               w2[:, e, :], start=True, stop=True)
                    ins.then_inc(down, 1)

                def turn_weights(chunk):
                    pe.wait_ge(w_ready, chunk + 1)
                    for j in range(CT):
                        ins = nc.tensor.transpose(k.ps[0:E, WT, j * P:(j + 1) * P],
                                                  wc[:, j, :],
                                                  k.cst[:, C_ID:C_ID + P])
                    ins.then_inc(w_turned, 1)

                def add_b2(chunk):
                    pe.wait_ge(wT_ready, chunk + 1)
                    for j in range(CT):
                        ins = nc.tensor.matmul(k.ps[:, G, j * P:(j + 1) * P], wT[:, j * P:(j + 1) * P], b2[:],
                                               start=True, stop=True)
                    ins.then_inc(b2_done, 1)

                by_distance.pick(pe, WT)
                pe.wait_ge(gate_in, 16)
                for t in range(NT):
                    ins = nc.tensor.matmul(k.ps[:, G, t * E:(t + 1) * E], k.hT[:, t * P:(t + 1) * P], wg[:], start=True, stop=True)
                ins.then_inc(logits, 1)
                pe.wait_ge(loaded, 5 * 16)
                upper(0, 0, 0)
                pe.wait_ge(sig, 1)
                pe.wait_ge(by_distance.strip_ready, 1)
                turn_weights(0)
                add_b2(0)

                def chunk_of(chunk, more):
                    n0 = chunk * E
                    for e in range(E):
                        if e + 1 < E:
                            upper(n0 + e + 1, e + 1, chunk)
                        elif more:
                            upper(n0 + E, 0, chunk + 1)
                        lower(n0 + e, e)
                        if more and e == E - 2:
                            turn_weights(chunk + 1)
                        if more and e == E - 1:
                            add_b2(chunk + 1)

                chunks(pe, chunk_of)

            @block.scalar
            def _(act):
                def silu_of(n, e):
                    act.wait_ge(up, n + 1)
                    act.wait_ge(prod, n + 1)
                    nc.scalar.activation(sg[:, e % 2, :], k.ps[:, A + e % 2, :], ACT.Silu,
                                         bias=bias[:, 0, e:e + 1]).then_inc(silu, 1)

                def keep_weights(chunk):
                    act.wait_ge(w_turned, chunk + 1)
                    nc.scalar.copy(wT[:], k.ps[0:E, WT, :]).then_inc(wT_ready, 1)

                def begin_y(chunk):
                    act.wait_ge(b2_done, chunk + 1)
                    nc.scalar.copy(y[:, bass.ds(chunk * CT, CT), :],
                                   k.ps[:, G, :].rearrange("p (t d) -> p t d", t=CT)).then_inc(y_begun, 1)

                act.wait_ge(logits, 1)
                nc.scalar.activation(s[:].rearrange("p t e -> p (t e)"), k.ps[:, G, :], ACT.Sigmoid).then_inc(sig, 1)
                by_distance.exps(act, WT)
                act.wait_ge(loaded, 5 * 16)
                silu_of(0, 0)
                keep_weights(0)
                begin_y(0)

                def chunk_of(chunk, more):
                    n0 = chunk * E
                    for e in range(E):
                        if e + 1 < E or more:
                            silu_of(n0 + e + 1, (e + 1) % E)
                        if more and e == E - 2:
                            keep_weights(chunk + 1)
                        if more and e == E - 1:
                            begin_y(chunk + 1)

                chunks(act, chunk_of)

            @block.vector
            def _(dve):
                ch = Chain(dve, chain)

                def route(chunk, step):
                    tiles = bass.ds(chunk * CT, CT)
                    sc = s[:, tiles, :]
                    if step == 0:
                        ch.link(nc.vector.tensor_reduce(gmax[:], sc.rearrange("p t (g e) -> p t g e", g=GR), AX.X, ALU.max))
                        rank(nc, ch, gmax, GR, gbef, range(GR))
                    elif step == 1:
                        ch.link(nc.vector.tensor_reduce(gcnt[:], gbef[:], AX.X, ALU.add))
                        ch.link(nc.vector.tensor_scalar(gcnt[:], gcnt[:], float(TOPG), -4.0, ALU.is_ge, ALU.mult))
                        ch.link(nc.vector.tensor_tensor(v[:].rearrange("p t (g e) -> p t g e", g=GR),
                                                        sc.rearrange("p t (g e) -> p t g e", g=GR),
                                                        gcnt[:].unsqueeze(3).broadcast_to([P, CT, GR, PER]), ALU.add))
                    elif step < 10:
                        rank(nc, ch, v, E, bef, (2 * step - 4, 2 * step - 3))
                    elif step == 10:
                        ch.link(nc.vector.tensor_reduce(cnt[:], bef[:], AX.X, ALU.add))
                    elif step == 11:
                        ch.link(nc.vector.scalar_tensor_tensor(v[:], cnt[:], float(TOPK), sc, ALU.is_lt, ALU.mult))
                        ch.link(nc.vector.tensor_reduce(total[:], v[:], AX.X, ALU.add))
                    elif step == 12:
                        ch.link(nc.vector.reciprocal(total[:], total[:]))
                        ch.link(nc.vector.tensor_scalar(total[:], total[:], ROUTE, None, ALU.mult))
                    elif step == 13:
                        if not (isinstance(chunk, int) and chunk == 0):
                            dve.wait_ge(w_turned, chunk)
                        ch.link(nc.vector.tensor_tensor(wc[:], v[:], total[:].unsqueeze(2).broadcast_to([P, CT, E]), ALU.mult))
                        nc.vector.tensor_copy(w[:, tiles, :], wc[:]).then_inc(w_ready, 1)

                def product(n, e):
                    dve.wait_ge(silu, n + 1)
                    dve.wait_ge(down, n + 1)
                    nc.vector.scalar_tensor_tensor(hc[:, e % 2, :], k.ps[:, C + e % 2, :], bias[:, 1, e:e + 1],
                                                   sg[:, e % 2, :], ALU.add, ALU.mult).then_inc(prod, 1)

                def add(n, chunk, e):
                    dve.wait_ge(down, n + 3)
                    dve.wait_ge(added, n + 2)
                    if e == 0:
                        dve.wait_ge(y_begun, chunk + 1)
                        dve.wait_ge(w_ready, chunk + 1)
                    for j in range(CT):
                        t = bass.ds(chunk * CT + j, 1)
                        yt = y[:, t, :].rearrange("p a d -> p (a d)")
                        ins = nc.vector.scalar_tensor_tensor(yt, k.ps[:, O + e % 2, j * P:(j + 1) * P],
                                                             w[:, t, e], yt, ALU.mult, ALU.add)
                    ins.then_inc(added, 1)

                dve.sem_inc(prod, 2)
                dve.sem_inc(added, 2)
                dve.sem_inc(down, 2)
                ch.link(nc.vector.memset(gbef[:], 0.0))
                ch.link(nc.vector.memset(bef[:], 0.0))
                by_distance.largest(dve, WT)
                dve.wait_ge(sig, 1)
                for step in range(14):
                    route(0, step)
                links = ch.at - 2
                product(0, 0)

                def chunk_of(chunk, more):
                    n0 = chunk * E
                    if more:
                        ch.base, ch.at = (chunk + 1) * links, 2
                    for e in range(E):
                        if e + 1 < E or more:
                            product(n0 + e + 1, (e + 1) % E)
                        if more:
                            route(chunk + 1, e)
                        add(n0 + e, chunk, e)

                chunks(dve, chunk_of)

            @block.gpsimd
            def _(pool):
                nc.gpsimd.memset(zero[:], 0.0).then_inc(zero_set, 1)
                nc.gpsimd.memset(k.kop[:].rearrange("p g a n -> p (g a n)").bitcast(I32), 0).then_inc(zero_set, 1)
                nc.gpsimd.memset(k.qop[:].rearrange("p g a n -> p (g a n)").bitcast(I32), 0).then_inc(zero_set, 1)
                nc.gpsimd.memset(k.row0[:], 0.0)
                nc.gpsimd.memset(row1[:], 1.0).then_inc(zero_set, 1)
                pool.sem_inc(gated_step, 1)
                with pool.Fori(0, B) as b:
                    with pool.Fori(0, L // CH) as half:
                        chunk = b * (L // CH) + half
                        tiles = bass.ds(chunk * CT, CT)
                        pool.wait_ge(added, (chunk + 1) * E + 2)
                        gate = k.row[:, 5, bass.ds(b, 1), :].broadcast_to([P, CT, D])
                        pool.wait_ge(gated_step, 2 * chunk + 1)
                        nc.gpsimd.tensor_tensor(gated[:], y[:, tiles, :], gate, ALU.mult).then_inc(gated_step, 1)
                        pool.wait_ge(gated_step, 2 * chunk + 2)
                        nc.gpsimd.tensor_tensor(k.x[:, tiles, :], k.x[:, tiles, :], gated[:], ALU.add).then_inc(gated_step, 1)


def attention_inputs(nc, m, a, c):
    def sb(name, shape):
        return c.enter_context(nc.sbuf_tensor(a.tag + name, shape, F32))

    a.w, a.bias, a.vb = sb("w", [P, 3, D]), sb("bias", [P, 2]), sb("vb", [P, D])
    a.w_in = nc.alloc_semaphore(a.tag + "w_in")
    a.loads = [nc.alloc_semaphore(a.tag + f"loads{g}") for g in range(NG)]

    def loads(sp):
        sp.dma_start(a.w[:], m[a.tag + "w"]).then_inc(a.w_in, 16)
        sp.dma_start(a.bias[:], m[a.tag + "bias"]).then_inc(a.w_in, 16)
        sp.dma_start(a.vb[:], m[a.tag + "vb"].broadcast_to([P, D])).then_inc(a.w_in, 16)
        if a.causal:
            sp.dma_start(a.ob[:].rearrange("p b d -> p (b d)"), m["ca_ob"].broadcast_to([P, D])).then_inc(a.w_in, 16)

    return loads


def project(nc, k, m, a):
    tag = a.tag + "pr_"
    SLOTS = 3
    FLIPS = H * NEAR // CH
    with ExitStack() as c:
        def sb(name, shape, dt=F32):
            return c.enter_context(nc.sbuf_tensor(tag + name, shape, dt))

        w, bias = a.w, a.bias
        full = sb("full", [P, SLOTS, 2, CH])
        rest = sb("rest", [P, SLOTS, 2, CH])
        parts = sb("parts", [P, 2, 2, 3, L], BF16)
        loaded = a.w_in
        done, v_done, v_kept = (nc.alloc_semaphore(tag + n) for n in ("done", "v_done", "v_kept"))
        stored = [nc.alloc_semaphore(tag + f"stored{s}") for s in range(2)]
        whole, part1, rest1, part2, rest2 = (
            [nc.alloc_semaphore(tag + f"{n}{o}") for o in "qk"] for n in ("whole", "part1_", "rest1_", "part2_", "rest2_"))
        scale = (HD ** -0.5, 1.0)
        CB_ = L // CH

        def flips(i):
            return range(i * FLIPS // NCH, (i + 1) * FLIPS // NCH)

        def part(o, n, i):
            return parts[:, i // CB_ % 2, o, n, i % CB_ * CH:(i % CB_ + 1) * CH]
        if not a.causal:
            flipped, near_kept = nc.alloc_semaphore("rb_flipped"), nc.alloc_semaphore("rb_near_kept")
            near = a.near[:].rearrange("p h q -> p (h q)")

        with nc.Block() as block:
            @block.sync
            def _(sp):
                for b in range(B):
                    for n in range(3):
                        for o in range(2):
                            sp.wait_ge((part1, part2, rest2)[n][o], CB_ * (b + 1))
                            sp.dma_start(a.qk[o, :, n if o else 2 - n, :, b * L:(b + 1) * L],
                                         parts[:, b % 2, o, n, :]).then_inc(stored[b % 2], 16)
                    if b == 1:
                        sp.wait_ge(stored[0], 6 * 16)
                        load_operands(sp, k, a, 0, 0)
                for s in range(2):
                    sp.wait_ge(stored[s], B // 2 * 6 * 16)

            @block.tensor
            def _(pe):
                pe.wait_ge(loaded, (4 if a.causal else 3) * 16)
                for i in range(NCH):
                    if i >= 2:
                        for o in range(2):
                            pe.wait_ge(whole[o], i - 1)
                        pe.wait_ge(v_kept, i - 1)
                    for o in range(2):
                        ins = nc.tensor.matmul(k.ps[:, 2 * o + i % 2, :], w[:, o, :], k.hT[:, i * CH:(i + 1) * CH],
                                               start=True, stop=True)
                        ins.then_inc(done, 1)
                    for j in range(4):
                        t = 4 * i + j
                        ins = nc.tensor.matmul(k.ps[:, 4 + i % 2, j * P:(j + 1) * P], k.hT[:, t * P:(t + 1) * P],
                                               w[:, 2, :], start=True, stop=True)
                    ins.then_inc(v_done, 1)
                    if not a.causal:
                        for f in flips(i):
                            if f >= 2:
                                pe.wait_ge(near_kept, f - 1)
                            nc.tensor.matmul(k.ps[:, 6 + f % 2, :], k.cst[:, C_FLIP:C_FLIP + P], near[:, f * CH:(f + 1) * CH],
                                             start=True, stop=True).then_inc(flipped, 1)

            def first_rest(eng, o, i):
                s = i % SLOTS
                eng.wait_ge(part1[o], i + 1)
                if i >= SLOTS:
                    eng.wait_ge(rest2[o], i - SLOTS + 1)
                eng.tensor_tensor(rest[:, s, o, :], full[:, s, o, :], part(o, 0, i), ALU.subtract).then_inc(rest1[o], 1)

            def third_part(eng, o, i):
                s = i % SLOTS
                eng.wait_ge(part2[o], i + 1)
                eng.tensor_tensor(part(o, 2, i), rest[:, s, o, :], part(o, 1, i), ALU.subtract).then_inc(rest2[o], 1)

            @block.scalar
            def _(act):
                for i in range(NCH + 1):
                    for o in range(2):
                        if i < NCH:
                            s = i % SLOTS
                            act.wait_ge(whole[o], i + 1)
                            if i >= 2 * CB_:
                                act.wait_ge(stored[i // CB_ % 2], i // (2 * CB_) * 6 * 16)
                            nc.scalar.copy(part(o, 0, i), full[:, s, o, :]).then_inc(part1[o], 1)
                        if i:
                            s = (i - 1) % SLOTS
                            act.wait_ge(rest1[o], i)
                            nc.scalar.copy(part(o, 1, i - 1), rest[:, s, o, :]).then_inc(part2[o], 1)
                    if not a.causal and i < NCH:
                        for f in flips(i):
                            act.wait_ge(flipped, f + 1)
                            nc.scalar.copy(near[:, f * CH:(f + 1) * CH], k.ps[:, 6 + f % 2, :]).then_inc(near_kept, 1)

            @block.gpsimd
            def _(pool):
                for i in range(NCH + 1):
                    if i < NCH:
                        first_rest(nc.gpsimd, 1, i)
                    if i:
                        third_part(nc.gpsimd, 1, i - 1)

            @block.vector
            def _(dve):
                nc.vector.memset(a.v[:, :, :, HD:VA], 1.0)
                dve.wait_ge(loaded, (4 if a.causal else 3) * 16)
                for i in range(NCH + 1):
                    if i < NCH:
                        for o in range(2):
                            dve.wait_ge(done, 2 * i + o + 1)
                            if i >= SLOTS:
                                dve.wait_ge(rest1[o], i - SLOTS + 1)
                            nc.vector.tensor_scalar(full[:, i % SLOTS, o, :], k.ps[:, 2 * o + i % 2, :], bias[:, o:o + 1], scale[o],
                                                    ALU.add, ALU.mult).then_inc(whole[o], 1)
                    if i:
                        first_rest(nc.vector, 0, i - 1)
                    if i < NCH:
                        dve.wait_ge(v_done, i + 1)
                        out = a.v[:, 4 * i:4 * i + 4, :, 0:HD]
                        src = k.ps[:, 4 + i % 2, :].rearrange("p (t h d) -> p t h d", h=H, d=HD)
                        row = a.vb[:].rearrange("p (t h d) -> p t h d", t=1, d=HD).broadcast_to([P, 4, H, HD])
                        nc.vector.tensor_tensor(out, src, row, ALU.add).then_inc(v_kept, 1)
                    if i:
                        third_part(nc.vector, 0, i - 1)


ROWS = 6 * HD
NLOAD = 14 * 16


def load_operands(sp, k, a, b, g):
    for base in range(2):
        last = 64 * base + ROWS
        sp.dma_start(k.qop[last:last + 1, g, :, :], k.row0[:].unsqueeze(1).broadcast_to([1, 2, L])).then_inc(a.loads[g], 16)
        for o in range(2):
            row = 64 * base
            for n in (3, 2, 1):
                start = a.qk[o, g * HG + base, 3 - n if o == 0 else 0, :, bass.ds(b * L, L)]
                rows = bass.AP(start.tensor, start.offset, [[TOK, n * HD], [2 * 3 * HD * TOK, 2], [1, L]])
                slot = k.qop[row:row + n * HD, g, :, :] if o == 0 else k.kop[row:row + n * HD, g, base::2, :]
                sp.dma_start(slot, rows).then_inc(a.loads[g], 16)
                row += n * HD


def attend(nc, k, a):
    causal, tag = a.causal, a.tag + "at_"
    RING = 16
    LAG = 2
    NV = 1 if causal else 3
    NBANK = 3
    AHEAD = 0.13
    GAP = 3

    def pieces():
        order = ([0, 1, 2, 3, 4, 5, 6, 7],) * 2 if causal else ([1, 5, 2, 6, 0, 7, 3, 4], [3, 0, 6, 1, 5, 2, 7, 4])
        out = []
        for half in range(2):
            for i in order[half]:
                q0, q1 = half * CH, (half + 1) * CH
                if causal:
                    q0 = max(q0, i * P)
                if q0 < q1:
                    out.append((i, half, q0, q1))
        return out

    PIECES = pieces()
    NP_ = len(PIECES)
    NB_ = NP_ * HG
    NA_ = HG * TB + 1
    last_of = {half: max(n for n, p in enumerate(PIECES) if p[1] == half) for half in range(2)}
    first_of = {half: min(n for n, p in enumerate(PIECES) if p[1] == half) for half in range(2)}

    def near(n):
        i, half, q0, q1 = PIECES[n]
        lo, hi = max(q0, (i - 1) * P), min(q1, (i + 2) * P)
        return (lo, hi) if lo < hi and not causal else None

    def segments(n):
        i, half, q0, q1 = PIECES[n]
        if causal:
            return [(0, q0, q1)]
        cuts = [(2, q0, min(q1, (i - 1) * P)), (0, max(q0, (i - 1) * P), min(q1, (i + 2) * P)), (1, max(q0, (i + 2) * P), q1)]
        return [s for s in cuts if s[1] < s[2]]

    def value_parts(n):
        segs = segments(n)
        if len(segs) == 1 and segs[0][2] - segs[0][1] > P:
            var, s0, s1 = segs[0]
            mid = s0 + (s1 - s0) // P // 2 * P
            segs = [(var, s0, mid), (var, mid, s1)]
        return segs[:(len(segs) + 1) // 2], segs[(len(segs) + 1) // 2:]

    TILES = [7, 0, 6, 1, 5, 2, 4, 3]

    def top_of(n):
        return n // TB, TILES[n % TB]

    def top_keys(n):
        return (top_of(n)[1] + 1) * P if causal else L

    def plan_tops():
        a = [top_keys(n) + 64 for n in range(NA_ - 1)]
        b = [p[3] - p[2] + 64 for p in PIECES for _ in range(HG)]
        ends = [sum(a[:n + 1]) / sum(a) - AHEAD for n in range(NA_ - 1)]
        out = [[] for _ in b]

        def turn_at(x):
            return min(t for t in range(len(b)) if sum(b[:t + 1]) >= x * sum(b) - 1e-6)

        for n, x in enumerate(ends):
            if x > 0:
                out[turn_at(x)].append((0, n))
        last = turn_at(ends[-1]) + GAP
        out[last].append((0, NA_ - 1))
        for n, x in enumerate(ends):
            if x <= 0:
                out[max(last, turn_at(1 + x))].append((1, n))
        return out

    NEARS = [n for n in range(NP_) if near(n)]

    with ExitStack() as c:
        def sb(name, shape, dt=F32):
            return c.enter_context(nc.sbuf_tensor(tag + name, shape, dt))

        def sem(name):
            return nc.alloc_semaphore(tag + name)

        qop, kop, loads = k.qop, k.kop, a.loads
        top = sb("top", [P, HG * TB])
        negm = sb("negm", [HG * TB, P], BF16)
        ring = sb("ring", [P, RING, CH])
        vs = sb("vs", [P, 2, NV, TB, HG, 32])
        osb = sb("osb", [P, L])
        mrow = [sem(f"mrow{g}") for g in range(NG)]
        stored = sem("stored")
        (a_filled, a_read, b_filled, exped, scaled, pv_done, o_copied,
         vs_zero, vs_ready) = (sem(n) for n in
                               ("a_filled", "a_read", "b_filled", "exped", "scaled",
                                "pv_done", "o_copied", "vs_zero", "vs_ready"))
        A_BANK, B_BANK, O_BANK = 0, 4, 7

        def place(j):
            return 64 * (j % 2), j // 2

        def unit(b, g):
            return b * NG + g

        def after(b, g):
            return (b, g + 1) if g < NG - 1 else (b + 1, 0)

        def before(b, g):
            return (b, g - 1) if g else (b - 1, NG - 1)

        def units(eng, one):
            one(0, 0)
            with eng.Fori(0, B - 1) as b:
                for g in range(1, NG):
                    one(b, g)
                one(b + 1, 0)
            for g in range(1, NG):
                one(B - 1, g)

        def is_first(b, g):
            return isinstance(b, int) and b == 0 and g == 0

        def is_last(b, g):
            return isinstance(b, int) and b == B - 1 and g == NG - 1

        def bank_of(g, t):
            return (g * NB_ + t) % NBANK

        def bank_free(g, t):
            if t >= NBANK:
                return t - NBANK + 1
            last = (g - 1) % NG
            return max(x + 1 - NB_ for x in range(NB_) if bank_of(last, x) == bank_of(g, t) and x + 1 - NB_ <= 0)

        with nc.Block() as block:
            @block.sync
            def _(sp):
                def largest(b, g):
                    sp.wait_ge(a_read, (unit(b, g) + 1) * NA_)
                    for j in range(HG):
                        base, pair = place(j)
                        sp.dma_start(qop[base + ROWS:base + ROWS + 1, g, pair, :],
                                     negm[j * TB:(j + 1) * TB, :]).then_inc(mrow[g], 16)

                def store(b, g):
                    u = unit(b, g)
                    sp.wait_ge(o_copied, 2 * (u + 1))
                    for j in range(HG):
                        sp.dma_start(a.o[b, g * HG + j, :, :], osb[32 * j:32 * j + VA, :]).then_inc(stored, 16)

                def step(b, g):
                    far = after(*after(b, g))
                    if not (isinstance(far[0], int) and far[0] == B):
                        if not is_first(b, g):
                            sp.wait_ge(pv_done, unit(b, g) * NP_ - LAG)
                        load_operands(sp, k, a, *far)
                    if not is_last(b, g):
                        largest(*after(b, g))
                    store(b, g)

                load_operands(sp, k, a, 0, 1)
                largest(0, 0)
                units(sp, step)
                sp.wait_ge(stored, B * NG * HG * 16)

            @block.tensor
            def _(pe):
                def top_turn(b, g, n):
                    turn = unit(b, g) * NA_ + n
                    slot = A_BANK + 2 * ((g * NA_ + n) % 2)
                    if n == 0:
                        pe.wait_ge(loads[g], (b + 1) * NLOAD)
                    if not (isinstance(turn, int) and turn < 2):
                        pe.wait_ge(a_read, turn - 1)
                    if n == NA_ - 1:
                        pe.wait_ge(a_read, turn)
                        nc.tensor.transpose(k.ps[0:HG * TB, slot, 0:P], top[:], k.cst[:, C_ID:C_ID + P]).then_inc(a_filled, 1)
                        return
                    j, i = top_of(n)
                    pair = j // 2
                    keys = top_keys(n)
                    for half in range(2):
                        k0, k1 = half * CH, min(keys, (half + 1) * CH)
                        if k0 >= k1:
                            continue
                        diag = causal and k0 <= i * P < k1
                        ins = nc.tensor.matmul(k.ps[:, slot + half, 0:k1 - k0], qop[:, g, pair, i * P:(i + 1) * P],
                                               kop[:, g, j, k0:k1], start=True, stop=not diag)
                        if diag:
                            ins = nc.tensor.matmul(k.ps[:, slot + half, i * P - k0:(i + 1) * P - k0], k.cstb[:, C_ID:C_ID + P],
                                                   k.cstb[:, C_MA:C_MA + P], start=False, stop=True)
                    ins.then_inc(a_filled, 1)

                def score_turn(b, g, t):
                    n, j = t // HG, t % HG
                    i, half, q0, q1 = PIECES[n]
                    pair = j // 2
                    u = unit(b, g)
                    if t == 0:
                        pe.wait_ge(mrow[g], (b + 1) * HG * 16)
                    if not is_first(b, g) or t >= NBANK:
                        pe.wait_ge(exped, u * NB_ + bank_free(g, t))
                    bank = B_BANK + bank_of(g, t)
                    diag = causal and q0 == i * P
                    ins = nc.tensor.matmul(k.ps[:, bank, 0:q1 - q0], kop[:, g, j, i * P:(i + 1) * P],
                                           qop[:, g, pair, q0:q1], start=True, stop=not diag)
                    if diag:
                        ins = nc.tensor.matmul(k.ps[:, bank, 0:P], k.cstb[:, C_ID:C_ID + P], k.cstb[:, C_MB:C_MB + P],
                                               start=False, stop=True)
                    ins.then_inc(b_filled, 1)

                def value_turn(b, g, n, part):
                    i, half, q0, q1 = PIECES[n]
                    u = unit(b, g)
                    parts = value_parts(n)
                    if part == 0:
                        if n == 0:
                            pe.wait_ge(vs_ready, u + 1)
                        if n == first_of[half] and not (is_first(b, g) and half == 0):
                            pe.wait_ge(o_copied, 2 * u + half)
                        pe.wait_ge(exped, u * NB_ + (n + 1) * HG)
                        if n in NEARS:
                            pe.wait_ge(scaled, u * len(NEARS) + NEARS.index(n) + 1)
                    for x, (var, s0, s1) in enumerate(parts[part]):
                        for j in range(HG):
                            ins = nc.tensor.matmul(k.ps[32 * j:32 * j + 32, O_BANK, s0 - half * CH:s1 - half * CH],
                                                   vs[:, g % 2, var, i, j, :], ring[:, (n % (RING // HG)) * HG + j, s0 - q0:s1 - q0],
                                                   start=(n == first_of[half] and part == 0 and x == 0),
                                                   stop=(n == last_of[half] and x == len(parts[part]) - 1 and (part == 1 or not parts[1])),
                                                   skip_group_check=True)
                    if part == 1 or not parts[1]:
                        ins.then_inc(pv_done, 1)

                TOPS = plan_tops()

                def run(b, g):
                    for n in range(NP_):
                        if n >= LAG:
                            owner, vn = (b, g), n - LAG
                        else:
                            owner, vn = None if is_first(b, g) else before(b, g), NP_ - LAG + n
                        for j in range(HG):
                            t = n * HG + j
                            score_turn(b, g, t)
                            for far, x in TOPS[t]:
                                of = after(*after(b, g)) if far else after(b, g)
                                if not (isinstance(of[0], int) and of[0] == B):
                                    top_turn(*of, x)
                            if owner and j == 1:
                                value_turn(*owner, vn, 0)
                            if owner and j == 3 and value_parts(vn)[1]:
                                value_turn(*owner, vn, 1)

                for n in range(NA_):
                    top_turn(0, 0, n)
                for n in sorted(x for turns in TOPS for far, x in turns if far):
                    top_turn(0, 1, n)
                units(pe, run)
                for n in range(NP_ - LAG, NP_):
                    for part in range(2):
                        if value_parts(n)[part]:
                            value_turn(B - 1, NG - 1, n, part)

            @block.vector
            def _(dve):
                def tops(b, g):
                    for n in range(NA_):
                        turn = unit(b, g) * NA_ + n
                        slot = A_BANK + 2 * ((g * NA_ + n) % 2)
                        dve.wait_ge(a_filled, turn + 1)
                        if n == NA_ - 1:
                            if not is_first(b, g):
                                pb, pg = before(b, g)
                                dve.wait_ge(mrow[pg], (pb + 1) * HG * 16)
                            nc.vector.tensor_scalar(negm[:], k.ps[0:HG * TB, slot, 0:P], -1.0, None, ALU.mult).then_inc(a_read, 1)
                        else:
                            keys = top_keys(n)
                            src = k.ps[:, slot:slot + 2, :].rearrange("p a n -> p (a n)")[:, 0:keys]
                            j, i = top_of(n)
                            nc.vector.tensor_reduce(top[:, j * TB + i:j * TB + i + 1], src, AX.X, ALU.max).then_inc(a_read, 1)

                units(dve, tops)

            @block.scalar
            def _(act):
                def copy_out(b, g, half):
                    u = unit(b, g)
                    if half == 0 and not is_first(b, g):
                        act.wait_ge(stored, u * HG * 16)
                    act.wait_ge(pv_done, u * NP_ + last_of[half] + 1)
                    nc.scalar.copy(osb[:, half * CH:(half + 1) * CH], k.ps[:, O_BANK, :]).then_inc(o_copied, 1)

                def exps(b, g):
                    u = unit(b, g)
                    for t in range(NB_):
                        n = t // HG
                        i, half, q0, q1 = PIECES[n]
                        if t == LAG * HG and not is_first(b, g):
                            copy_out(*before(b, g), 1)
                        if t == (last_of[0] + 1 + LAG) * HG:
                            copy_out(b, g, 0)
                        act.wait_ge(b_filled, u * NB_ + t + 1)
                        if t % HG == 0 and (n >= RING // HG or not is_first(b, g)):
                            act.wait_ge(pv_done, u * NP_ + n + 1 - RING // HG)
                        nc.scalar.activation(ring[:, t % RING, 0:q1 - q0], k.ps[:, B_BANK + bank_of(g, t), 0:q1 - q0],
                                             ACT.Exp).then_inc(exped, 1)

                units(act, exps)
                copy_out(B - 1, NG - 1, 1)

            @block.gpsimd
            def _(pool):
                def values(b, g):
                    s = g % 2
                    src = a.v[:, bass.ds(b * TB, TB), g * HG:(g + 1) * HG, :]
                    ins = nc.gpsimd.tensor_copy(vs[:, s, 0, :, :, 0:VA], src)
                    if not causal:
                        for var, f in ((1, a.left), (2, a.right)):
                            by = f[:, g * HG:(g + 1) * HG].unsqueeze(1).unsqueeze(3).broadcast_to([P, TB, HG, VA])
                            ins = nc.gpsimd.tensor_tensor(vs[:, s, var, :, :, 0:VA], src, by, ALU.mult)
                    ins.then_inc(vs_ready, 1)

                def next_values(b, g):
                    if is_last(b, g):
                        return
                    if not is_first(b, g):
                        pool.wait_ge(pv_done, unit(b, g) * NP_)
                    values(*after(b, g))

                def bias(b, g):
                    u = unit(b, g)
                    for n in NEARS:
                        i, half, q0, q1 = PIECES[n]
                        if n == NEARS[len(NEARS) // 2]:
                            next_values(b, g)
                        lo, hi = near(n)
                        for j in range(HG):
                            pool.wait_ge(exped, u * NB_ + n * HG + j + 1)
                            w = ring[:, (n * HG + j) % RING, lo - q0:hi - q0]
                            ins = nc.gpsimd.tensor_tensor(w, w, a.near[:, g * HG + j, lo - (i - 1) * P:hi - (i - 1) * P], ALU.mult)
                        ins.then_inc(scaled, 1)

                nc.gpsimd.memset(vs[:], 0.0).then_inc(vs_zero, 1)
                pool.wait_ge(vs_zero, 1)
                values(0, 0)
                units(pool, next_values if causal else bias)


def join_heads(nc, k, m, a, dst, before):
    tag = a.tag + "jo_"
    with ExitStack() as c:
        num = c.enter_context(nc.sbuf_tensor(tag + "num", [P, B, L], F32))
        den = c.enter_context(nc.sbuf_tensor(tag + "den", [P, B, L], F32))
        few = c.enter_context(nc.sbuf_tensor(tag + "few", [P, B, P], F32))
        loaded, few_in, few_out = ([nc.alloc_semaphore(tag + f"{n}{b}") for b in range(B)] for n in ("loaded", "few_in", "few_out"))
        wo = c.enter_context(nc.sbuf_tensor(tag + "wo", [P, B, D], F32))
        inv, ready, y_ready, begun, wo_in = (nc.alloc_semaphore(tag + n) for n in ("inv", "ready", "y_ready", "begun", "wo_in"))
        with nc.Block() as block:
            @block.sync
            def _(sp):
                def sums(b):
                    return bass.AP(a.o.tensor, b * H * VA * L + HD * L, [[VA * L, H], [P, L // P], [1, P]])

                def few_of(b):
                    return few[:, b, :]

                sp.dma_start(wo[:], m[a.tag + "wo"].unsqueeze(1).broadcast_to([P, B, D])).then_inc(wo_in, 16)
                for b in range(B):
                    sp.dma_start(few_of(b), sums(b)).then_inc(few_in[b], 16)
                for b in range(B):
                    sp.dma_start(num[:, b, :], bass.AP(a.o.tensor, b * H * VA * L, [[VA * L, H], [L, HD], [1, L]])).then_inc(loaded[b], 16)
                for b in range(B):
                    sp.wait_ge(inv, b + 1)
                    sp.dma_start(sums(b), few_of(b)).then_inc(few_out[b], 16)
                for b in range(B):
                    sp.wait_ge(few_out[b], 16)
                    sp.dma_start(den[:, b, :], bass.AP(a.o.tensor, b * H * VA * L + HD * L, [[VA * L, H], [0, HD], [1, L]])).then_inc(loaded[b], 16)

            @block.vector
            def _(dve):
                dve.wait_ge(wo_in, 16)
                before(wo).then_inc(begun, 1)
                for b in range(B):
                    dve.wait_ge(few_in[b], 16)
                    nc.vector.reciprocal(few[:, b, :], few[:, b, :]).then_inc(inv, 1)
                for b in range(B + 1):
                    if b < B:
                        dve.wait_ge(loaded[b], 32)
                        nc.vector.tensor_tensor(num[:, b, :], num[:, b, :], den[:, b, :], ALU.mult).then_inc(ready, 1)
                    if b:
                        if b == 1:
                            dve.wait_ge(begun, 1)
                        for i in (2 * b - 2, 2 * b - 1):
                            dve.wait_ge(y_ready, i + 1)
                            xs = dst[:, 4 * i:4 * i + 4, :].rearrange("p t d -> p (t d)")
                            nc.vector.tensor_tensor(xs, xs, k.ps[:, i, :], ALU.add)

            @block.tensor
            def _(pe):
                pe.wait_ge(begun, 1)
                for t in range(NT):
                    b = t // TB
                    if t % TB == 0:
                        pe.wait_ge(ready, b + 1)
                    ins = nc.tensor.matmul(k.ps[:, t // 4, (t % 4) * P:(t % 4 + 1) * P], num[:, b, (t % TB) * P:(t % TB + 1) * P],
                                           wo[:, b, :], start=True, stop=True)
                    if t % 4 == 3:
                        ins.then_inc(y_ready, 1)


class BiasByDistance:

    def __init__(self, nc, k, c):
        def sb(name, shape):
            return c.enter_context(nc.sbuf_tensor("rb_" + name, shape, F32))

        self.nc, self.k = nc, k
        self.near, self.left, self.right = sb("near", [P, H, NEAR]), sb("left", [P, H]), sb("right", [P, H])
        self.rel, self.top, self.strip = sb("rel", [NBK, H]), sb("top", [H, 1]), sb("strip", [H, STRIP])
        self.rel_in, self.picked, self.top_ready, self.strip_ready, self.strip_out, self.spread = (
            nc.alloc_semaphore("rb_" + n) for n in ("rel_in", "picked", "top", "strip_r", "strip_out", "spread"))

    def load(self, sp, m):
        sp.dma_start(self.rel[:], m["rel_emb"]).then_inc(self.rel_in, 16)

    def spread_out(self, sp):
        dram = self.k.strip_dram
        sp.wait_ge(self.strip_ready, 1)
        sp.dma_start(dram, self.strip[:]).then_inc(self.strip_out, 16)
        sp.wait_ge(self.strip_out, 16)
        sp.dma_start(self.near[:], bass.AP(dram.tensor, 0, [[1, P], [STRIP, H], [1, NEAR]])).then_inc(self.spread, 16)
        sp.dma_start(self.left[:], bass.AP(dram.tensor, STRIP - 1, [[0, P], [STRIP, H]]),
                     allow_slow_non_contiguous=True).then_inc(self.spread, 16)
        sp.dma_start(self.right[:], bass.AP(dram.tensor, 0, [[0, P], [STRIP, H]]),
                     allow_slow_non_contiguous=True).then_inc(self.spread, 16)
        sp.wait_ge(self.spread, 48)

    def pick(self, pe, bank):
        pe.wait_ge(self.rel_in, 16)
        self.nc.tensor.matmul(self.k.ps[0:H, bank, :], self.rel[:], self.k.cst[0:NBK, C_OH:C_OH + STRIP],
                              start=True, stop=True).then_inc(self.picked, 1)

    def largest(self, dve, bank):
        dve.wait_ge(self.picked, 1)
        self.nc.vector.tensor_reduce(self.top[:], self.k.ps[0:H, bank, :], AX.X, ALU.max, negate=True).then_inc(self.top_ready, 1)

    def exps(self, act, bank):
        act.wait_ge(self.top_ready, 1)
        self.nc.scalar.activation(self.strip[:], self.k.ps[0:H, bank, :], ACT.Exp, bias=self.top[:]).then_inc(self.strip_ready, 1)


def biased_attention(nc, k, m, by_distance):
    a = Core()
    a.tag, a.causal = "ba_", False
    a.near, a.left, a.right = by_distance.near, by_distance.left, by_distance.right
    with ExitStack() as c0:
        loads = attention_inputs(nc, m, a, c0)
        normalise(nc, k, "n2", k.x, k.hT, lambda b: k.mod[:, 1, CA, b:b + 1], lambda b: k.mod[:, 1, SA, b:b + 1], loads)
        with ExitStack() as c:
            def sb(name, shape, dt=F32):
                return c.enter_context(nc.sbuf_tensor("ba_" + name, shape, dt))

            a.v = sb("v", [P, NT, H, VA])
            a.qk, a.o = k.qk_dram, k.o_dram
            project(nc, k, m, a)
            attend(nc, k, a)
        join_heads(nc, k, m, a, k.x, lambda wo: nc.vector.tensor_tensor(wo[:], wo[:], k.row[:, 1, :, :], ALU.mult))


def modulate(nc, k, tag, src, dst, row_scale, row_shift, loads):
    with ExitStack() as c:
        def sb(name, shape, dt=F32):
            return c.enter_context(nc.sbuf_tensor(tag + name, shape, dt))

        stats = sb("stats", [P, NT, 6])
        mean, var, rstd, dif, shift = (sb(n, [P, NT]) for n in ("mean", "var", "rstd", "dif", "shift"))
        counted, var_ready, sd_ready, chain, rstd_ready, dve_plain, act_plain, scaled = (
            nc.alloc_semaphore(tag + n) for n in ("counted", "var_r", "sd", "chain", "rstd", "dve_plain", "act_plain", "scaled"))
        with nc.Block() as block:
            block.sync(loads)

            @block.vector
            def _(dve):
                ch = Chain(dve, chain)
                statistics(nc, dve, ch, src, stats, mean, var, dif, counted, var_ready)
                scales(nc, dve, ch, var, mean, rstd, shift, sd_ready, rstd_ready)
                for b in range(B):
                    for t in range(b * TB, b * TB + TB // 2):
                        nc.vector.tensor_scalar(dst[:, t, :], src[:, t, :], col(mean, t), col(rstd, t),
                                                ALU.subtract, ALU.mult).then_inc(dve_plain, 1)
                    dve.wait_ge(dve_plain, (b + 1) * TB // 2)
                    dve.wait_ge(act_plain, (b + 1) * TB // 2)
                    d = dst[:, b * TB:(b + 1) * TB, :]
                    nc.vector.tensor_tensor(d, d, row_scale[:, b:b + 1, :].broadcast_to([P, TB, D]), ALU.mult).then_inc(scaled, 1)
                    dve.wait_ge(scaled, b + 1)
                    nc.vector.tensor_tensor(d, d, row_shift[:, b:b + 1, :].broadcast_to([P, TB, D]), ALU.add)

            @block.scalar
            def _(act):
                act.wait_ge(var_ready, 1)
                nc.scalar.activation(var[:], var[:], ACT.Sqrt).then_inc(sd_ready, 1)
                act.wait_ge(rstd_ready, 1)
                for b in range(B):
                    for t in range(b * TB + TB // 2, (b + 1) * TB):
                        nc.scalar.activation(dst[:, t, :], src[:, t, :], ACT.Identity, bias=col(shift, t),
                                             scale=col(rstd, t)).then_inc(act_plain, 1)


def route(nc, k, m, r):
    with ExitStack() as c:
        def sb(name, shape, dt=F32):
            return c.enter_context(nc.sbuf_tensor("ro_" + name, shape, dt))

        wr, trash, ids = r.wr, r.trash, r.ids
        stats = sb("stats", [P, NT, 6])
        mean, var, rstd, dif, shift = (sb(n, [P, NT]) for n in ("mean", "var", "rstd", "dif", "shift"))
        counted, var_ready, sd_ready, rstd_ready, dve_plain, act_plain = (
            nc.alloc_semaphore("ro_" + n) for n in ("counted", "var_r", "sd", "rstd", "dve_plain", "act_plain"))
        lg, ex, l2, c1, slot = (sb(n, [P, NT, E]) for n in ("lg", "ex", "l2", "c1", "slot"))
        pick = sb("pick", [P, 2, NT, E])
        pickb = sb("pickb", [P, 2, NT, E], BF16)
        tot = sb("tot", [P, 2, E, NT])
        inc = sb("inc", [P, 2, E, NT])
        keep1 = sb("keep1", [P, E, NT])
        col1, col2 = (sb(n, [P, NT]) for n in ("col1", "col2"))
        kept = sb("kept", [P, 2, NT])
        row = sb("row", [P, 2, NT])
        onesb = sb("onesb", [P, P], BF16)
        loaded = r.route_in
        logits, e_ready, chain, ch_ready, counts, turned, moved = (
            nc.alloc_semaphore("ro_" + n) for n in
            ("logits", "e_ready", "chain", "ch_ready", "counts", "turned", "moved"))
        ex_go, to_ready, ids_set = (nc.alloc_semaphore("ro_" + n) for n in ("ex_go", "to_ready", "ids_set"))

        def v(t):
            return t[:].unsqueeze(2).broadcast_to([P, NT, E])

        def const(at):
            return k.cst[:, at:at + E].unsqueeze(1).broadcast_to([P, NT, E])

        with nc.Block() as block:
            block.sync(r.loads)

            @block.tensor
            def _(pe):
                for t in range(NT):
                    if t >= 8 and t % 4 == 0:
                        pe.wait_ge(moved, t // 4 - 1)
                    pe.wait_ge((dve_plain, act_plain)[t % 2], t // 2 + 1)
                    ins = nc.tensor.transpose(k.ps[:, (t // 4) % 2, (t % 4) * P:(t % 4 + 1) * P], r.xt[:, 0, t, 0:D], k.cst[:, C_ID:C_ID + P])
                    if t % 4 == 3:
                        ins.then_inc(turned, 1)
                pe.wait_ge(loaded, 48)
                for t in range(NT):
                    if t % 4 == 0:
                        pe.wait_ge(moved, t // 4 + 1)
                    ins = nc.tensor.matmul(k.ps[:, 2, t * E:(t + 1) * E], k.hT[:, t * P:(t + 1) * P], wr[:], start=True, stop=True)
                ins.then_inc(logits, 1)
                for i in range(2):
                    pe.wait_ge(ch_ready, i + 1)
                    one = pickb[:, i, :, :].rearrange("p t e -> p (t e)")
                    nc.tensor.matmul(k.ps[:, 3 + i, :], k.cstb[:, C_TRI:C_TRI + P], one, start=True, stop=True)
                    ins = nc.tensor.matmul(k.ps[:, 5 + i, :], onesb[:], one, start=True, stop=True)
                    ins.then_inc(counts, 1)

            @block.scalar
            def _(act):
                act.wait_ge(var_ready, 1)
                nc.scalar.activation(var[:], var[:], ACT.Sqrt).then_inc(sd_ready, 1)
                act.wait_ge(rstd_ready, 1)
                for i in range(NCH + 1):
                    if i < NCH:
                        for t in range(4 * i + 1, 4 * i + 4, 2):
                            nc.scalar.activation(r.xt[:, 0, t, 0:D], r.hidden[:, t, :], ACT.Identity, bias=col(shift, t),
                                                 scale=col(rstd, t)).then_inc(act_plain, 1)
                    if i:
                        act.wait_ge(turned, i)
                        nc.scalar.activation(k.hT[:, (i - 1) * CH:i * CH], k.ps[:, (i - 1) % 2, :], ACT.Identity,
                                             bias=r.ln2[:, 1:2], scale=r.ln2[:, 0:1]).then_inc(moved, 1)
                act.wait_ge(ex_go, 1)
                nc.scalar.activation(ex[:], lg[:], ACT.Exp).then_inc(e_ready, 1)
                act.wait_ge(dve_plain, NT // 2)
                act.wait_ge(act_plain, NT // 2)
                for b in range(B):
                    ts = slice(b * TB, (b + 1) * TB)
                    nc.scalar.copy(r.xt[:, 1, ts, 0:D], r.xt[:, 0, ts, 0:D])

            @block.gpsimd
            def _(pool):
                pool.wait_ge(loaded, 48)
                for i in range(2):
                    nc.gpsimd.tensor_copy(r.xt[:, i, :, D:D + 1].bitcast(I32), ids[:, i, :].unsqueeze(2)).then_inc(ids_set, 1)
                pool.wait_ge(ids_set, 2)
                pool.wait_ge(to_ready, 1)
                pool.wait_ge(dve_plain, NT // 2)
                pool.wait_ge(act_plain, NT // 2)
                send_copies(nc, k, r, 0)

            @block.vector
            def _(dve):
                ch = Chain(dve, chain)
                L_, vec = ch.link, nc.vector
                statistics(nc, dve, ch, r.hidden, stats, mean, var, dif, counted, var_ready)
                scales(nc, dve, ch, var, mean, rstd, shift, sd_ready, rstd_ready)
                for t in range(0, NT, 2):
                    vec.tensor_scalar(r.xt[:, 0, t, 0:D], r.hidden[:, t, :], col(mean, t), col(rstd, t),
                                      ALU.subtract, ALU.mult).then_inc(dve_plain, 1)
                L_(vec.memset(onesb[:], 1.0))
                L_(vec.memset(keep1[:], 1.0))
                L_(vec.memset(keep1[:, :, 0:1], 0.0))
                dve.wait_ge(loaded, 48)
                dve.wait_ge(logits, 1)
                raw = k.ps[:, 2, :].rearrange("p (t e) -> p t e", e=E)
                L_(vec.tensor_reduce(col1[:], raw, AX.X, ALU.max))
                vec.tensor_tensor(lg[:], raw, v(col1), ALU.subtract).then_inc(ex_go, 1)
                dve.wait_ge(e_ready, 1)
                L_(vec.tensor_reduce(col1[:], ex[:], AX.X, ALU.add))
                L_(vec.reciprocal(col1[:], col1[:]))
                L_(vec.tensor_tensor(ex[:], ex[:], v(col1), ALU.mult))

                def first_of(values, i):
                    L_(vec.tensor_reduce(col1[:], values, AX.X, ALU.max))
                    L_(vec.tensor_tensor(c1[:], values, v(col1), ALU.is_equal))
                    L_(vec.tensor_tensor(c1[:], c1[:], const(C_FIRST), ALU.mult))
                    L_(vec.tensor_reduce(col1[:], c1[:], AX.X, ALU.max))
                    L_(vec.tensor_tensor(pick[:, i, :, :], c1[:], v(col1), ALU.is_equal))

                first_of(ex[:], 0)
                vec.tensor_copy(pickb[:, 0, :, :], pick[:, 0, :, :]).then_inc(ch_ready, 1)
                L_(vec.scalar_tensor_tensor(l2[:].rearrange("p t e -> p (t e)"), pick[:, 0, :, :].rearrange("p t e -> p (t e)"),
                                            NEG, lg[:].rearrange("p t e -> p (t e)"), ALU.mult, ALU.add))
                first_of(l2[:], 1)
                vec.tensor_copy(pickb[:, 1, :, :], pick[:, 1, :, :]).then_inc(ch_ready, 1)
                for i in range(2):
                    dve.wait_ge(counts, i + 1)
                    L_(vec.tensor_copy(tot[:, i, :, :], k.ps[:, 5 + i, :].rearrange("p (t e) -> p e t", e=E)))
                    L_(vec.tensor_tensor_scan(inc[:, i, :, :].rearrange("p e t -> p (e t)"), keep1[:].rearrange("p e t -> p (e t)"),
                                              tot[:, i, :, :].rearrange("p e t -> p (e t)"), 0.0, ALU.mult, ALU.add))
                    L_(vec.tensor_tensor(c1[:], inc[:, i, :, :].rearrange("p e t -> p t e"), tot[:, i, :, :].rearrange("p e t -> p t e"), ALU.subtract))
                    L_(vec.tensor_tensor(c1[:], c1[:], k.ps[:, 3 + i, :].rearrange("p (t e) -> p t e", e=E), ALU.add))
                    if i:
                        L_(vec.tensor_tensor(c1[:], c1[:], inc[:, 0, :, NT - 1:NT].rearrange("p e a -> p a e").broadcast_to([P, NT, E]), ALU.add))
                    L_(vec.tensor_scalar(c1[:], c1[:], -1.0, None, ALU.add))
                    L_(vec.tensor_scalar(l2[:], c1[:], float(CAP), None, ALU.is_lt))
                    L_(vec.tensor_tensor(l2[:], l2[:], pick[:, i, :, :], ALU.mult))
                    L_(vec.tensor_tensor(slot[:], c1[:], const(C_SLOT), ALU.add))
                    L_(vec.tensor_tensor(slot[:], slot[:], l2[:], ALU.mult))
                    L_(vec.tensor_reduce(row[:, i, :], slot[:], AX.X, ALU.add))
                    L_(vec.tensor_reduce(kept[:, i, :], l2[:], AX.X, ALU.add))
                    L_(vec.tensor_scalar(kept[:, i, :], kept[:, i, :], -1.0, 1.0, ALU.mult, ALU.add))
                    L_(vec.tensor_tensor(kept[:, i, :], kept[:, i, :], trash[:, i, :], ALU.mult))
                    L_(vec.tensor_tensor(row[:, i, :], row[:, i, :], kept[:, i, :], ALU.add))
                    vec.tensor_copy(r.to[:, i, :], row[:, i, :]).then_inc(to_ready, 1)
                    L_(vec.tensor_tensor(slot[:], ex[:], l2[:], ALU.mult))
                    L_(vec.tensor_reduce(r.g[:, i, :], slot[:], AX.X, ALU.add))
                L_(vec.tensor_tensor(col1[:], r.g[:, 0, :], r.g[:, 1, :], ALU.add))
                L_(vec.tensor_scalar(col1[:], col1[:], 1.1920929e-07, None, ALU.max))
                L_(vec.reciprocal(col2[:], col1[:]))
                L_(vec.tensor_scalar(col2[:], col2[:], KEEP, None, ALU.mult))
                vec.tensor_tensor(r.g[:], r.g[:], col2[:].unsqueeze(1).broadcast_to([P, 2, NT]), ALU.mult)


def send_copies(nc, k, r, i):
    for t in range(NT):
        nc.gpsimd.indirect_dma_start(k.rows_in, bass.IndirectOffsetOnAxis(ap=r.to[:, i, t:t + 1], axis=0),
                                     r.xt[:, i, t, :], None).then_inc(r.sent, 16)


def load_expert(sp, m, r, e, s):
    sp.dma_start(r.fc1[:, s, :], m["fc1_w"][e]).then_inc(r.w_in[s], 16)
    sp.dma_start(r.fc2[:, s, :, :], m["fc2_w"][e]).then_inc(r.w_in[s], 16)


def experts(nc, k, m, r):
    QT, FB = CAP // P, FF // P
    with ExitStack() as c:
        def sb(name, shape, dt=F32):
            return c.enter_context(nc.sbuf_tensor("ex_" + name, shape, dt))

        fc1, fc2, b1, b2 = r.fc1, r.fc2, r.b1, r.b2
        xi = sb("xi", [P, 2, QT, D + 1])
        to = sb("to", [P, E, QT, 1], I32)
        xT = sb("xT", [P, 2, CAP])
        hh = sb("hh", [P, 2, FB, CAP])
        eo = sb("eo", [P, 2, QT, D])
        back = k.qop[:].rearrange("p g a n -> p (g a n)").bitcast(F32).rearrange("p (i n j d) -> p i n j d", i=2, n=4, j=4)
        consts_in, w_in = r.consts_in, r.w_in
        turned, xT_ready, up, act_done, down, eo_ready = (
            nc.alloc_semaphore("ex_" + n) for n in
            ("turned", "xT_ready", "up", "act_done", "down", "eo_ready"))
        x_in = [nc.alloc_semaphore(f"ex_x_in{s}") for s in range(2)]
        eo_out = [nc.alloc_semaphore(f"ex_eo_out{s}") for s in range(2)]
        got = [nc.alloc_semaphore(f"ex_got{s}") for s in range(4)]
        first, both, gated, summed, x_plain, ids_kept = (
            nc.alloc_semaphore("ex_" + n) for n in ("first", "both", "gated", "summed", "x_plain", "ids_kept"))
        chain = nc.alloc_semaphore("ex_chain")

        with nc.Block() as block:
            @block.gpsimd
            def _(pool):
                send_copies(nc, k, r, 1)
                for e in range(E):
                    pool.wait_ge(eo_ready, e + 1)
                    for q in range(QT):
                        nc.gpsimd.indirect_dma_start(k.rows_out, bass.IndirectOffsetOnAxis(ap=to[:, e, q, :], axis=0),
                                                     eo[:, e % 2, q, :], None).then_inc(eo_out[e % 2], 16)
                for n in range(NCH):
                    pool.wait_ge(both, 4 * (n + 1))
                    y = back[:, 1, n % 4, :, :]
                    b = n * CH // L
                    nc.gpsimd.tensor_tensor(y, y, k.row[:, 2, b:b + 1, :].broadcast_to([P, 4, D]), ALU.mult).then_inc(gated, 1)

            @block.sync
            def _(sp):
                def rows(e, s):
                    sp.dma_start(xi[:, s, :, :], k.rows_in[bass.ds(e * CAP, CAP), :].rearrange("(q p) d -> p q d", p=P)).then_inc(x_in[s], 16)

                sp.wait_ge(r.sent, NT * 2 * 16)
                rows(0, 0)
                rows(1, 1)

                def step(e, s):
                    sp.wait_ge(down, e + 1)
                    load_expert(sp, m, r, e + 2, s)
                    sp.wait_ge(xT_ready, e + 1)
                    rows(e + 2, s)

                with sp.Fori(0, (E - 2) // 2) as i:
                    step(2 * i, 0)
                    step(2 * i + 1, 1)
                for s in range(2):
                    sp.wait_ge(eo_out[s], E // 2 * QT * 16)
                for n in range(NCH):
                    if n >= 4:
                        sp.wait_ge(summed, n - 3)
                    for i in range(2):
                        sp.dma_start(back[:, i, n % 4, :, :], k.rows_out[i * TOK + n * CH:i * TOK + (n + 1) * CH, :]
                                     .rearrange("(j p) d -> p j d", p=P)).then_inc(got[n % 4], 16)

            @block.tensor
            def _(pe):
                def turn(e, s, n):
                    pe.wait_ge(x_in[s], 16 * n)
                    if not (isinstance(e, int) and e < 2):
                        pe.wait_ge(xT_ready, e - 1)
                    for q in range(QT):
                        ins = nc.tensor.transpose(k.ps[:, s, q * P:(q + 1) * P], xi[:, s, q, 0:D], k.cst[:, C_ID:C_ID + P])
                    ins.then_inc(turned, 1)

                def upper(e, s, n):
                    pe.wait_ge(w_in[s], 32 * n)
                    pe.wait_ge(xT_ready, e + 1)
                    for f in range(FB):
                        if not (isinstance(e, int) and e == 0):
                            pe.wait_ge(act_done, e * FB + f - (FB - 1))
                        nc.tensor.matmul(k.ps[:, 2 + f, :], fc1[:, s, f * P:(f + 1) * P], xT[:, s, :], start=True, stop=True).then_inc(up, 1)

                def lower(e, s):
                    pe.wait_ge(act_done, (e + 1) * FB)
                    if not (isinstance(e, int) and e < 2):
                        pe.wait_ge(eo_ready, e - 1)
                    for q in range(QT):
                        for f in range(FB):
                            ins = nc.tensor.matmul(k.ps[:, 6 + s, q * P:(q + 1) * P], hh[:, s, f, q * P:(q + 1) * P], fc2[:, s, f, :],
                                                   start=(f == 0), stop=(f == FB - 1))
                    ins.then_inc(down, 1)

                turn(0, 0, 1)
                upper(0, 0, 1)
                turn(1, 1, 1)
                lower(0, 0)
                upper(1, 1, 1)
                with pe.Fori(1, E // 2) as i:
                    turn(2 * i, 0, i + 1)
                    lower(2 * i - 1, 1)
                    upper(2 * i, 0, i + 1)
                    turn(2 * i + 1, 1, i + 1)
                    lower(2 * i, 0)
                    upper(2 * i + 1, 1, i + 1)
                lower(E - 1, 1)

            @block.scalar
            def _(act):
                act.wait_ge(consts_in, 32)

                def gelus(e, s, first=False):
                    for f in range(FB):
                        act.wait_ge(up, e * FB + f + 1)
                        if f == 0 and not first:
                            act.wait_ge(down, e - 1)
                        bias = b1[:, e, f:f + 1] if isinstance(e, int) else b1[:, bass.ds(e, 1), f]
                        nc.scalar.activation(hh[:, s, f, :], k.ps[:, 2 + f, :], ACT.Gelu, bias=bias).then_inc(act_done, 1)

                gelus(0, 0, True)
                gelus(1, 1, True)
                with act.Fori(1, E // 2) as i:
                    gelus(2 * i, 0)
                    gelus(2 * i + 1, 1)
                for t in range(NT):
                    n = t // 4
                    if t % 4 == 0:
                        act.wait_ge(got[n % 4], (n // 4 + 1) * 2 * 16)
                    y1 = back[:, 0, n % 4, t % 4, :]
                    nc.scalar.activation(y1, y1, ACT.Copy, scale=r.g[:, 0, t:t + 1]).then_inc(first, 1)

            @block.vector
            def _(dve):
                dve.wait_ge(consts_in, 32)

                def turned_in(e, s, n):
                    dve.wait_ge(turned, e + 1)
                    if not (isinstance(e, int) and e < 2):
                        dve.wait_ge(up, (e - 1) * FB)
                    dve.wait_ge(x_in[s], 16 * n)
                    nc.vector.tensor_copy(to[:, bass.ds(e, 1), :, :].rearrange("p a q b -> p (a q) b"), xi[:, s, :, D:D + 1].bitcast(I32)).then_inc(ids_kept, 1)
                    dve.wait_ge(ids_kept, e + 1)
                    nc.vector.tensor_scalar(xT[:, s, :], k.ps[:, s, :], r.ln2[:, 0:1], r.ln2[:, 1:2], ALU.mult, ALU.add).then_inc(xT_ready, 1)

                def out(e, s, n):
                    dve.wait_ge(down, e + 1)
                    if not (isinstance(n, int) and n == 0):
                        dve.wait_ge(eo_out[s], QT * 16 * n)
                    row = b2[:, bass.ds(e, 1), :].broadcast_to([P, QT, D])
                    nc.vector.tensor_tensor(eo[:, s, :, :], k.ps[:, 6 + s, :].rearrange("p (q d) -> p q d", d=D), row, ALU.add).then_inc(eo_ready, 1)

                def pair(i):
                    turned_in(2 * i, 0, i + 1)
                    out(2 * i - 1, 1, i - 1)
                    turned_in(2 * i + 1, 1, i + 1)
                    out(2 * i, 0, i)

                def add(n):
                    xs = k.x[:, 4 * n:4 * n + 4, :]
                    dve.wait_ge(gated, n + 1)
                    dve.wait_ge(x_plain, B)
                    nc.vector.tensor_tensor(xs, xs, back[:, 1, n % 4, :, :], ALU.add).then_inc(summed, 1)

                turned_in(0, 0, 1)
                turned_in(1, 1, 1)
                out(0, 0, 0)
                pair(1)
                with dve.Fori(2, E // 2) as i:
                    pair(i)
                out(E - 1, 1, E // 2 - 1)
                for b in range(B):
                    h = r.hidden[:, b * TB:(b + 1) * TB, :]
                    xs = k.x[:, b * TB:(b + 1) * TB, :]
                    nc.vector.tensor_tensor(h, h, k.row[:, 2, b:b + 1, :].broadcast_to([P, TB, D]), ALU.mult).then_inc(chain, 1)
                    dve.wait_ge(chain, b + 1)
                    nc.vector.tensor_tensor(xs, xs, h, ALU.add).then_inc(x_plain, 1)
                for t in range(NT):
                    dve.wait_ge(first, t + 1)
                    y1, y2 = back[:, 0, t // 4 % 4, t % 4, :], back[:, 1, t // 4 % 4, t % 4, :]
                    nc.vector.scalar_tensor_tensor(y2, y2, r.g[:, 1, t:t + 1], y1, ALU.mult, ALU.add).then_inc(both, 1)
                    if t % 4 == 3 and t >= 7:
                        add(t // 4 - 1)
                add(NCH - 1)


def causal_sublayer(nc, k, m):
    a = Core()
    a.tag, a.causal = "ca_", True
    r = Core()
    with ExitStack() as c:
        def sb(name, shape, dt=F32):
            return c.enter_context(nc.sbuf_tensor("cs_" + name, shape, dt))

        h = sb("h", [P, NT, D])
        ln1 = sb("ln1", [P, 2])
        r.ln2 = sb("ln2", [P, 2])
        a.ob = sb("ob", [P, 1, D])
        ln_in = nc.alloc_semaphore("cs_ln_in")
        attention_loads = attention_inputs(nc, m, a, c)

        def norm_loads(sp):
            sp.dma_start(ln1[:], m["ln1"]).then_inc(ln_in, 16)
            sp.dma_start(r.ln2[:], m["ln2"]).then_inc(ln_in, 16)

        modulate(nc, k, "m3", k.x, h, k.row[:, 3], k.row[:, 4], norm_loads)
        with nc.Block() as block:
            @block.sync
            def _(sp):
                sp.wait_ge(ln_in, 32)
        normalise(nc, k, "n4", h, k.hT, lambda b: ln1[:, 0:1], lambda b: ln1[:, 1:2], attention_loads)
        with ExitStack() as c2:
            a.v = c2.enter_context(nc.sbuf_tensor("ca_v", [P, NT, H, VA], F32))
            a.qk, a.o = k.qk_dram, k.o_dram
            with nc.cleanup_on_exit():
                project(nc, k, m, a)
                attend(nc, k, a)
        join_heads(nc, k, m, a, h, lambda wo: nc.vector.tensor_tensor(h[:], h[:], a.ob[:].broadcast_to([P, NT, D]), ALU.add))
        r.hidden = h
        r.xt = sb("xt", [P, 2, NT, D + 1])
        r.to = sb("to", [P, 2, NT], I32)
        r.sent = nc.alloc_semaphore("cs_sent")
        r.g = sb("g", [P, 2, NT])
        r.wr, r.trash, r.ids = sb("wr", [P, E]), sb("trash", [P, 2, NT]), sb("ids", [P, 2, NT], I32)
        r.fc1, r.fc2 = sb("fc1", [P, 2, FF]), sb("fc2", [P, 2, FF // P, D])
        r.b1, r.b2 = sb("b1", [P, E, FF // P]), sb("b2", [P, E, D])
        r.route_in, r.consts_in = nc.alloc_semaphore("cs_route_in"), nc.alloc_semaphore("cs_consts_in")
        r.w_in = [nc.alloc_semaphore(f"cs_w_in{s}") for s in range(2)]

        def route_loads(sp):
            sp.dma_start(r.wr[:], m["router_w"]).then_inc(r.route_in, 16)
            sp.dma_start(r.trash[:], m["trash_rows"]).then_inc(r.route_in, 16)
            sp.dma_start(r.ids[:], m["result_rows"]).then_inc(r.route_in, 16)
            sp.dma_start(r.b1[:], m["fc1_b"]).then_inc(r.consts_in, 16)
            sp.dma_start(r.b2[:], m["fc2_b"].broadcast_to([P, E, D])).then_inc(r.consts_in, 16)
            for s in range(2):
                load_expert(sp, m, r, s, s)

        r.loads = route_loads
        route(nc, k, m, r)
        experts(nc, k, m, r)



def store(nc, k, m):
    stored = nc.alloc_semaphore("stored")
    with nc.Block() as block:
        @block.sync
        def _(sp):
            sp.dma_start(m["out"].rearrange("b (t p) d -> p (b t) d", p=P), k.x[:]).then_inc(stored, 16)
            sp.wait_ge(stored, 16)


def program(nc, m, stop):
    with ExitStack() as c:
        def sb(name, shape, dt=F32):
            return c.enter_context(nc.sbuf_tensor(name, shape, dt))

        k = Core()
        k.ps = c.enter_context(nc.psum_tensor("ps", [P, 8, CH], F32))
        k.x = sb("x_tok", [P, NT, D])
        k.hT = sb("hT", [P, TOK])
        k.cst = sb("cst", [P, C_W])
        k.cstb = sb("cstb", [P, C_FIRST], BF16)
        k.ones = sb("ones", [P, P])
        k.mod = sb("mod", [P, 2, 6, B])
        k.qop = sb("qop", [P, NG, 2, L], BF16)
        k.kop = sb("kop", [P, NG, HG, L], BF16)
        k.row0 = sb("row0", [1, L], BF16)
        k.row_of = [(0, GA), (1, GA), (1, GB), (1, CB), (1, SB), (0, GB)]
        k.row = sb("row", [P, len(k.row_of), B, D])
        k.qk_dram = nc.dram_tensor("qk_parts", (2, H, 3, HD, TOK), BF16).ap()
        k.o_dram = nc.dram_tensor("head_sums", (B, H, VA, L), F32).ap()
        k.strip_dram = nc.dram_tensor("bias_strip", (H, STRIP), F32).ap()
        k.rows_in = nc.dram_tensor("expert_rows_in", (E * CAP + 2 * TOK, D + 1), F32).ap()
        k.rows_out = nc.dram_tensor("expert_rows_out", (2 * TOK + E * CAP, D), F32).ap()
        load_and_modulate(nc, k, m)
        scan_sublayer(nc, k, m)
        with ExitStack() as c2:
            by_distance = BiasByDistance(nc, k, c2)
            first_mixture(nc, k, m, by_distance)
            with nc.cleanup_on_exit():
                biased_attention(nc, k, m, by_distance)
        with nc.cleanup_on_exit():
            causal_sublayer(nc, k, m)
        store(nc, k, m)


def constants():
    import numpy as np

    a = np.zeros((P, C_W), np.float32)
    i = np.arange(P)
    a[i, C_ID + i] = 1.0
    a[i, C_FLIP + P - 1 - i] = 1.0
    a[:, C_TRI:C_TRI + P] = i[:, None] <= i[None, :]
    a[:, C_MA:C_MA + P] = np.where(i[None, :] > i[:, None], NEG, 0.0)
    a[:, C_MB:C_MB + P] = np.where(i[None, :] < i[:, None], NEG, 0.0)
    a[:, C_FIRST:C_FIRST + E] = E - np.arange(E)
    a[:, C_SLOT:C_SLOT + E] = CAP * np.arange(E)
    edges = np.array([1, 2, 3, 4, 5, 6, 7, 11, 15, 21, 30, 44, 62, 90, 128])
    rel = 255 - np.arange(STRIP)
    bucket = (np.abs(rel)[:, None] >= edges[None, :]).sum(1) + 16 * (rel > 0)
    a[bucket, C_OH + np.arange(STRIP)] = 1.0
    return a


def layouts(i):
    import numpy as np

    def c(a):
        return np.ascontiguousarray(a)

    i = {n: np.asarray(a) for n, a in i.items()}
    d = {"consts": constants(), "x": c(i["L0_attn_x"]), "c0T": c(i["L0_c"].T), "c1T": c(i["L1_c"].T),
         "L0_wmod": c(i["L0_wmod"]), "L1_wmod": c(i["L1_wmod"])}
    wx = i["L0_attn_Wxproj"]
    wp = np.zeros((D, 3, SP), np.float32)
    wp[:, 0, :NST] = wx[RANK:RANK + NST].T
    wp[:, 1, :NST] = wx[RANK + NST:].T
    wp[:, 2, :NST] = i["L0_attn_Wxs"].T
    d["ssm_wp"], d["ssm_wx"] = wp, c(wx[:RANK])
    d["ssm_wdt"] = c(np.repeat(i["L0_attn_Wdt"].T, SP, axis=1))
    col = np.zeros((P, 3), np.float32)
    wout = np.zeros((P, B, D), np.float32)
    for b in range(B):
        col[SP * b:SP * b + NST, 0] = i["L0_attn_A_log"][0]
        wout[SP * b:SP * b + NST, b] = i["L0_attn_Wout"].T
    col[:, 1] = i["L0_attn_bdt"][0]
    col[:, 2] = i["L0_attn_Dp"]
    d["ssm_col"], d["ssm_wout"] = col, wout
    d["gate_w"] = c(i["L0_ffn_Wg"].T)
    d["ffn_w1"] = c(i["L0_ffn_W1"].transpose(2, 0, 1))
    d["ffn_w3"] = c(i["L0_ffn_W3"].transpose(2, 0, 1))
    d["ffn_w2"] = c(i["L0_ffn_W2"].transpose(2, 0, 1))
    d["ffn_bias"] = c(np.stack([i["L0_ffn_b1"].T, i["L0_ffn_b3"].T], axis=1))
    d["ffn_b2"] = c(i["L0_ffn_b2"])
    d["ba_w"] = c(np.stack([i["L1_attn_W" + n].T for n in "qkv"], axis=1))
    d["ba_bias"] = np.zeros((P, 2), np.float32)
    d["ba_vb"] = np.zeros((1, D), np.float32)
    d["ba_wo"] = c(i["L1_attn_Wo"].T)
    d["rel_emb"] = c(i["L1_attn_rel_emb"])
    d["ln1"] = c(np.stack([i["L1_ffn_ln1_w"], i["L1_ffn_ln1_b"]], axis=1))
    d["ln2"] = c(np.stack([i["L1_ffn_ln2_w"], i["L1_ffn_ln2_b"]], axis=1))
    d["ca_w"] = c(np.stack([i["L1_ffn_" + n + "_w"] for n in "qkv"], axis=1))
    d["ca_bias"] = c(np.stack([i["L1_ffn_q_b"], i["L1_ffn_k_b"]], axis=1))
    d["ca_vb"] = c(i["L1_ffn_v_b"]).reshape(1, D)
    d["ca_wo"] = c(i["L1_ffn_o_w"])
    d["ca_ob"] = c(i["L1_ffn_o_b"]).reshape(1, D)
    d["router_w"] = c(i["L1_ffn_router_w"])
    d["trash_rows"] = (E * CAP + np.arange(2)[None, :, None] * TOK + np.arange(NT)[None, None, :] * P
                       + np.arange(P)[:, None, None]).astype(np.float32)
    d["result_rows"] = (np.arange(2)[None, :, None] * TOK + np.arange(NT)[None, None, :] * P
                        + np.arange(P)[:, None, None]).astype(np.int32)
    d["unused_rows"] = (2 * TOK + np.arange(E * CAP)).reshape(P, E * CAP // P).astype(np.int32)
    d["fc1_w"] = c(i["L1_ffn_fc1_w"])
    d["fc2_w"] = c(i["L1_ffn_fc2_w"].reshape(E, FF // P, P, D).transpose(0, 2, 1, 3))
    d["fc1_b"] = c(i["L1_ffn_fc1_b"].reshape(E, FF // P, P).transpose(2, 0, 1))
    d["fc2_b"] = c(i["L1_ffn_fc2_b"]).reshape(1, E, D)
    return d


def kernel(**inputs):
    import concourse.bacc as _bacc
    from concourse import mybir as _mybir
    from concourse.bass_utils import run_bass_kernel_spmd as _run

    nc = _bacc.Bacc("TRN2", target_bir_lowering=False, num_devices=1)
    arrays = layouts(inputs)
    m = {n: nc.dram_tensor("in_" + n, a.shape, _mybir.dt.from_np(a.dtype), kind="ExternalInput").ap()
         for n, a in arrays.items()}
    m["out"] = nc.dram_tensor("out_x", (B, L, D), F32, kind="ExternalOutput").ap()
    program(nc, m, None)
    r = _run(nc, [{"in_" + n: a for n, a in arrays.items()}], core_ids=[0])
    return r.results[0]["out_x"]
```

```python
from contextlib import ExitStack

import concourse.bass as bass
from concourse import mybir

F32 = mybir.dt.float32
BF16 = mybir.dt.bfloat16
I32 = mybir.dt.int32
ALU = mybir.AluOpType
ACT = mybir.ActivationFunctionType
AX = mybir.AxisListType

P = 128
B, L, D = 4, 1024, 128
TOK = B * L
NT = TOK // P
TB = L // P
CH = 512
NCH = TOK // CH
EPS = 1e-5

NST = 16
RANK = 64
SP = 32
E = 16
H, HD = 16, 8
HG = 4
NG = H // HG
VA = HD + 1
NBK = 32
STRIP = 512
NEAR = 3 * P
FF = 512
CAP = 2 * (TOK // E)
KEEP = 1.0 - 0.2
NEG = -1.0e30

C_ID, C_TRI, C_MA, C_MB = 0, 128, 256, 384
C_FIRST, C_SLOT, C_OH = 512, 528, 544
C_FLIP = C_OH + STRIP
C_W = C_FLIP + P

SA, CA, GA, SB, CB, GB = range(6)


class Chain:

    def __init__(self, eng, sem):
        self.eng, self.sem, self.at, self.base = eng, sem, 0, 0

    def link(self, ins):
        ins.then_inc(self.sem, 1)
        self.at += 1
        self.eng.wait_ge(self.sem, self.base + self.at)


def col(tensor, t):
    return tensor[:, bass.ds(t, 1)]


class Core:
    pass


def load_and_modulate(nc, k, m):
    with ExitStack() as c:
        cT = c.enter_context(nc.sbuf_tensor("cT", [P, 2, B], F32))
        cS = c.enter_context(nc.sbuf_tensor("cS", [P, 2, B], F32))
        wm = c.enter_context(nc.sbuf_tensor("wm", [P, 2, 6 * D], F32))
        diag = c.enter_context(nc.sbuf_tensor("diag", [P, len(k.row_of), B, D], F32))
        t0 = c.enter_context(nc.sbuf_tensor("modt0", [P, 2, 2, B], F32))
        t1 = c.enter_context(nc.sbuf_tensor("modt1", [P, 2, 2, B], F32))
        t2 = c.enter_context(nc.sbuf_tensor("modt2", [P, 2, 2, B], F32))
        loaded = nc.alloc_semaphore("loaded")
        xloaded = nc.alloc_semaphore("xloaded")
        silu_done = nc.alloc_semaphore("silu_done")
        mod_ready = nc.alloc_semaphore("mod_ready")
        ones_ready = nc.alloc_semaphore("ones_ready")
        chain = nc.alloc_semaphore("mod_chain")
        diag_ready = nc.alloc_semaphore("diag_ready")
        rows_ready = nc.alloc_semaphore("rows_ready")
        rows_kept = nc.alloc_semaphore("rows_kept")
        pm = k.ps[:, 7, 0:2 * 6 * B].rearrange("p (l r b) -> p l r b", l=2, r=6)
        with nc.Block() as block:
            @block.sync
            def _(sp):
                sp.dma_start(cT[:, 0, :], m["c0T"]).then_inc(loaded, 16)
                sp.dma_start(cT[:, 1, :], m["c1T"]).then_inc(loaded, 16)
                sp.dma_start(k.cst[:], m["consts"]).then_inc(loaded, 16)
                sp.dma_start(wm[:, 0, :], m["L0_wmod"]).then_inc(loaded, 16)
                sp.dma_start(wm[:, 1, :], m["L1_wmod"]).then_inc(loaded, 16)
                sp.dma_start(k.x[:], m["x"].rearrange("b (t p) d -> p (b t) d", p=P)).then_inc(xloaded, 16)
                sp.wait_ge(xloaded, 16)

            @block.scalar
            def _(act):
                act.wait_ge(loaded, 5 * 16)
                nc.scalar.activation(cS[:], cT[:], ACT.Silu).then_inc(silu_done, 1)
                for i in range(len(k.row_of)):
                    act.wait_ge(rows_ready, i + 1)
                    nc.scalar.copy(k.row[:, i, :, :].rearrange("p b d -> p (b d)"), k.ps[:, i, :]).then_inc(rows_kept, 1)

            @block.tensor
            def _(pe):
                pe.wait_ge(silu_done, 1)
                for l in range(2):
                    for r in range(6):
                        ins = nc.tensor.matmul(pm[:, l, r, :], wm[:, l, r * D:(r + 1) * D], cS[:, l, :],
                                               start=True, stop=True)
                ins.then_inc(mod_ready, 1)
                pe.wait_ge(ones_ready, 1)
                for i in range(len(k.row_of)):
                    pe.wait_ge(diag_ready, 4 * (i + 1))
                    nc.tensor.matmul(k.ps[:, i, :], k.ones[:], diag[:, i, :, :].rearrange("p b d -> p (b d)"),
                                     start=True, stop=True).then_inc(rows_ready, 1)

            @block.vector
            def _(dve):
                ch = Chain(dve, chain)
                nc.vector.memset(k.ones[:], 1.0).then_inc(ones_ready, 1)
                dve.wait_ge(mod_ready, 1)
                ch.link(nc.vector.tensor_copy(k.mod[:], pm))
                ch.link(nc.vector.tensor_scalar(k.mod[:, :, CA::3, :], k.mod[:, :, CA::3, :], 1.0, None, ALU.add))
                g = k.mod[:, :, GA::3, :]
                ch.link(nc.vector.tensor_scalar(t0[:], g, 0.0, None, ALU.is_ge))
                ch.link(nc.vector.tensor_scalar(t1[:], g, 0.25, None, ALU.max))
                ch.link(nc.vector.tensor_tensor(t1[:], t1[:], t0[:], ALU.mult))
                ch.link(nc.vector.tensor_scalar(t0[:], g, 0.0, None, ALU.is_lt))
                ch.link(nc.vector.tensor_scalar(t2[:], g, -0.25, None, ALU.min))
                ch.link(nc.vector.tensor_tensor(t2[:], t2[:], t0[:], ALU.mult))
                ch.link(nc.vector.tensor_tensor(g, t1[:], t2[:], ALU.add))
                for i, (l, r) in enumerate(k.row_of):
                    for b in range(B):
                        nc.vector.tensor_scalar(diag[:, i, b, :], k.cst[:, C_ID:C_ID + D], k.mod[:, l, r, b:b + 1],
                                                None, ALU.mult).then_inc(diag_ready, 1)
                nc.vector.tensor_copy(k.cstb[:], k.cst[:, 0:C_FIRST])


def measure(nc, k, src, tiles):
    for t in tiles:
        ins = nc.vector.bn_stats(k.stats[:, t, :], src[:, t, :])
    return ins


def combine(nc, k, ch, mean, var, dif, var_ready):
    stats = k.stats
    me, mo, qe, qo = (stats[:, :, j] for j in (1, 4, 2, 5))
    ch.link(nc.vector.tensor_tensor(mean[:], me, mo, ALU.add))
    ch.link(nc.vector.tensor_tensor(dif[:], me, mo, ALU.subtract))
    ch.link(nc.vector.tensor_tensor(var[:], qe, qo, ALU.add))
    ch.link(nc.vector.tensor_scalar(mean[:], mean[:], 0.5, None, ALU.mult))
    ch.link(nc.vector.tensor_tensor(dif[:], dif[:], dif[:], ALU.mult))
    ch.link(nc.vector.tensor_scalar(dif[:], dif[:], 0.25, EPS, ALU.mult, ALU.add))
    nc.vector.scalar_tensor_tensor(var[:], var[:], 1.0 / D, dif[:], ALU.mult, ALU.add).then_inc(var_ready, 1)


def scales(nc, dve, ch, var, mean, rstd, shift, sd_ready, rstd_ready):
    dve.wait_ge(sd_ready, 1)
    ch.link(nc.vector.reciprocal(rstd[:], var[:]))
    nc.vector.scalar_tensor_tensor(shift[:], mean[:], -1.0, rstd[:], ALU.mult, ALU.mult).then_inc(rstd_ready, 1)


def normalise(nc, k, tag, src, dst, scale_of, shift_of, loads, measured=0):
    QT = CH // P
    SLOTS = 4
    with ExitStack() as c:
        def sb(name, shape, dt=F32):
            return c.enter_context(nc.sbuf_tensor(tag + name, shape, dt))

        mean, var, rstd, dif, shift = (sb(n, [P, NT]) for n in ("mean", "var", "rstd", "dif", "shift"))
        xn = sb("xn", [P, SLOTS, QT, D])
        var_ready, sd_ready, chain, rstd_ready, dve_xn, pool_xn, turned, kept = (
            nc.alloc_semaphore(tag + n) for n in ("var_r", "sd", "chain", "rstd", "dve_xn", "pool_xn", "turned", "kept"))
        with nc.Block() as block:
            block.sync(loads)

            @block.vector
            def _(dve):
                ch = Chain(dve, chain)
                if measured < NT:
                    ch.link(measure(nc, k, src, range(measured, NT)))
                combine(nc, k, ch, mean, var, dif, var_ready)
                scales(nc, dve, ch, var, mean, rstd, shift, sd_ready, rstd_ready)
                for i in range(NCH):
                    if i >= SLOTS:
                        dve.wait_ge(turned, i - SLOTS + 1)
                    for j in range(QT - 1):
                        t = i * QT + j
                        nc.vector.tensor_scalar(xn[:, i % SLOTS, j, :], src[:, t, :], col(mean, t), col(rstd, t),
                                                ALU.subtract, ALU.mult).then_inc(dve_xn, 1)

            @block.gpsimd
            def _(pool):
                pool.wait_ge(rstd_ready, 1)
                for i in range(NCH):
                    if i >= SLOTS:
                        pool.wait_ge(turned, i - SLOTS + 1)
                    t = i * QT + QT - 1
                    nc.gpsimd.tensor_scalar(xn[:, i % SLOTS, QT - 1, :], src[:, t, :], col(mean, t), col(rstd, t),
                                            ALU.subtract, ALU.mult).then_inc(pool_xn, 1)

            @block.scalar
            def _(act):
                act.wait_ge(var_ready, 1)
                nc.scalar.activation(var[:], var[:], ACT.Sqrt).then_inc(sd_ready, 1)
                for i in range(NCH):
                    act.wait_ge(turned, i + 1)
                    b = i * CH // L
                    nc.scalar.activation(dst[:, i * CH:(i + 1) * CH], k.ps[:, i % SLOTS, :], ACT.Identity,
                                         bias=shift_of(b), scale=scale_of(b)).then_inc(kept, 1)

            @block.tensor
            def _(pe):
                for i in range(NCH):
                    if i >= SLOTS:
                        pe.wait_ge(kept, i - SLOTS + 1)
                    for j in range(QT):
                        if j < QT - 1:
                            pe.wait_ge(dve_xn, i * (QT - 1) + j + 1)
                        else:
                            pe.wait_ge(pool_xn, i + 1)
                        ins = nc.tensor.transpose(k.ps[:, i % SLOTS, j * P:(j + 1) * P], xn[:, i % SLOTS, j, :],
                                                  k.cst[:, C_ID:C_ID + P])
                    ins.then_inc(turned, 1)


def scan_sublayer(nc, k, m):
    with ExitStack() as c:
        def sb(name, shape, dt=F32):
            return c.enter_context(nc.sbuf_tensor("ss_" + name, shape, dt))

        wp = sb("wp", [P, 3, SP])
        wx = sb("wx", [RANK, D])
        wdt = sb("wdt", [RANK, SP])
        wdtx = sb("wdtx", [P, SP])
        col = sb("col", [P, 3])
        aneg = sb("aneg", [P, 1])
        wout = sb("wout", [P, B, D])
        dpg = sb("dpg", [P, B, D])
        z, e1, dt, abar, bx, hs = (sb(n, [P, L]) for n in ("z", "e1", "dt", "abar", "bx", "hs"))
        loaded, dtw, dtw_kept, proj, chain, act_done, y_ready, aready = (
            nc.alloc_semaphore("ss_" + n) for n in
            ("loaded", "dtw", "dtw_kept", "proj", "chain", "act_done", "y_ready", "aready"))
        hs_ready, w_ready, z_ready, x_new = (nc.alloc_semaphore("ss_" + n) for n in ("hs_ready", "w_ready", "z_ready", "x_new"))

        def q(i):
            return k.ps[:, 2 * i:2 * i + 2, :].rearrange("p h n -> p (h n)")

        def loads(sp):
            sp.dma_start(wp[:], m["ssm_wp"]).then_inc(loaded, 16)
            sp.dma_start(wx[:], m["ssm_wx"]).then_inc(loaded, 16)
            sp.dma_start(wdt[:], m["ssm_wdt"]).then_inc(loaded, 16)
            sp.dma_start(col[:], m["ssm_col"]).then_inc(loaded, 16)
            sp.dma_start(wout[:], m["ssm_wout"]).then_inc(loaded, 16)

        normalise(nc, k, "n0", k.x, k.hT, lambda b: k.mod[:, 0, CA, b:b + 1], lambda b: k.mod[:, 0, SA, b:b + 1], loads)
        with nc.Block() as block:
            @block.tensor
            def _(pe):
                pe.wait_ge(loaded, 5 * 16)
                nc.tensor.matmul(k.ps[:, 0, 0:SP], wx[:], wdt[:], start=True, stop=True).then_inc(dtw, 1)
                pe.wait_ge(dtw_kept, 1)
                for i in range(4):
                    for half in range(2):
                        for b in range(B):
                            w = wdtx[:] if i == 0 else wp[:, i - 1, :]
                            at = b * L + half * CH
                            ins = nc.tensor.matmul(k.ps[SP * b:SP * b + SP, 2 * i + half, :], w, k.hT[:, at:at + CH],
                                                   start=True, stop=True)
                    ins.then_inc(proj, 1)
                pe.wait_ge(hs_ready, 1)
                pe.wait_ge(w_ready, 1)
                for t in range(NT):
                    b, bank = t // TB, t // 4
                    o = k.ps[:, bank, (t % 4) * P:(t % 4 + 1) * P]
                    nc.tensor.matmul(o, hs[:, (t % TB) * P:(t % TB + 1) * P], wout[:, b, :], start=True, stop=False)
                    ins = nc.tensor.matmul(o, k.hT[:, t * P:(t + 1) * P], dpg[:, b, :], start=False, stop=True)
                    if t % 4 == 3:
                        ins.then_inc(y_ready, 1)

            @block.scalar
            def _(act):
                act.wait_ge(w_ready, 2)
                nc.scalar.activation(aneg[:], col[:, 0:1], ACT.Exp).then_inc(act_done, 1)
                act.wait_ge(z_ready, 1)
                nc.scalar.activation(e1[:], z[:], ACT.Abs).then_inc(act_done, 1)
                act.wait_ge(act_done, 2)
                nc.scalar.activation(e1[:], e1[:], ACT.Exp, scale=-1.0).then_inc(act_done, 1)
                act.wait_ge(act_done, 3)
                nc.scalar.activation(e1[:], e1[:], ACT.Ln, bias=1.0).then_inc(act_done, 1)
                act.wait_ge(aready, 3)
                nc.scalar.activation(abar[:], z[:], ACT.Exp).then_inc(act_done, 1)

            @block.vector
            def _(dve):
                ch = Chain(dve, chain)
                dve.wait_ge(loaded, 5 * 16)
                for b in range(B):
                    nc.vector.tensor_tensor(wout[:, b, :], wout[:, b, :], k.row[:, 0, b, :], ALU.mult)
                    ins = nc.vector.tensor_scalar(dpg[:, b, :], k.cst[:, C_ID:C_ID + D], col[:, 2:3],
                                                  k.mod[:, 0, GA, b:b + 1], ALU.mult, ALU.mult)
                ins.then_inc(w_ready, 1)
                nc.vector.tensor_scalar(col[:, 0:1], col[:, 0:1], 88.0, None, ALU.min).then_inc(w_ready, 1)
                dve.wait_ge(dtw, 1)
                nc.vector.tensor_copy(wdtx[:], k.ps[:, 0, 0:SP]).then_inc(dtw_kept, 1)
                dve.wait_ge(act_done, 1)
                nc.vector.tensor_scalar(aneg[:], aneg[:], -1.0, None, ALU.mult).then_inc(aready, 1)
                dve.wait_ge(proj, 1)
                nc.vector.tensor_scalar(z[:], q(0), col[:, 1:2], None, ALU.add).then_inc(z_ready, 1)
                dve.wait_ge(z_ready, 1)
                dve.wait_ge(act_done, 4)
                nc.vector.scalar_tensor_tensor(dt[:], z[:], 0.0, e1[:], ALU.max, ALU.add).then_inc(aready, 1)
                dve.wait_ge(aready, 2)
                nc.vector.tensor_scalar(z[:], dt[:], aneg[:], -104.0, ALU.mult, ALU.max).then_inc(aready, 1)
                dve.wait_ge(proj, 4)
                ch.link(nc.vector.tensor_tensor(bx[:], q(1), dt[:], ALU.mult))
                ch.link(nc.vector.tensor_tensor(bx[:], q(3), bx[:], ALU.mult))
                dve.wait_ge(act_done, 5)
                ch.link(nc.vector.tensor_tensor_scan(hs[:], abar[:], bx[:], 0.0, ALU.mult, ALU.add))
                nc.vector.tensor_tensor(hs[:], q(2), hs[:], ALU.mult).then_inc(hs_ready, 1)
                for i in range(NCH):
                    dve.wait_ge(y_ready, i + 1)
                    xs = k.x[:, 4 * i:4 * i + 4, :].rearrange("p t d -> p (t d)")
                    nc.vector.tensor_tensor(xs, xs, k.ps[:, i, :], ALU.add).then_inc(x_new, 1)
                    dve.wait_ge(x_new, i + 1)
                    measure(nc, k, k.x, range(4 * i, 4 * i + 4))


CT = CH // P


def rank(nc, ch, v, n, before, js):
    for j in js:
        vj = v[:, :, j:j + 1]
        if j + 1 < n:
            ins = nc.vector.tensor_tensor(before[:, :, j + 1:n, j], vj.broadcast_to([P, CT, n - j - 1]),
                                          v[:, :, j + 1:n], ALU.is_ge)
        if j:
            ins = nc.vector.tensor_tensor(before[:, :, 0:j, j], vj.broadcast_to([P, CT, j]), v[:, :, 0:j], ALU.is_gt)
        ins.then_inc(ch.sem, 1)
        ch.at += 1
    ch.eng.wait_ge(ch.sem, ch.base + ch.at)


def first_mixture(nc, k, m, by_distance):
    GR, PER, TOPG, TOPK, ROUTE = 4, E // 4, 2, 4, 2.5
    with ExitStack() as c:
        def sb(name, shape, dt=F32):
            return c.enter_context(nc.sbuf_tensor("gm_" + name, shape, dt))

        w1, w3, w2 = (sb(n, [P, E, D]) for n in ("w1", "w3", "w2"))
        bias, b2, wg = sb("bias", [P, 2, E]), sb("b2", [E, D]), sb("wg", [P, E])
        sg, hc = sb("sg", [P, 2, CH]), sb("hc", [P, 2, CH])
        y = sb("y", [P, NT, D])
        gated = sb("gated", [P, CT, D])
        s, w = sb("s", [P, NT, E]), sb("w", [P, NT, E])
        wc = sb("wc", [P, CT, E])
        wT = sb("wT", [E, CH])
        v, cnt = sb("v", [P, CT, E]), sb("cnt", [P, CT, E])
        gmax, gcnt = sb("gmax", [P, CT, GR]), sb("gcnt", [P, CT, GR])
        gbef, bef = sb("gbef", [P, CT, GR, GR]), sb("bef", [P, CT, E, E])
        total = sb("total", [P, CT])
        zero = sb("zero", [P, CH])
        row1 = sb("row1", [1, L], BF16)
        zero_set, cleared = nc.alloc_semaphore("gm_zero_set"), nc.alloc_semaphore("gm_cleared")
        (gate_in, loaded, logits, sig, chain, w_ready, w_turned, wT_ready, b2_done, y_begun, up, silu, prod, down,
         added, gated_step) = (
            nc.alloc_semaphore("gm_" + n) for n in
            ("gate_in", "loaded", "logits", "sig", "chain", "w_ready", "w_turned", "wT_ready", "b2_done", "y_begun",
             "up", "silu", "prod", "down", "added", "gated_step"))
        A, C, O, G, WT = 0, 2, 4, 6, 7

        def chunks(eng, body):
            with eng.Fori(0, NCH - 1) as ci:
                body(ci, True)
            body(NCH - 1, False)

        def loads(sp):
            by_distance.load(sp, m)
            sp.dma_start(wg[:], m["gate_w"]).then_inc(gate_in, 16)
            for t, name in ((w1, "w1"), (w3, "w3"), (w2, "w2"), (bias, "bias"), (b2, "b2")):
                sp.dma_start(t[:], m["ffn_" + name]).then_inc(loaded, 16)

        normalise(nc, k, "n1", k.x, k.hT, lambda b: k.mod[:, 0, CB, b:b + 1], lambda b: k.mod[:, 0, SB, b:b + 1], loads,
                  measured=NT)
        with nc.Block() as block:
            @block.sync
            def _(sp):
                by_distance.spread_out(sp)
                sp.wait_ge(zero_set, 4)
                sp.dma_start(k.rows_in[0:E * CAP, 0:D].rearrange("(p a) d -> p a d", p=P),
                             zero[:, 0:D].unsqueeze(1).broadcast_to([P, E * CAP // P, D])).then_inc(cleared, 16)
                sp.dma_start(k.rows_in[0:E * CAP, D:D + 1].bitcast(I32).rearrange("(p a) b -> p (a b)", p=P), m["unused_rows"],
                             allow_slow_non_contiguous=True).then_inc(cleared, 16)
                sp.dma_start(k.rows_out[0:2 * TOK, :].rearrange("(a p q) d -> p a (q d)", p=P, q=CH // D),
                             zero[:].unsqueeze(1).broadcast_to([P, 2 * TOK // (P * CH // D), CH])).then_inc(cleared, 16)
                for base in range(2):
                    last = 64 * base + ROWS
                    for g in range(NG):
                        sp.dma_start(k.kop[last:last + 1, g, base::2, :], row1[:].unsqueeze(1).broadcast_to([1, 2, L])).then_inc(cleared, 16)
                sp.wait_ge(cleared, (3 + 2 * NG) * 16)

            @block.tensor
            def _(pe):
                def upper(n, e, chunk):
                    pe.wait_ge(prod, n + 1)
                    tok = bass.ds(chunk * CH, CH)
                    nc.tensor.matmul(k.ps[:, A + e % 2, :], w1[:, e, :], k.hT[:, tok], start=True, stop=True)
                    nc.tensor.matmul(k.ps[:, C + e % 2, :], w3[:, e, :], k.hT[:, tok], start=True, stop=True).then_inc(up, 1)

                def lower(n, e):
                    pe.wait_ge(prod, n + 3)
                    pe.wait_ge(added, n + 1)
                    for j in range(CT):
                        ins = nc.tensor.matmul(k.ps[:, O + e % 2, j * P:(j + 1) * P], hc[:, e % 2, j * P:(j + 1) * P],
                                               w2[:, e, :], start=True, stop=True)
                    ins.then_inc(down, 1)

                def turn_weights(chunk):
                    pe.wait_ge(w_ready, chunk + 1)
                    for j in range(CT):
                        ins = nc.tensor.transpose(k.ps[0:E, WT, j * P:(j + 1) * P],
                                                  wc[:, j, :],
                                                  k.cst[:, C_ID:C_ID + P])
                    ins.then_inc(w_turned, 1)

                def add_b2(chunk):
                    pe.wait_ge(wT_ready, chunk + 1)
                    for j in range(CT):
                        ins = nc.tensor.matmul(k.ps[:, G, j * P:(j + 1) * P], wT[:, j * P:(j + 1) * P], b2[:],
                                               start=True, stop=True)
                    ins.then_inc(b2_done, 1)

                by_distance.pick(pe, WT)
                pe.wait_ge(gate_in, 16)
                for bank, tiles in ((O, range(CT)), (G, range(CT, NT))):
                    for t in tiles:
                        ins = nc.tensor.matmul(k.ps[:, bank, t * E:(t + 1) * E], k.hT[:, t * P:(t + 1) * P], wg[:], start=True, stop=True)
                    ins.then_inc(logits, 1)
                pe.wait_ge(loaded, 5 * 16)
                upper(0, 0, 0)
                pe.wait_ge(sig, 2)
                pe.wait_ge(by_distance.strip_ready, 1)
                turn_weights(0)
                add_b2(0)

                def chunk_of(chunk, more):
                    n0 = chunk * E
                    for e in range(E):
                        if e + 1 < E:
                            upper(n0 + e + 1, e + 1, chunk)
                        elif more:
                            upper(n0 + E, 0, chunk + 1)
                        lower(n0 + e, e)
                        if more and e == E - 2:
                            turn_weights(chunk + 1)
                        if more and e == E - 1:
                            add_b2(chunk + 1)

                chunks(pe, chunk_of)

            @block.scalar
            def _(act):
                def silu_of(n, e):
                    act.wait_ge(up, n + 1)
                    act.wait_ge(prod, n + 1)
                    nc.scalar.activation(sg[:, e % 2, :], k.ps[:, A + e % 2, :], ACT.Silu,
                                         bias=bias[:, 0, e:e + 1]).then_inc(silu, 1)

                def keep_weights(chunk):
                    act.wait_ge(w_turned, chunk + 1)
                    nc.scalar.copy(wT[:], k.ps[0:E, WT, :]).then_inc(wT_ready, 1)

                def begin_y(chunk):
                    act.wait_ge(b2_done, chunk + 1)
                    nc.scalar.copy(y[:, bass.ds(chunk * CT, CT), :],
                                   k.ps[:, G, :].rearrange("p (t d) -> p t d", t=CT)).then_inc(y_begun, 1)

                for i, (bank, t0, t1) in enumerate(((O, 0, CT), (G, CT, NT))):
                    act.wait_ge(logits, i + 1)
                    nc.scalar.activation(s[:, t0:t1, :].rearrange("p t e -> p (t e)"), k.ps[:, bank, t0 * E:t1 * E],
                                         ACT.Sigmoid).then_inc(sig, 1)
                by_distance.exps(act, WT)
                act.wait_ge(loaded, 5 * 16)
                silu_of(0, 0)
                keep_weights(0)
                begin_y(0)

                def chunk_of(chunk, more):
                    n0 = chunk * E
                    for e in range(E):
                        if e + 1 < E or more:
                            silu_of(n0 + e + 1, (e + 1) % E)
                        if more and e == E - 2:
                            keep_weights(chunk + 1)
                        if more and e == E - 1:
                            begin_y(chunk + 1)

                chunks(act, chunk_of)

            @block.vector
            def _(dve):
                ch = Chain(dve, chain)

                def route(chunk, step):
                    tiles = bass.ds(chunk * CT, CT)
                    sc = s[:, tiles, :]
                    if step == 0:
                        ch.link(nc.vector.tensor_reduce(gmax[:], sc.rearrange("p t (g e) -> p t g e", g=GR), AX.X, ALU.max))
                        rank(nc, ch, gmax, GR, gbef, range(GR))
                    elif step == 1:
                        ch.link(nc.vector.tensor_reduce(gcnt[:], gbef[:], AX.X, ALU.add))
                        ch.link(nc.vector.tensor_scalar(gcnt[:], gcnt[:], float(TOPG), -4.0, ALU.is_ge, ALU.mult))
                        ch.link(nc.vector.tensor_tensor(v[:].rearrange("p t (g e) -> p t g e", g=GR),
                                                        sc.rearrange("p t (g e) -> p t g e", g=GR),
                                                        gcnt[:].unsqueeze(3).broadcast_to([P, CT, GR, PER]), ALU.add))
                    elif step < 10:
                        rank(nc, ch, v, E, bef, (2 * step - 4, 2 * step - 3))
                    elif step == 10:
                        ch.link(nc.vector.tensor_reduce(cnt[:], bef[:], AX.X, ALU.add))
                    elif step == 11:
                        ch.link(nc.vector.scalar_tensor_tensor(v[:], cnt[:], float(TOPK), sc, ALU.is_lt, ALU.mult))
                        ch.link(nc.vector.tensor_reduce(total[:], v[:], AX.X, ALU.add))
                    elif step == 12:
                        ch.link(nc.vector.reciprocal(total[:], total[:]))
                        ch.link(nc.vector.tensor_scalar(total[:], total[:], ROUTE, None, ALU.mult))
                    elif step == 13:
                        if not (isinstance(chunk, int) and chunk == 0):
                            dve.wait_ge(w_turned, chunk)
                        ch.link(nc.vector.tensor_tensor(wc[:], v[:], total[:].unsqueeze(2).broadcast_to([P, CT, E]), ALU.mult))
                        nc.vector.tensor_copy(w[:, tiles, :], wc[:]).then_inc(w_ready, 1)

                def product(n, e):
                    dve.wait_ge(silu, n + 1)
                    dve.wait_ge(down, n + 1)
                    nc.vector.scalar_tensor_tensor(hc[:, e % 2, :], k.ps[:, C + e % 2, :], bias[:, 1, e:e + 1],
                                                   sg[:, e % 2, :], ALU.add, ALU.mult).then_inc(prod, 1)

                def add(n, chunk, e):
                    dve.wait_ge(down, n + 3)
                    dve.wait_ge(added, n + 2)
                    if e == 0:
                        dve.wait_ge(y_begun, chunk + 1)
                        dve.wait_ge(w_ready, chunk + 1)
                    for j in range(CT):
                        t = bass.ds(chunk * CT + j, 1)
                        yt = y[:, t, :].rearrange("p a d -> p (a d)")
                        ins = nc.vector.scalar_tensor_tensor(yt, k.ps[:, O + e % 2, j * P:(j + 1) * P],
                                                             w[:, t, e], yt, ALU.mult, ALU.add)
                    ins.then_inc(added, 1)

                dve.sem_inc(prod, 2)
                dve.sem_inc(added, 2)
                dve.sem_inc(down, 2)
                ch.link(nc.vector.memset(gbef[:], 0.0))
                ch.link(nc.vector.memset(bef[:], 0.0))
                by_distance.largest(dve, WT)
                dve.wait_ge(sig, 1)
                for step in range(14):
                    route(0, step)
                dve.wait_ge(sig, 2)
                links = ch.at - 2
                product(0, 0)

                def chunk_of(chunk, more):
                    n0 = chunk * E
                    if more:
                        ch.base, ch.at = (chunk + 1) * links, 2
                    for e in range(E):
                        if e + 1 < E or more:
                            product(n0 + e + 1, (e + 1) % E)
                        if more:
                            route(chunk + 1, e)
                        add(n0 + e, chunk, e)
                        if not more and e < (NT - CT) // 2:
                            dve.wait_ge(gated_step, 2 * (2 * e // CT) + 3)
                            measure(nc, k, k.x, (2 * e, 2 * e + 1))

                chunks(dve, chunk_of)

            @block.gpsimd
            def _(pool):
                nc.gpsimd.memset(zero[:], 0.0).then_inc(zero_set, 1)
                nc.gpsimd.memset(k.kop[:].rearrange("p g a n -> p (g a n)").bitcast(I32), 0).then_inc(zero_set, 1)
                nc.gpsimd.memset(k.qop[:].rearrange("p g a n -> p (g a n)").bitcast(I32), 0).then_inc(zero_set, 1)
                nc.gpsimd.memset(k.row0[:], 0.0)
                nc.gpsimd.memset(row1[:], 1.0).then_inc(zero_set, 1)
                pool.sem_inc(gated_step, 1)
                with pool.Fori(0, B) as b:
                    with pool.Fori(0, L // CH) as half:
                        chunk = b * (L // CH) + half
                        tiles = bass.ds(chunk * CT, CT)
                        pool.wait_ge(added, (chunk + 1) * E + 2)
                        gate = k.row[:, 5, bass.ds(b, 1), :].broadcast_to([P, CT, D])
                        pool.wait_ge(gated_step, 2 * chunk + 1)
                        nc.gpsimd.tensor_tensor(gated[:], y[:, tiles, :], gate, ALU.mult).then_inc(gated_step, 1)
                        pool.wait_ge(gated_step, 2 * chunk + 2)
                        nc.gpsimd.tensor_tensor(k.x[:, tiles, :], k.x[:, tiles, :], gated[:], ALU.add).then_inc(gated_step, 1)


def attention_inputs(nc, m, a, c):
    def sb(name, shape):
        return c.enter_context(nc.sbuf_tensor(a.tag + name, shape, F32))

    a.w, a.bias, a.vb = sb("w", [P, 3, D]), sb("bias", [P, 2]), sb("vb", [P, D])
    a.w_in = nc.alloc_semaphore(a.tag + "w_in")
    a.loads = [nc.alloc_semaphore(a.tag + f"loads{g}") for g in range(NG)]

    def loads(sp):
        sp.dma_start(a.w[:], m[a.tag + "w"]).then_inc(a.w_in, 16)
        sp.dma_start(a.bias[:], m[a.tag + "bias"]).then_inc(a.w_in, 16)
        sp.dma_start(a.vb[:], m[a.tag + "vb"].broadcast_to([P, D])).then_inc(a.w_in, 16)
        if a.causal:
            sp.dma_start(a.ob[:].rearrange("p b d -> p (b d)"), m["ca_ob"].broadcast_to([P, D])).then_inc(a.w_in, 16)

    return loads


def projection(nc, k, a):
    tag = a.tag + "pr_"
    SLOTS = 3
    FLIPS = H * NEAR // CH
    w, bias = a.w, a.bias
    half = SLOTS * 2 * CH
    full, rest = (a.low[:, x:x + half].rearrange("p (s o n) -> p s o n", s=SLOTS, o=2) for x in (0, half))
    parts = a.ring[:].rearrange("p r n -> p (r n)")[:, 0:2 * 2 * 3 * L // 2].bitcast(BF16).rearrange(
        "p (s o t n) -> p s o t n", s=2, o=2, t=3)
    loaded = a.w_in
    done, v_done, v_kept, ones_set = (nc.alloc_semaphore(tag + n) for n in ("done", "v_done", "v_kept", "ones_set"))
    stored = [nc.alloc_semaphore(tag + f"stored{s}") for s in range(2)]
    whole, part1, rest1, part2, rest2 = (
        [nc.alloc_semaphore(tag + f"{n}{o}") for o in "qk"] for n in ("whole", "part1_", "rest1_", "part2_", "rest2_"))
    scale = (HD ** -0.5, 1.0)
    PER = L // CH

    def flips(i):
        return range(i * FLIPS // NCH, (i + 1) * FLIPS // NCH)

    def part(o, n, i):
        return parts[:, i // PER % 2, o, n, i % PER * CH:(i % PER + 1) * CH]
    if not a.causal:
        flipped, near_kept = nc.alloc_semaphore("rb_flipped"), nc.alloc_semaphore("rb_near_kept")
        near = a.near[:].rearrange("p h q -> p (h q)")

    def sync(sp):
        for b in range(B):
            for n in range(3):
                for o in range(2):
                    sp.wait_ge((part1, part2, rest2)[n][o], PER * (b + 1))
                    sp.dma_start(a.qk[o, :, n if o else 2 - n, :, b * L:(b + 1) * L],
                                 parts[:, b % 2, o, n, :]).then_inc(stored[b % 2], 16)
            if b == 1:
                sp.wait_ge(stored[0], 6 * 16)
                load_operands(sp, k, a, 0, 0)
        for s in range(2):
            sp.wait_ge(stored[s], B // 2 * 6 * 16)

    def tensor(pe):
        pe.wait_ge(loaded, (4 if a.causal else 3) * 16)
        for i in range(NCH):
            if i >= 2:
                for o in range(2):
                    pe.wait_ge(whole[o], i - 1)
                pe.wait_ge(v_kept, i - 1)
            for o in range(2):
                ins = nc.tensor.matmul(k.ps[:, 2 * o + i % 2, :], w[:, o, :], k.hT[:, i * CH:(i + 1) * CH],
                                       start=True, stop=True)
                ins.then_inc(done, 1)
            for j in range(4):
                t = 4 * i + j
                ins = nc.tensor.matmul(k.ps[:, 4 + i % 2, j * P:(j + 1) * P], k.hT[:, t * P:(t + 1) * P],
                                       w[:, 2, :], start=True, stop=True)
            ins.then_inc(v_done, 1)
            if not a.causal:
                for f in flips(i):
                    if f >= 2:
                        pe.wait_ge(near_kept, f - 1)
                    nc.tensor.matmul(k.ps[:, 6 + f % 2, :], k.cst[:, C_FLIP:C_FLIP + P], near[:, f * CH:(f + 1) * CH],
                                     start=True, stop=True).then_inc(flipped, 1)
        for o in range(2):
            pe.wait_ge(whole[o], NCH)
        pe.wait_ge(v_kept, NCH)
        if not a.causal:
            pe.wait_ge(near_kept, FLIPS)

    def first_rest(eng, o, i):
        s = i % SLOTS
        eng.wait_ge(part1[o], i + 1)
        if i >= SLOTS:
            eng.wait_ge(rest2[o], i - SLOTS + 1)
        eng.tensor_tensor(rest[:, s, o, :], full[:, s, o, :], part(o, 0, i), ALU.subtract).then_inc(rest1[o], 1)

    def third_part(eng, o, i):
        s = i % SLOTS
        eng.wait_ge(part2[o], i + 1)
        eng.tensor_tensor(part(o, 2, i), rest[:, s, o, :], part(o, 1, i), ALU.subtract).then_inc(rest2[o], 1)

    def scalar(act):
        for i in range(NCH + 1):
            for o in range(2):
                if i < NCH:
                    s = i % SLOTS
                    act.wait_ge(whole[o], i + 1)
                    if i >= 2 * PER:
                        act.wait_ge(stored[i // PER % 2], i // (2 * PER) * 6 * 16)
                    nc.scalar.copy(part(o, 0, i), full[:, s, o, :]).then_inc(part1[o], 1)
                if i:
                    s = (i - 1) % SLOTS
                    act.wait_ge(rest1[o], i)
                    nc.scalar.copy(part(o, 1, i - 1), rest[:, s, o, :]).then_inc(part2[o], 1)
            if not a.causal and i < NCH:
                for f in flips(i):
                    act.wait_ge(flipped, f + 1)
                    nc.scalar.copy(near[:, f * CH:(f + 1) * CH], k.ps[:, 6 + f % 2, :]).then_inc(near_kept, 1)
        for s in range(2):
            act.wait_ge(stored[s], B // 2 * 6 * 16)

    def gpsimd(pool):
        for i in range(NCH + 1):
            if i < NCH:
                first_rest(nc.gpsimd, 1, i)
            if i:
                third_part(nc.gpsimd, 1, i - 1)
        pool.wait_ge(ones_set, 1)
        pool.wait_ge(v_kept, NCH)
        for o in range(2):
            pool.wait_ge(rest2[o], NCH)
        if not a.causal:
            pool.wait_ge(near_kept, FLIPS)

    def vector(dve):
        nc.vector.memset(a.v[:, :, :, HD:VA], 1.0).then_inc(ones_set, 1)
        dve.wait_ge(loaded, (4 if a.causal else 3) * 16)
        for i in range(NCH + 1):
            if i < NCH:
                for o in range(2):
                    dve.wait_ge(done, 2 * i + o + 1)
                    if i >= SLOTS:
                        dve.wait_ge(rest1[o], i - SLOTS + 1)
                    nc.vector.tensor_scalar(full[:, i % SLOTS, o, :], k.ps[:, 2 * o + i % 2, :], bias[:, o:o + 1], scale[o],
                                            ALU.add, ALU.mult).then_inc(whole[o], 1)
            if i:
                first_rest(nc.vector, 0, i - 1)
            if i < NCH:
                dve.wait_ge(v_done, i + 1)
                out = a.v[:, 4 * i:4 * i + 4, :, 0:HD]
                src = k.ps[:, 4 + i % 2, :].rearrange("p (t h d) -> p t h d", h=H, d=HD)
                row = a.vb[:].rearrange("p (t h d) -> p t h d", t=1, d=HD).broadcast_to([P, 4, H, HD])
                nc.vector.tensor_tensor(out, src, row, ALU.add).then_inc(v_kept, 1)
            if i:
                third_part(nc.vector, 0, i - 1)

    first = Core()
    first.sync, first.tensor, first.scalar, first.gpsimd, first.vector = sync, tensor, scalar, gpsimd, vector
    return first


ROWS = 6 * HD
NLOAD = 14 * 16


def load_operands(sp, k, a, b, g):
    for base in range(2):
        last = 64 * base + ROWS
        sp.dma_start(k.qop[last:last + 1, g, :, :], k.row0[:].unsqueeze(1).broadcast_to([1, 2, L])).then_inc(a.loads[g], 16)
        for o in range(2):
            row = 64 * base
            for n in (3, 2, 1):
                start = a.qk[o, g * HG + base, 3 - n if o == 0 else 0, :, bass.ds(b * L, L)]
                rows = bass.AP(start.tensor, start.offset, [[TOK, n * HD], [2 * 3 * HD * TOK, 2], [1, L]])
                slot = k.qop[row:row + n * HD, g, :, :] if o == 0 else k.kop[row:row + n * HD, g, base::2, :]
                sp.dma_start(slot, rows).then_inc(a.loads[g], 16)
                row += n * HD


def attend(nc, k, a):
    causal, tag = a.causal, a.tag + "at_"
    RING = 16
    LAG = 2
    NV = 1 if causal else 3
    NBANK = 3
    AHEAD = 0.17
    GAP = 3

    def pieces():
        order = ([0, 1, 2, 3, 4, 5, 6, 7],) * 2 if causal else ([1, 5, 2, 6, 0, 7, 3, 4], [3, 0, 6, 1, 5, 2, 7, 4])
        out = []
        for half in range(2):
            for i in order[half]:
                q0, q1 = half * CH, (half + 1) * CH
                if causal:
                    q0 = max(q0, i * P)
                if q0 < q1:
                    out.append((i, half, q0, q1))
        return out

    PIECES = pieces()
    NP_ = len(PIECES)
    NB_ = NP_ * HG
    NA_ = HG * TB + 1
    last_of = {half: max(n for n, p in enumerate(PIECES) if p[1] == half) for half in range(2)}
    first_of = {half: min(n for n, p in enumerate(PIECES) if p[1] == half) for half in range(2)}

    def near(n):
        i, half, q0, q1 = PIECES[n]
        lo, hi = max(q0, (i - 1) * P), min(q1, (i + 2) * P)
        return (lo, hi) if lo < hi and not causal else None

    def segments(n):
        i, half, q0, q1 = PIECES[n]
        if causal:
            return [(0, q0, q1)]
        cuts = [(2, q0, min(q1, (i - 1) * P)), (0, max(q0, (i - 1) * P), min(q1, (i + 2) * P)), (1, max(q0, (i + 2) * P), q1)]
        return [s for s in cuts if s[1] < s[2]]

    def value_parts(n):
        segs = segments(n)
        if len(segs) == 1 and segs[0][2] - segs[0][1] > P:
            var, s0, s1 = segs[0]
            mid = s0 + (s1 - s0) // P // 2 * P
            segs = [(var, s0, mid), (var, mid, s1)]
        return segs[:(len(segs) + 1) // 2], segs[(len(segs) + 1) // 2:]

    TILES = [0, 7, 1, 6, 2, 5, 3, 4]

    def top_of(n):
        return n // TB, TILES[n % TB]

    def top_keys(n):
        return (top_of(n)[1] + 1) * P if causal else L

    def plan_tops():
        a = [top_keys(n) + 64 for n in range(NA_ - 1)]
        b = [p[3] - p[2] + 64 for p in PIECES for _ in range(HG)]
        ends = [sum(a[:n + 1]) / sum(a) - AHEAD for n in range(NA_ - 1)]
        out = [[] for _ in b]

        def turn_at(x):
            return min(t for t in range(len(b)) if sum(b[:t + 1]) >= x * sum(b) - 1e-6)

        for n, x in enumerate(ends):
            if x > 0:
                out[turn_at(x)].append((0, n))
        last = turn_at(ends[-1]) + GAP
        out[last].append((0, NA_ - 1))
        for n, x in enumerate(ends):
            if x <= 0:
                out[max(last, turn_at(1 + x))].append((1, n))
        return out

    NEARS = [n for n in range(NP_) if near(n)]

    with ExitStack() as c:
        def sb(name, shape, dt=F32):
            return c.enter_context(nc.sbuf_tensor(tag + name, shape, dt))

        def sem(name):
            return nc.alloc_semaphore(tag + name)

        qop, kop, loads = k.qop, k.kop, a.loads
        top = sb("top", [P, HG * TB])
        negm = sb("negm", [HG * TB, P], BF16)
        ring = a.ring = sb("ring", [P, RING, CH])
        a.low = sb("low", [P, 2 * 3 * TB * HG * 32])
        vs = a.low[:, 0:2 * NV * TB * HG * 32].rearrange("p (s v t h d) -> p s v t h d", s=2, v=NV, t=TB, h=HG)
        few = a.low[:, 0:(B - 1) * P].rearrange("p (b q) -> p b q", b=B - 1)
        osb = sb("osb", [P, L])
        mrow = [sem(f"mrow{g}") for g in range(NG)]
        stored = sem("stored")
        few_in, few_out, inverted = (sem(n) for n in ("few_in", "few_out", "inverted"))
        (a_filled, a_read, b_filled, exped, scaled, pv_done, o_copied,
         vs_zero, vs_ready) = (sem(n) for n in
                               ("a_filled", "a_read", "b_filled", "exped", "scaled",
                                "pv_done", "o_copied", "vs_zero", "vs_ready"))
        A_BANK, B_BANK, O_BANK = 0, 4, 7

        def place(j):
            return 64 * (j % 2), j // 2

        def unit(b, g):
            return b * NG + g

        def after(b, g):
            return (b, g + 1) if g < NG - 1 else (b + 1, 0)

        def before(b, g):
            return (b, g - 1) if g else (b - 1, NG - 1)

        def units(eng, one):
            one(0, 0)
            with eng.Fori(0, B - 1) as b:
                for g in range(1, NG):
                    one(b, g)
                one(b + 1, 0)
            for g in range(1, NG):
                one(B - 1, g)

        def is_first(b, g):
            return isinstance(b, int) and b == 0 and g == 0

        def is_last(b, g):
            return isinstance(b, int) and b == B - 1 and g == NG - 1

        def bank_of(g, t):
            return (g * NB_ + t) % NBANK

        def bank_free(g, t):
            if t >= NBANK:
                return t - NBANK + 1
            last = (g - 1) % NG
            return max(x + 1 - NB_ for x in range(NB_) if bank_of(last, x) == bank_of(g, t) and x + 1 - NB_ <= 0)

        first = projection(nc, k, a)
        with nc.Block() as block:
            @block.sync
            def _(sp):
                first.sync(sp)

                def largest(b, g):
                    sp.wait_ge(a_read, (unit(b, g) + 1) * NA_)
                    for j in range(HG):
                        base, pair = place(j)
                        sp.dma_start(qop[base + ROWS:base + ROWS + 1, g, pair, :],
                                     negm[j * TB:(j + 1) * TB, :]).then_inc(mrow[g], 16)

                def store(b, g):
                    u = unit(b, g)
                    sp.wait_ge(o_copied, 2 * (u + 1))
                    for j in range(HG):
                        sp.dma_start(a.o[b, g * HG + j, :, :], osb[32 * j:32 * j + VA, :]).then_inc(stored, 16)

                def invert():
                    sp.wait_ge(pv_done, (unit(B - 1, NG - 2) + 1) * NP_)
                    sp.wait_ge(stored, unit(B - 1, 0) * HG * 16)
                    for e in range(B - 1):
                        sp.dma_start(few[:, e, :], weight_sums(a, e)).then_inc(few_in, 16)
                    sp.wait_ge(inverted, 1)
                    for e in range(B - 1):
                        sp.dma_start(weight_sums(a, e), few[:, e, :]).then_inc(few_out, 16)

                def step(b, g):
                    far = after(*after(b, g))
                    if not (isinstance(far[0], int) and far[0] == B):
                        if not is_first(b, g):
                            sp.wait_ge(pv_done, unit(b, g) * NP_ - LAG)
                        load_operands(sp, k, a, *far)
                    if not is_last(b, g):
                        largest(*after(b, g))
                    else:
                        invert()
                    store(b, g)

                load_operands(sp, k, a, 0, 1)
                largest(0, 0)
                units(sp, step)
                sp.wait_ge(stored, B * NG * HG * 16)
                sp.wait_ge(few_out, (B - 1) * 16)

            @block.tensor
            def _(pe):
                first.tensor(pe)

                def top_turn(b, g, n):
                    turn = unit(b, g) * NA_ + n
                    slot = A_BANK + 2 * ((g * NA_ + n) % 2)
                    if n == 0:
                        pe.wait_ge(loads[g], (b + 1) * NLOAD)
                    if not (isinstance(turn, int) and turn < 2):
                        pe.wait_ge(a_read, turn - 1)
                    if n == NA_ - 1:
                        pe.wait_ge(a_read, turn)
                        nc.tensor.transpose(k.ps[0:HG * TB, slot, 0:P], top[:], k.cst[:, C_ID:C_ID + P]).then_inc(a_filled, 1)
                        return
                    j, i = top_of(n)
                    pair = j // 2
                    keys = top_keys(n)
                    for half in range(2):
                        k0, k1 = half * CH, min(keys, (half + 1) * CH)
                        if k0 >= k1:
                            continue
                        diag = causal and k0 <= i * P < k1
                        ins = nc.tensor.matmul(k.ps[:, slot + half, 0:k1 - k0], qop[:, g, pair, i * P:(i + 1) * P],
                                               kop[:, g, j, k0:k1], start=True, stop=not diag)
                        if diag:
                            ins = nc.tensor.matmul(k.ps[:, slot + half, i * P - k0:(i + 1) * P - k0], k.cstb[:, C_ID:C_ID + P],
                                                   k.cstb[:, C_MA:C_MA + P], start=False, stop=True)
                    ins.then_inc(a_filled, 1)

                def score_turn(b, g, t):
                    n, j = t // HG, t % HG
                    i, half, q0, q1 = PIECES[n]
                    pair = j // 2
                    u = unit(b, g)
                    if t == 0:
                        pe.wait_ge(mrow[g], (b + 1) * HG * 16)
                    if not is_first(b, g) or t >= NBANK:
                        pe.wait_ge(exped, u * NB_ + bank_free(g, t))
                    bank = B_BANK + bank_of(g, t)
                    diag = causal and q0 == i * P
                    ins = nc.tensor.matmul(k.ps[:, bank, 0:q1 - q0], kop[:, g, j, i * P:(i + 1) * P],
                                           qop[:, g, pair, q0:q1], start=True, stop=not diag)
                    if diag:
                        ins = nc.tensor.matmul(k.ps[:, bank, 0:P], k.cstb[:, C_ID:C_ID + P], k.cstb[:, C_MB:C_MB + P],
                                               start=False, stop=True)
                    ins.then_inc(b_filled, 1)

                def value_turn(b, g, n, part):
                    i, half, q0, q1 = PIECES[n]
                    u = unit(b, g)
                    parts = value_parts(n)
                    if part == 0:
                        if n == 0:
                            pe.wait_ge(vs_ready, u + 1)
                        if n == first_of[half] and not (is_first(b, g) and half == 0):
                            pe.wait_ge(o_copied, 2 * u + half)
                        pe.wait_ge(exped, u * NB_ + (n + 1) * HG)
                        if n in NEARS:
                            pe.wait_ge(scaled, u * len(NEARS) + NEARS.index(n) + 1)
                    for x, (var, s0, s1) in enumerate(parts[part]):
                        for j in range(HG):
                            ins = nc.tensor.matmul(k.ps[32 * j:32 * j + 32, O_BANK, s0 - half * CH:s1 - half * CH],
                                                   vs[:, g % 2, var, i, j, :], ring[:, (n % (RING // HG)) * HG + j, s0 - q0:s1 - q0],
                                                   start=(n == first_of[half] and part == 0 and x == 0),
                                                   stop=(n == last_of[half] and x == len(parts[part]) - 1 and (part == 1 or not parts[1])),
                                                   skip_group_check=True)
                    if part == 1 or not parts[1]:
                        ins.then_inc(pv_done, 1)

                TOPS = plan_tops()

                def run(b, g):
                    for n in range(NP_):
                        if n >= LAG:
                            owner, vn = (b, g), n - LAG
                        else:
                            owner, vn = None if is_first(b, g) else before(b, g), NP_ - LAG + n
                        for j in range(HG):
                            t = n * HG + j
                            score_turn(b, g, t)
                            for far, x in TOPS[t]:
                                of = after(*after(b, g)) if far else after(b, g)
                                if not (isinstance(of[0], int) and of[0] == B):
                                    top_turn(*of, x)
                            if owner and j == 1:
                                value_turn(*owner, vn, 0)
                            if owner and j == 3 and value_parts(vn)[1]:
                                value_turn(*owner, vn, 1)

                for n in range(NA_):
                    top_turn(0, 0, n)
                for n in sorted(x for turns in TOPS for far, x in turns if far):
                    top_turn(0, 1, n)
                units(pe, run)
                for n in range(NP_ - LAG, NP_):
                    for part in range(2):
                        if value_parts(n)[part]:
                            value_turn(B - 1, NG - 1, n, part)

            @block.vector
            def _(dve):
                first.vector(dve)

                def tops(b, g):
                    for n in range(NA_):
                        turn = unit(b, g) * NA_ + n
                        slot = A_BANK + 2 * ((g * NA_ + n) % 2)
                        dve.wait_ge(a_filled, turn + 1)
                        if n == NA_ - 1:
                            if not is_first(b, g):
                                pb, pg = before(b, g)
                                dve.wait_ge(mrow[pg], (pb + 1) * HG * 16)
                            nc.vector.tensor_scalar(negm[:], k.ps[0:HG * TB, slot, 0:P], -1.0, None, ALU.mult).then_inc(a_read, 1)
                        else:
                            keys = top_keys(n)
                            src = k.ps[:, slot:slot + 2, :].rearrange("p a n -> p (a n)")[:, 0:keys]
                            j, i = top_of(n)
                            nc.vector.tensor_reduce(top[:, j * TB + i:j * TB + i + 1], src, AX.X, ALU.max).then_inc(a_read, 1)

                units(dve, tops)
                dve.wait_ge(few_in, (B - 1) * 16)
                nc.vector.reciprocal(few, few).then_inc(inverted, 1)

            @block.scalar
            def _(act):
                first.scalar(act)

                def copy_out(b, g, half):
                    u = unit(b, g)
                    if half == 0 and not is_first(b, g):
                        act.wait_ge(stored, u * HG * 16)
                    act.wait_ge(pv_done, u * NP_ + last_of[half] + 1)
                    nc.scalar.copy(osb[:, half * CH:(half + 1) * CH], k.ps[:, O_BANK, :]).then_inc(o_copied, 1)

                def exps(b, g):
                    u = unit(b, g)
                    for t in range(NB_):
                        n = t // HG
                        i, half, q0, q1 = PIECES[n]
                        if t == LAG * HG and not is_first(b, g):
                            copy_out(*before(b, g), 1)
                        if t == (last_of[0] + 1 + LAG) * HG:
                            copy_out(b, g, 0)
                        act.wait_ge(b_filled, u * NB_ + t + 1)
                        if t % HG == 0 and (n >= RING // HG or not is_first(b, g)):
                            act.wait_ge(pv_done, u * NP_ + n + 1 - RING // HG)
                        nc.scalar.activation(ring[:, t % RING, 0:q1 - q0], k.ps[:, B_BANK + bank_of(g, t), 0:q1 - q0],
                                             ACT.Exp).then_inc(exped, 1)

                units(act, exps)
                copy_out(B - 1, NG - 1, 1)

            @block.gpsimd
            def _(pool):
                first.gpsimd(pool)

                def values(b, g):
                    s = g % 2
                    src = a.v[:, bass.ds(b * TB, TB), g * HG:(g + 1) * HG, :]
                    ins = nc.gpsimd.tensor_copy(vs[:, s, 0, :, :, 0:VA], src)
                    if not causal:
                        for var, f in ((1, a.left), (2, a.right)):
                            by = f[:, g * HG:(g + 1) * HG].unsqueeze(1).unsqueeze(3).broadcast_to([P, TB, HG, VA])
                            ins = nc.gpsimd.tensor_tensor(vs[:, s, var, :, :, 0:VA], src, by, ALU.mult)
                    ins.then_inc(vs_ready, 1)

                def next_values(b, g):
                    if is_last(b, g):
                        return
                    if not is_first(b, g):
                        pool.wait_ge(pv_done, unit(b, g) * NP_)
                    values(*after(b, g))

                def bias(b, g):
                    u = unit(b, g)
                    for n in NEARS:
                        i, half, q0, q1 = PIECES[n]
                        if n == NEARS[len(NEARS) // 2]:
                            next_values(b, g)
                        lo, hi = near(n)
                        for j in range(HG):
                            pool.wait_ge(exped, u * NB_ + n * HG + j + 1)
                            w = ring[:, (n * HG + j) % RING, lo - q0:hi - q0]
                            ins = nc.gpsimd.tensor_tensor(w, w, a.near[:, g * HG + j, lo - (i - 1) * P:hi - (i - 1) * P], ALU.mult)
                        ins.then_inc(scaled, 1)

                nc.gpsimd.memset(vs, 0.0).then_inc(vs_zero, 1)
                pool.wait_ge(vs_zero, 1)
                values(0, 0)
                units(pool, next_values if causal else bias)


def weight_sums(a, b):
    return bass.AP(a.o.tensor, b * H * VA * L + HD * L, [[VA * L, H], [P, L // P], [1, P]])


def join_heads(nc, k, m, a, dst, before):
    tag = a.tag + "jo_"
    with ExitStack() as c:
        num = c.enter_context(nc.sbuf_tensor(tag + "num", [P, B, L], F32))
        den = c.enter_context(nc.sbuf_tensor(tag + "den", [P, B, L], F32))
        few = c.enter_context(nc.sbuf_tensor(tag + "few", [P, P], F32))
        loaded = [nc.alloc_semaphore(tag + f"loaded{b}") for b in range(B)]
        few_in, few_out = (nc.alloc_semaphore(tag + n) for n in ("few_in", "few_out"))
        wo = c.enter_context(nc.sbuf_tensor(tag + "wo", [P, B, D], F32))
        inv, first, ready, y_ready, begun, wo_in, new = (nc.alloc_semaphore(tag + n) for n in ("inv", "first", "ready", "y_ready", "begun", "wo_in", "new"))
        with nc.Block() as block:
            @block.sync
            def _(sp):
                def load_num(b):
                    sp.dma_start(num[:, b, :], bass.AP(a.o.tensor, b * H * VA * L, [[VA * L, H], [L, HD], [1, L]])).then_inc(loaded[b], 16)

                def load_den(b):
                    sp.dma_start(den[:, b, :], bass.AP(a.o.tensor, b * H * VA * L + HD * L, [[VA * L, H], [0, HD], [1, L]])).then_inc(loaded[b], 16)

                sp.dma_start(few[:], weight_sums(a, B - 1)).then_inc(few_in, 16)
                sp.dma_start(wo[:], m[a.tag + "wo"].unsqueeze(1).broadcast_to([P, B, D])).then_inc(wo_in, 16)
                for b in range(B - 1):
                    load_den(b)
                    load_num(b)
                    if b == 0:
                        sp.wait_ge(inv, 1)
                        sp.dma_start(weight_sums(a, B - 1), few[:]).then_inc(few_out, 16)
                load_num(B - 1)
                sp.wait_ge(few_out, 16)
                load_den(B - 1)

            @block.vector
            def _(dve):
                dve.wait_ge(few_in, 16)
                nc.vector.reciprocal(few[:], few[:]).then_inc(inv, 1)
                dve.wait_ge(wo_in, 16)
                before(wo).then_inc(begun, 1)
                dve.wait_ge(loaded[0], 32)
                nc.vector.tensor_tensor(num[:, 0, :], num[:, 0, :], den[:, 0, :], ALU.mult).then_inc(first, 1)
                dve.wait_ge(begun, 1)
                for i in range(NCH):
                    dve.wait_ge(y_ready, i + 1)
                    xs = dst[:, 4 * i:4 * i + 4, :].rearrange("p t d -> p (t d)")
                    nc.vector.tensor_tensor(xs, xs, k.ps[:, i, :], ALU.add).then_inc(new, 1)
                    if i % 2:
                        for j in (i - 1, i):
                            dve.wait_ge(new, j + 1)
                            measure(nc, k, dst, range(4 * j, 4 * j + 4))

            @block.gpsimd
            def _(pool):
                for b in range(1, B):
                    pool.wait_ge(loaded[b], 32)
                    nc.gpsimd.tensor_tensor(num[:, b, :], num[:, b, :], den[:, b, :], ALU.mult).then_inc(ready, 1)

            @block.tensor
            def _(pe):
                pe.wait_ge(begun, 1)
                for t in range(NT):
                    b = t // TB
                    if t == 0:
                        pe.wait_ge(first, 1)
                    elif t % TB == 0:
                        pe.wait_ge(ready, b)
                    ins = nc.tensor.matmul(k.ps[:, t // 4, (t % 4) * P:(t % 4 + 1) * P], num[:, b, (t % TB) * P:(t % TB + 1) * P],
                                           wo[:, b, :], start=True, stop=True)
                    if t % 4 == 3:
                        ins.then_inc(y_ready, 1)


class BiasByDistance:

    def __init__(self, nc, k, c):
        def sb(name, shape):
            return c.enter_context(nc.sbuf_tensor("rb_" + name, shape, F32))

        self.nc, self.k = nc, k
        self.near, self.left, self.right = sb("near", [P, H, NEAR]), sb("left", [P, H]), sb("right", [P, H])
        self.rel, self.top, self.strip = sb("rel", [NBK, H]), sb("top", [H, 1]), sb("strip", [H, STRIP])
        self.rel_in, self.picked, self.top_ready, self.strip_ready, self.strip_out, self.spread = (
            nc.alloc_semaphore("rb_" + n) for n in ("rel_in", "picked", "top", "strip_r", "strip_out", "spread"))

    def load(self, sp, m):
        sp.dma_start(self.rel[:], m["rel_emb"]).then_inc(self.rel_in, 16)

    def spread_out(self, sp):
        dram = self.k.strip_dram
        sp.wait_ge(self.strip_ready, 1)
        sp.dma_start(dram, self.strip[:]).then_inc(self.strip_out, 16)
        sp.wait_ge(self.strip_out, 16)
        sp.dma_start(self.near[:], bass.AP(dram.tensor, 0, [[1, P], [STRIP, H], [1, NEAR]])).then_inc(self.spread, 16)
        sp.dma_start(self.left[:], bass.AP(dram.tensor, STRIP - 1, [[0, P], [STRIP, H]]),
                     allow_slow_non_contiguous=True).then_inc(self.spread, 16)
        sp.dma_start(self.right[:], bass.AP(dram.tensor, 0, [[0, P], [STRIP, H]]),
                     allow_slow_non_contiguous=True).then_inc(self.spread, 16)
        sp.wait_ge(self.spread, 48)

    def pick(self, pe, bank):
        pe.wait_ge(self.rel_in, 16)
        self.nc.tensor.matmul(self.k.ps[0:H, bank, :], self.rel[:], self.k.cst[0:NBK, C_OH:C_OH + STRIP],
                              start=True, stop=True).then_inc(self.picked, 1)

    def largest(self, dve, bank):
        dve.wait_ge(self.picked, 1)
        self.nc.vector.tensor_reduce(self.top[:], self.k.ps[0:H, bank, :], AX.X, ALU.max, negate=True).then_inc(self.top_ready, 1)

    def exps(self, act, bank):
        act.wait_ge(self.top_ready, 1)
        self.nc.scalar.activation(self.strip[:], self.k.ps[0:H, bank, :], ACT.Exp, bias=self.top[:]).then_inc(self.strip_ready, 1)


def biased_attention(nc, k, m, by_distance):
    a = Core()
    a.tag, a.causal = "ba_", False
    a.near, a.left, a.right = by_distance.near, by_distance.left, by_distance.right
    with ExitStack() as c0:
        loads = attention_inputs(nc, m, a, c0)
        normalise(nc, k, "n2", k.x, k.hT, lambda b: k.mod[:, 1, CA, b:b + 1], lambda b: k.mod[:, 1, SA, b:b + 1], loads,
                  measured=NT - CT)
        with ExitStack() as c:
            def sb(name, shape, dt=F32):
                return c.enter_context(nc.sbuf_tensor("ba_" + name, shape, dt))

            a.v = sb("v", [P, NT, H, VA])
            a.qk, a.o = k.qk_dram, k.o_dram
            attend(nc, k, a)
        join_heads(nc, k, m, a, k.x, lambda wo: nc.vector.tensor_tensor(wo[:], wo[:], k.row[:, 1, :, :], ALU.mult))


def modulate(nc, k, tag, src, dst, row_scale, row_shift, loads):
    with ExitStack() as c:
        def sb(name, shape, dt=F32):
            return c.enter_context(nc.sbuf_tensor(tag + name, shape, dt))

        mean, var, rstd, dif, shift = (sb(n, [P, NT]) for n in ("mean", "var", "rstd", "dif", "shift"))
        var_ready, sd_ready, chain, rstd_ready, dve_plain, scaled, last_scaled = (
            nc.alloc_semaphore(tag + n) for n in ("var_r", "sd", "chain", "rstd", "dve_plain", "scaled", "last_scaled"))
        act_plain = [nc.alloc_semaphore(tag + f"act_plain{b}") for b in range(B)]

        def to_rows(eng, b, op, rows):
            d = dst[:, b * TB:(b + 1) * TB, :]
            return eng.tensor_tensor(d, d, rows[:, b:b + 1, :].broadcast_to([P, TB, D]), op)

        with nc.Block() as block:
            block.sync(loads)

            @block.vector
            def _(dve):
                ch = Chain(dve, chain)
                combine(nc, k, ch, mean, var, dif, var_ready)
                scales(nc, dve, ch, var, mean, rstd, shift, sd_ready, rstd_ready)
                for b in range(B - 1):
                    for t in range(b * TB, b * TB + TB // 2):
                        nc.vector.tensor_scalar(dst[:, t, :], src[:, t, :], col(mean, t), col(rstd, t),
                                                ALU.subtract, ALU.mult).then_inc(dve_plain, 1)
                    dve.wait_ge(dve_plain, (b + 1) * TB // 2)
                    dve.wait_ge(act_plain[b], 1)
                    to_rows(nc.vector, b, ALU.mult, row_scale).then_inc(scaled, 1)
                    dve.wait_ge(scaled, b + 1)
                    to_rows(nc.vector, b, ALU.add, row_shift)

            @block.gpsimd
            def _(pool):
                pool.wait_ge(act_plain[B - 1], 1)
                to_rows(nc.gpsimd, B - 1, ALU.mult, row_scale).then_inc(last_scaled, 1)
                pool.wait_ge(last_scaled, 1)
                to_rows(nc.gpsimd, B - 1, ALU.add, row_shift)

            @block.scalar
            def _(act):
                act.wait_ge(var_ready, 1)
                nc.scalar.activation(var[:], var[:], ACT.Sqrt).then_inc(sd_ready, 1)
                act.wait_ge(rstd_ready, 1)
                for b in (*range(B - 2), B - 1, B - 2):
                    for t in range(b * TB + (0 if b == B - 1 else TB // 2), (b + 1) * TB):
                        ins = nc.scalar.activation(dst[:, t, :], src[:, t, :], ACT.Identity, bias=col(shift, t),
                                                   scale=col(rstd, t))
                    ins.then_inc(act_plain[b], 1)


def route(nc, k, m, r):
    with ExitStack() as c:
        def sb(name, shape, dt=F32):
            return c.enter_context(nc.sbuf_tensor("ro_" + name, shape, dt))

        wr, trash, ids = r.wr, r.trash, r.ids
        mean, var, rstd, dif, shift = (sb(n, [P, NT]) for n in ("mean", "var", "rstd", "dif", "shift"))
        var_ready, sd_ready, rstd_ready, dve_plain, act_plain = (
            nc.alloc_semaphore("ro_" + n) for n in ("var_r", "sd", "rstd", "dve_plain", "act_plain"))
        lg, ex, l2, c1, slot, slots = (sb(n, [P, NT, E]) for n in ("lg", "ex", "l2", "c1", "slot", "slots"))
        pick = sb("pick", [P, 2, NT, E])
        pickb = sb("pickb", [P, 2, NT, E], BF16)
        tot = sb("tot", [P, 2, E, NT])
        inc = sb("inc", [P, 2, E, NT])
        keep1 = sb("keep1", [P, E, NT])
        col1, col2 = (sb(n, [P, NT]) for n in ("col1", "col2"))
        kept = sb("kept", [P, 2, NT])
        row = sb("row", [P, 2, NT])
        onesb = sb("onesb", [P, P], BF16)
        loaded = r.route_in
        logits, e_ready, chain, ch_ready, counts, turned, moved = (
            nc.alloc_semaphore("ro_" + n) for n in
            ("logits", "e_ready", "chain", "ch_ready", "counts", "turned", "moved"))
        ex_go, to_ready, ids_set = (nc.alloc_semaphore("ro_" + n) for n in ("ex_go", "to_ready", "ids_set"))

        def v(t):
            return t[:].unsqueeze(2).broadcast_to([P, NT, E])

        def const(at):
            return k.cst[:, at:at + E].unsqueeze(1).broadcast_to([P, NT, E])

        def flat(t):
            return t[:].rearrange("p t e -> p (t e)")

        with nc.Block() as block:
            block.sync(r.loads)

            @block.tensor
            def _(pe):
                def turn(i):
                    if i >= 2:
                        pe.wait_ge(moved, i - 1)
                    for j in range(4):
                        t = 4 * i + j
                        pe.wait_ge((dve_plain, act_plain)[t % 2], t // 2 + 1)
                        ins = nc.tensor.transpose(k.ps[:, i % 2, j * P:(j + 1) * P], r.xt[:, 0, t, 0:D], k.cst[:, C_ID:C_ID + P])
                    ins.then_inc(turned, 1)

                turn(0)
                pe.wait_ge(loaded, 48)
                for i in range(NCH):
                    if i + 1 < NCH:
                        turn(i + 1)
                    pe.wait_ge(moved, i + 1)
                    for t in range(4 * i, 4 * i + 4):
                        ins = nc.tensor.matmul(k.ps[:, 2, t * E:(t + 1) * E], k.hT[:, t * P:(t + 1) * P], wr[:], start=True, stop=True)
                ins.then_inc(logits, 1)
                for i in range(2):
                    pe.wait_ge(ch_ready, i + 1)
                    one = pickb[:, i, :, :].rearrange("p t e -> p (t e)")
                    nc.tensor.matmul(k.ps[:, 3 + i, :], k.cstb[:, C_TRI:C_TRI + P], one, start=True, stop=True)
                    ins = nc.tensor.matmul(k.ps[:, 5 + i, :], onesb[:], one, start=True, stop=True)
                    ins.then_inc(counts, 1)

            @block.scalar
            def _(act):
                act.wait_ge(var_ready, 1)
                nc.scalar.activation(var[:], var[:], ACT.Sqrt).then_inc(sd_ready, 1)
                act.wait_ge(rstd_ready, 1)
                for i in range(NCH + 1):
                    if i < NCH:
                        for t in range(4 * i + 1, 4 * i + 4, 2):
                            nc.scalar.activation(r.xt[:, 0, t, 0:D], r.hidden[:, t, :], ACT.Identity, bias=col(shift, t),
                                                 scale=col(rstd, t)).then_inc(act_plain, 1)
                    if i:
                        act.wait_ge(turned, i)
                        nc.scalar.activation(k.hT[:, (i - 1) * CH:i * CH], k.ps[:, (i - 1) % 2, :], ACT.Identity,
                                             bias=r.ln2[:, 1:2], scale=r.ln2[:, 0:1]).then_inc(moved, 1)
                act.wait_ge(ex_go, 1)
                nc.scalar.activation(ex[:], lg[:], ACT.Exp).then_inc(e_ready, 1)
                act.wait_ge(dve_plain, NT // 2)
                act.wait_ge(act_plain, NT // 2)
                for b in range(B):
                    ts = slice(b * TB, (b + 1) * TB)
                    nc.scalar.copy(r.xt[:, 1, ts, 0:D], r.xt[:, 0, ts, 0:D])

            @block.gpsimd
            def _(pool):
                pool.wait_ge(loaded, 48)
                for i in range(2):
                    nc.gpsimd.tensor_copy(r.xt[:, i, :, D:D + 1].bitcast(I32), ids[:, i, :].unsqueeze(2)).then_inc(ids_set, 1)
                pool.wait_ge(ids_set, 2)
                pool.wait_ge(to_ready, 1)
                pool.wait_ge(dve_plain, NT // 2)
                pool.wait_ge(act_plain, NT // 2)
                send_copies(nc, k, r, 0)

            @block.vector
            def _(dve):
                ch = Chain(dve, chain)
                L_, vec = ch.link, nc.vector
                combine(nc, k, ch, mean, var, dif, var_ready)
                scales(nc, dve, ch, var, mean, rstd, shift, sd_ready, rstd_ready)
                for t in range(0, NT, 2):
                    vec.tensor_scalar(r.xt[:, 0, t, 0:D], r.hidden[:, t, :], col(mean, t), col(rstd, t),
                                      ALU.subtract, ALU.mult).then_inc(dve_plain, 1)
                L_(vec.memset(onesb[:], 1.0))
                L_(vec.tensor_copy(slots[:], const(C_SLOT)))
                L_(vec.memset(keep1[:], 1.0))
                L_(vec.memset(keep1[:, :, 0:1], 0.0))
                dve.wait_ge(loaded, 48)
                dve.wait_ge(logits, 1)
                raw = k.ps[:, 2, :].rearrange("p (t e) -> p t e", e=E)
                L_(vec.tensor_reduce(col1[:], raw, AX.X, ALU.max))
                vec.tensor_tensor(lg[:], raw, v(col1), ALU.subtract).then_inc(ex_go, 1)
                dve.wait_ge(e_ready, 1)
                L_(vec.tensor_reduce(col1[:], ex[:], AX.X, ALU.add))
                L_(vec.reciprocal(col1[:], col1[:]))
                L_(vec.tensor_tensor(ex[:], ex[:], v(col1), ALU.mult))

                def first_of(values, i):
                    L_(vec.tensor_reduce(col1[:], values, AX.X, ALU.max))
                    L_(vec.tensor_tensor(c1[:], values, v(col1), ALU.is_equal))
                    L_(vec.tensor_tensor(c1[:], c1[:], const(C_FIRST), ALU.mult))
                    L_(vec.tensor_reduce(col1[:], c1[:], AX.X, ALU.max))
                    L_(vec.tensor_tensor(pick[:, i, :, :], c1[:], v(col1), ALU.is_equal))

                first_of(ex[:], 0)
                vec.tensor_copy(pickb[:, 0, :, :], pick[:, 0, :, :]).then_inc(ch_ready, 1)
                for i in range(2):
                    if i:
                        L_(vec.scalar_tensor_tensor(l2[:].rearrange("p t e -> p (t e)"), pick[:, 0, :, :].rearrange("p t e -> p (t e)"),
                                                    NEG, lg[:].rearrange("p t e -> p (t e)"), ALU.mult, ALU.add))
                        first_of(l2[:], 1)
                        vec.tensor_copy(pickb[:, 1, :, :], pick[:, 1, :, :]).then_inc(ch_ready, 1)
                    dve.wait_ge(counts, i + 1)
                    L_(vec.tensor_copy(tot[:, i, :, :], k.ps[:, 5 + i, :].rearrange("p (t e) -> p e t", e=E)))
                    L_(vec.tensor_tensor_scan(inc[:, i, :, :].rearrange("p e t -> p (e t)"), keep1[:].rearrange("p e t -> p (e t)"),
                                              tot[:, i, :, :].rearrange("p e t -> p (e t)"), 0.0, ALU.mult, ALU.add))
                    L_(vec.tensor_tensor(c1[:], inc[:, i, :, :].rearrange("p e t -> p t e"), tot[:, i, :, :].rearrange("p e t -> p t e"), ALU.subtract))
                    L_(vec.tensor_tensor(c1[:], c1[:], k.ps[:, 3 + i, :].rearrange("p (t e) -> p t e", e=E), ALU.add))
                    if i:
                        L_(vec.tensor_tensor(c1[:], c1[:], inc[:, 0, :, NT - 1:NT].rearrange("p e a -> p a e").broadcast_to([P, NT, E]), ALU.add))
                    L_(vec.scalar_tensor_tensor(flat(l2), flat(c1), float(CAP) + 1.0, pick[:, i, :, :].rearrange("p t e -> p (t e)"),
                                                ALU.is_lt, ALU.mult))
                    L_(vec.scalar_tensor_tensor(flat(slot), flat(c1), -1.0, flat(slots), ALU.add, ALU.add))
                    L_(vec.tensor_tensor(slot[:], slot[:], l2[:], ALU.mult))
                    L_(vec.tensor_reduce(row[:, i, :], slot[:], AX.X, ALU.add))
                    L_(vec.tensor_reduce(kept[:, i, :], l2[:], AX.X, ALU.add))
                    L_(vec.tensor_scalar(kept[:, i, :], kept[:, i, :], -1.0, 1.0, ALU.mult, ALU.add))
                    L_(vec.tensor_tensor(kept[:, i, :], kept[:, i, :], trash[:, i, :], ALU.mult))
                    L_(vec.tensor_tensor(row[:, i, :], row[:, i, :], kept[:, i, :], ALU.add))
                    vec.tensor_copy(r.to[:, i, :], row[:, i, :]).then_inc(to_ready, 1)
                    L_(vec.tensor_tensor(slot[:], ex[:], l2[:], ALU.mult))
                    L_(vec.tensor_reduce(r.g[:, i, :], slot[:], AX.X, ALU.add))
                L_(vec.tensor_tensor(col1[:], r.g[:, 0, :], r.g[:, 1, :], ALU.add))
                L_(vec.tensor_scalar(col1[:], col1[:], 1.1920929e-07, None, ALU.max))
                L_(vec.reciprocal(col2[:], col1[:]))
                L_(vec.tensor_scalar(col2[:], col2[:], KEEP, None, ALU.mult))
                vec.tensor_tensor(r.g[:], r.g[:], col2[:].unsqueeze(1).broadcast_to([P, 2, NT]), ALU.mult)


def send_copies(nc, k, r, i):
    for t in range(NT):
        nc.gpsimd.indirect_dma_start(k.rows_in, bass.IndirectOffsetOnAxis(ap=r.to[:, i, t:t + 1], axis=0),
                                     r.xt[:, i, t, :], None).then_inc(r.sent, 16)


def load_first(sp, m, r, e, s):
    sp.dma_start(r.fc1[:, s, :], m["fc1_w"][e]).then_inc(r.first_in[s], 16)


def load_second(sp, m, r, e, s):
    sp.dma_start(r.fc2[:, s, :, :], m["fc2_w"][e]).then_inc(r.second_in[s], 16)


def experts(nc, k, m, r):
    QT, FB = CAP // P, FF // P
    with ExitStack() as c:
        def sb(name, shape, dt=F32):
            return c.enter_context(nc.sbuf_tensor("ex_" + name, shape, dt))

        fc1, fc2, b1, b2 = r.fc1, r.fc2, r.b1, r.b2
        xi = sb("xi", [P, 2, QT, D + 1])
        to = sb("to", [P, E, QT, 1], I32)
        xT = sb("xT", [P, 2, CAP])
        hh = sb("hh", [P, 2, FB, CAP])
        eo = sb("eo", [P, 2, QT, D])
        back = k.qop[:].rearrange("p g a n -> p (g a n)").bitcast(F32).rearrange("p (i n j d) -> p i n j d", i=2, n=4, j=4)
        consts_in = r.consts_in
        turned, xT_ready, up, act_done, down, eo_ready = (
            nc.alloc_semaphore("ex_" + n) for n in
            ("turned", "xT_ready", "up", "act_done", "down", "eo_ready"))
        x_in = [nc.alloc_semaphore(f"ex_x_in{s}") for s in range(2)]
        eo_out = [nc.alloc_semaphore(f"ex_eo_out{s}") for s in range(2)]
        got = [nc.alloc_semaphore(f"ex_got{s}") for s in range(4)]
        first, both, gated, summed, x_plain, ids_kept, x_stored = (
            nc.alloc_semaphore("ex_" + n) for n in ("first", "both", "gated", "summed", "x_plain", "ids_kept", "x_stored"))
        chain = nc.alloc_semaphore("ex_chain")

        with nc.Block() as block:
            @block.gpsimd
            def _(pool):
                send_copies(nc, k, r, 1)
                for e in range(E):
                    pool.wait_ge(eo_ready, e + 1)
                    for q in range(QT):
                        nc.gpsimd.indirect_dma_start(k.rows_out, bass.IndirectOffsetOnAxis(ap=to[:, e, q, :], axis=0),
                                                     eo[:, e % 2, q, :], None).then_inc(eo_out[e % 2], 16)
                for n in range(NCH):
                    pool.wait_ge(both, 4 * (n + 1))
                    y = back[:, 1, n % 4, :, :]
                    b = n * CH // L
                    nc.gpsimd.tensor_tensor(y, y, k.row[:, 2, b:b + 1, :].broadcast_to([P, 4, D]), ALU.mult).then_inc(gated, 1)

            @block.sync
            def _(sp):
                def rows(e, s):
                    sp.dma_start(xi[:, s, :, :], k.rows_in[bass.ds(e * CAP, CAP), :].rearrange("(q p) d -> p q d", p=P)).then_inc(x_in[s], 16)

                sp.wait_ge(r.sent, NT * 2 * 16)
                rows(0, 0)
                rows(1, 1)

                def first_half(e, s):
                    sp.wait_ge(xT_ready, e + 1)
                    rows(e + 2, s)
                    sp.wait_ge(up, (e + 1) * FB)
                    load_first(sp, m, r, e + 2, s)

                def second_half(e, s):
                    sp.wait_ge(down, e)
                    load_second(sp, m, r, e + 1, s)

                first_half(0, 0)
                with sp.Fori(0, (E - 4) // 2) as i:
                    first_half(2 * i + 1, 1)
                    second_half(2 * i + 1, 0)
                    first_half(2 * i + 2, 0)
                    second_half(2 * i + 2, 1)
                first_half(E - 3, 1)
                second_half(E - 3, 0)
                second_half(E - 2, 1)
                for s in range(2):
                    sp.wait_ge(eo_out[s], E // 2 * QT * 16)
                for n in range(NCH):
                    if n >= 4:
                        sp.wait_ge(summed, n - 3)
                    for i in range(2):
                        sp.dma_start(back[:, i, n % 4, :, :], k.rows_out[i * TOK + n * CH:i * TOK + (n + 1) * CH, :]
                                     .rearrange("(j p) d -> p j d", p=P)).then_inc(got[n % 4], 16)
                x_out = m["out"].rearrange("b (t p) d -> p (b t) d", p=P)
                for n in range(NCH):
                    sp.wait_ge(summed, n + 1)
                    sp.dma_start(x_out[:, 4 * n:4 * n + 4, :], k.x[:, 4 * n:4 * n + 4, :]).then_inc(x_stored, 16)
                sp.wait_ge(x_stored, NCH * 16)

            @block.tensor
            def _(pe):
                def turn(e, s, n):
                    pe.wait_ge(x_in[s], 16 * n)
                    if not (isinstance(e, int) and e < 2):
                        pe.wait_ge(xT_ready, e - 1)
                    for q in range(QT):
                        ins = nc.tensor.transpose(k.ps[:, s, q * P:(q + 1) * P], xi[:, s, q, 0:D], k.cst[:, C_ID:C_ID + P])
                    ins.then_inc(turned, 1)

                def upper(e, s, n):
                    pe.wait_ge(r.first_in[s], 16 * n)
                    pe.wait_ge(xT_ready, e + 1)
                    for f in range(FB):
                        if not (isinstance(e, int) and e == 0):
                            pe.wait_ge(act_done, e * FB + f - (FB - 1))
                        nc.tensor.matmul(k.ps[:, 2 + f, :], fc1[:, s, f * P:(f + 1) * P], xT[:, s, :], start=True, stop=True).then_inc(up, 1)

                def lower(e, s, n):
                    pe.wait_ge(r.second_in[s], 16 * n)
                    pe.wait_ge(act_done, (e + 1) * FB)
                    if not (isinstance(e, int) and e < 2):
                        pe.wait_ge(eo_ready, e - 1)
                    for q in range(QT):
                        for f in range(FB):
                            ins = nc.tensor.matmul(k.ps[:, 6 + s, q * P:(q + 1) * P], hh[:, s, f, q * P:(q + 1) * P], fc2[:, s, f, :],
                                                   start=(f == 0), stop=(f == FB - 1))
                    ins.then_inc(down, 1)

                turn(0, 0, 1)
                turn(1, 1, 1)
                upper(0, 0, 1)
                turn(2, 0, 2)
                upper(1, 1, 1)
                lower(0, 0, 1)
                with pe.Fori(1, E // 2 - 1) as i:
                    turn(2 * i + 1, 1, i + 1)
                    upper(2 * i, 0, i + 1)
                    lower(2 * i - 1, 1, i)
                    turn(2 * i + 2, 0, i + 2)
                    upper(2 * i + 1, 1, i + 1)
                    lower(2 * i, 0, i + 1)
                turn(E - 1, 1, E // 2)
                upper(E - 2, 0, E // 2)
                lower(E - 3, 1, E // 2 - 1)
                upper(E - 1, 1, E // 2)
                lower(E - 2, 0, E // 2)
                lower(E - 1, 1, E // 2)

            @block.scalar
            def _(act):
                act.wait_ge(consts_in, 32)

                def gelus(e, s, first=False):
                    for f in range(FB):
                        act.wait_ge(up, e * FB + f + 1)
                        if f == 0 and not first:
                            act.wait_ge(down, e - 1)
                        bias = b1[:, e, f:f + 1] if isinstance(e, int) else b1[:, bass.ds(e, 1), f]
                        nc.scalar.activation(hh[:, s, f, :], k.ps[:, 2 + f, :], ACT.Gelu, bias=bias).then_inc(act_done, 1)

                gelus(0, 0, True)
                gelus(1, 1, True)
                with act.Fori(1, E // 2) as i:
                    gelus(2 * i, 0)
                    gelus(2 * i + 1, 1)
                for t in range(NT):
                    n = t // 4
                    if t % 4 == 0:
                        act.wait_ge(got[n % 4], (n // 4 + 1) * 2 * 16)
                    y1 = back[:, 0, n % 4, t % 4, :]
                    nc.scalar.activation(y1, y1, ACT.Copy, scale=r.g[:, 0, t:t + 1]).then_inc(first, 1)

            @block.vector
            def _(dve):
                for b in range(B):
                    h = r.hidden[:, b * TB:(b + 1) * TB, :]
                    xs = k.x[:, b * TB:(b + 1) * TB, :]
                    nc.vector.tensor_tensor(h, h, k.row[:, 2, b:b + 1, :].broadcast_to([P, TB, D]), ALU.mult).then_inc(chain, 1)
                    dve.wait_ge(chain, b + 1)
                    nc.vector.tensor_tensor(xs, xs, h, ALU.add).then_inc(x_plain, 1)
                dve.wait_ge(consts_in, 32)

                def turned_in(e, s, n):
                    dve.wait_ge(turned, e + 1)
                    if not (isinstance(e, int) and e < 2):
                        dve.wait_ge(up, (e - 1) * FB)
                    dve.wait_ge(x_in[s], 16 * n)
                    nc.vector.tensor_copy(to[:, bass.ds(e, 1), :, :].rearrange("p a q b -> p (a q) b"), xi[:, s, :, D:D + 1].bitcast(I32)).then_inc(ids_kept, 1)
                    dve.wait_ge(ids_kept, e + 1)
                    nc.vector.tensor_scalar(xT[:, s, :], k.ps[:, s, :], r.ln2[:, 0:1], r.ln2[:, 1:2], ALU.mult, ALU.add).then_inc(xT_ready, 1)

                def out(e, s, n):
                    dve.wait_ge(down, e + 1)
                    if not (isinstance(n, int) and n == 0):
                        dve.wait_ge(eo_out[s], QT * 16 * n)
                    row = b2[:, bass.ds(e, 1), :].broadcast_to([P, QT, D])
                    nc.vector.tensor_tensor(eo[:, s, :, :], k.ps[:, 6 + s, :].rearrange("p (q d) -> p q d", d=D), row, ALU.add).then_inc(eo_ready, 1)

                def pair(i):
                    turned_in(2 * i + 1, 1, i + 1)
                    out(2 * i - 1, 1, i - 1)
                    turned_in(2 * i + 2, 0, i + 2)
                    out(2 * i, 0, i)

                def add(n):
                    xs = k.x[:, 4 * n:4 * n + 4, :]
                    dve.wait_ge(gated, n + 1)
                    dve.wait_ge(x_plain, B)
                    nc.vector.tensor_tensor(xs, xs, back[:, 1, n % 4, :, :], ALU.add).then_inc(summed, 1)

                turned_in(0, 0, 1)
                turned_in(1, 1, 1)
                turned_in(2, 0, 2)
                out(0, 0, 0)
                pair(1)
                with dve.Fori(2, E // 2 - 1) as i:
                    pair(i)
                turned_in(E - 1, 1, E // 2)
                out(E - 3, 1, E // 2 - 2)
                out(E - 2, 0, E // 2 - 1)
                out(E - 1, 1, E // 2 - 1)
                for t in range(NT):
                    dve.wait_ge(first, t + 1)
                    y1, y2 = back[:, 0, t // 4 % 4, t % 4, :], back[:, 1, t // 4 % 4, t % 4, :]
                    nc.vector.scalar_tensor_tensor(y2, y2, r.g[:, 1, t:t + 1], y1, ALU.mult, ALU.add).then_inc(both, 1)
                    if t % 4 == 3 and t >= 7:
                        add(t // 4 - 1)
                add(NCH - 1)


def causal_sublayer(nc, k, m):
    a = Core()
    a.tag, a.causal = "ca_", True
    r = Core()
    with ExitStack() as c:
        def sb(name, shape, dt=F32):
            return c.enter_context(nc.sbuf_tensor("cs_" + name, shape, dt))

        h = sb("h", [P, NT, D])
        ln1 = sb("ln1", [P, 2])
        r.ln2 = sb("ln2", [P, 2])
        a.ob = sb("ob", [P, 1, D])
        ln_in = nc.alloc_semaphore("cs_ln_in")
        attention_loads = attention_inputs(nc, m, a, c)

        def norm_loads(sp):
            sp.dma_start(ln1[:], m["ln1"]).then_inc(ln_in, 16)
            sp.dma_start(r.ln2[:], m["ln2"]).then_inc(ln_in, 16)

        modulate(nc, k, "m3", k.x, h, k.row[:, 3], k.row[:, 4], norm_loads)
        with nc.Block() as block:
            @block.sync
            def _(sp):
                sp.wait_ge(ln_in, 32)
        normalise(nc, k, "n4", h, k.hT, lambda b: ln1[:, 0:1], lambda b: ln1[:, 1:2], attention_loads)
        with ExitStack() as c2:
            a.v = c2.enter_context(nc.sbuf_tensor("ca_v", [P, NT, H, VA], F32))
            a.qk, a.o = k.qk_dram, k.o_dram
            with nc.cleanup_on_exit():
                attend(nc, k, a)
        join_heads(nc, k, m, a, h, lambda wo: nc.vector.tensor_tensor(h[:], h[:], a.ob[:].broadcast_to([P, NT, D]), ALU.add))
        r.hidden = h
        r.xt = sb("xt", [P, 2, NT, D + 1])
        r.to = sb("to", [P, 2, NT], I32)
        r.sent = nc.alloc_semaphore("cs_sent")
        r.g = sb("g", [P, 2, NT])
        r.wr, r.trash, r.ids = sb("wr", [P, E]), sb("trash", [P, 2, NT]), sb("ids", [P, 2, NT], I32)
        r.fc1, r.fc2 = sb("fc1", [P, 2, FF]), sb("fc2", [P, 2, FF // P, D])
        r.b1, r.b2 = sb("b1", [P, E, FF // P]), sb("b2", [P, E, D])
        r.route_in, r.consts_in = nc.alloc_semaphore("cs_route_in"), nc.alloc_semaphore("cs_consts_in")
        r.first_in, r.second_in = ([nc.alloc_semaphore(f"cs_{n}_in{s}") for s in range(2)] for n in ("first", "second"))

        def route_loads(sp):
            sp.dma_start(r.wr[:], m["router_w"]).then_inc(r.route_in, 16)
            sp.dma_start(r.trash[:], m["trash_rows"]).then_inc(r.route_in, 16)
            sp.dma_start(r.ids[:], m["result_rows"]).then_inc(r.route_in, 16)
            sp.dma_start(r.b1[:], m["fc1_b"]).then_inc(r.consts_in, 16)
            sp.dma_start(r.b2[:], m["fc2_b"].broadcast_to([P, E, D])).then_inc(r.consts_in, 16)
            for s in range(2):
                load_first(sp, m, r, s, s)
                load_second(sp, m, r, s, s)

        r.loads = route_loads
        route(nc, k, m, r)
        experts(nc, k, m, r)





def program(nc, m):
    with ExitStack() as c:
        def sb(name, shape, dt=F32):
            return c.enter_context(nc.sbuf_tensor(name, shape, dt))

        k = Core()
        k.ps = c.enter_context(nc.psum_tensor("ps", [P, 8, CH], F32))
        k.x = sb("x_tok", [P, NT, D])
        k.hT = sb("hT", [P, TOK])
        k.cst = sb("cst", [P, C_W])
        k.cstb = sb("cstb", [P, C_FIRST], BF16)
        k.ones = sb("ones", [P, P])
        k.stats = sb("stats", [P, NT, 6])
        k.mod = sb("mod", [P, 2, 6, B])
        k.qop = sb("qop", [P, NG, 2, L], BF16)
        k.kop = sb("kop", [P, NG, HG, L], BF16)
        k.row0 = sb("row0", [1, L], BF16)
        k.row_of = [(0, GA), (1, GA), (1, GB), (1, CB), (1, SB), (0, GB)]
        k.row = sb("row", [P, len(k.row_of), B, D])
        k.qk_dram = nc.dram_tensor("qk_parts", (2, H, 3, HD, TOK), BF16).ap()
        k.o_dram = nc.dram_tensor("head_sums", (B, H, VA, L), F32).ap()
        k.strip_dram = nc.dram_tensor("bias_strip", (H, STRIP), F32).ap()
        k.rows_in = nc.dram_tensor("expert_rows_in", (E * CAP + 2 * TOK, D + 1), F32).ap()
        k.rows_out = nc.dram_tensor("expert_rows_out", (2 * TOK + E * CAP, D), F32).ap()
        load_and_modulate(nc, k, m)
        scan_sublayer(nc, k, m)
        with ExitStack() as c2:
            by_distance = BiasByDistance(nc, k, c2)
            first_mixture(nc, k, m, by_distance)
            with nc.cleanup_on_exit():
                biased_attention(nc, k, m, by_distance)
        with nc.cleanup_on_exit():
            causal_sublayer(nc, k, m)


def constants():
    import numpy as np

    a = np.zeros((P, C_W), np.float32)
    i = np.arange(P)
    a[i, C_ID + i] = 1.0
    a[i, C_FLIP + P - 1 - i] = 1.0
    a[:, C_TRI:C_TRI + P] = i[:, None] <= i[None, :]
    a[:, C_MA:C_MA + P] = np.where(i[None, :] > i[:, None], NEG, 0.0)
    a[:, C_MB:C_MB + P] = np.where(i[None, :] < i[:, None], NEG, 0.0)
    a[:, C_FIRST:C_FIRST + E] = E - np.arange(E)
    a[:, C_SLOT:C_SLOT + E] = CAP * np.arange(E)
    edges = np.array([1, 2, 3, 4, 5, 6, 7, 11, 15, 21, 30, 44, 62, 90, 128])
    rel = 255 - np.arange(STRIP)
    bucket = (np.abs(rel)[:, None] >= edges[None, :]).sum(1) + 16 * (rel > 0)
    a[bucket, C_OH + np.arange(STRIP)] = 1.0
    return a


def layouts(i):
    import numpy as np

    def c(a):
        return np.ascontiguousarray(a)

    i = {n: np.asarray(a) for n, a in i.items()}
    d = {"consts": constants(), "x": c(i["L0_attn_x"]), "c0T": c(i["L0_c"].T), "c1T": c(i["L1_c"].T),
         "L0_wmod": c(i["L0_wmod"]), "L1_wmod": c(i["L1_wmod"])}
    wx = i["L0_attn_Wxproj"]
    wp = np.zeros((D, 3, SP), np.float32)
    wp[:, 0, :NST] = wx[RANK:RANK + NST].T
    wp[:, 1, :NST] = wx[RANK + NST:].T
    wp[:, 2, :NST] = i["L0_attn_Wxs"].T
    d["ssm_wp"], d["ssm_wx"] = wp, c(wx[:RANK])
    d["ssm_wdt"] = c(np.repeat(i["L0_attn_Wdt"].T, SP, axis=1))
    col = np.zeros((P, 3), np.float32)
    wout = np.zeros((P, B, D), np.float32)
    for b in range(B):
        col[SP * b:SP * b + NST, 0] = i["L0_attn_A_log"][0]
        wout[SP * b:SP * b + NST, b] = i["L0_attn_Wout"].T
    col[:, 1] = i["L0_attn_bdt"][0]
    col[:, 2] = i["L0_attn_Dp"]
    d["ssm_col"], d["ssm_wout"] = col, wout
    d["gate_w"] = c(i["L0_ffn_Wg"].T)
    d["ffn_w1"] = c(i["L0_ffn_W1"].transpose(2, 0, 1))
    d["ffn_w3"] = c(i["L0_ffn_W3"].transpose(2, 0, 1))
    d["ffn_w2"] = c(i["L0_ffn_W2"].transpose(2, 0, 1))
    d["ffn_bias"] = c(np.stack([i["L0_ffn_b1"].T, i["L0_ffn_b3"].T], axis=1))
    d["ffn_b2"] = c(i["L0_ffn_b2"])
    d["ba_w"] = c(np.stack([i["L1_attn_W" + n].T for n in "qkv"], axis=1))
    d["ba_bias"] = np.zeros((P, 2), np.float32)
    d["ba_vb"] = np.zeros((1, D), np.float32)
    d["ba_wo"] = c(i["L1_attn_Wo"].T)
    d["rel_emb"] = c(i["L1_attn_rel_emb"])
    d["ln1"] = c(np.stack([i["L1_ffn_ln1_w"], i["L1_ffn_ln1_b"]], axis=1))
    d["ln2"] = c(np.stack([i["L1_ffn_ln2_w"], i["L1_ffn_ln2_b"]], axis=1))
    d["ca_w"] = c(np.stack([i["L1_ffn_" + n + "_w"] for n in "qkv"], axis=1))
    d["ca_bias"] = c(np.stack([i["L1_ffn_q_b"], i["L1_ffn_k_b"]], axis=1))
    d["ca_vb"] = c(i["L1_ffn_v_b"]).reshape(1, D)
    d["ca_wo"] = c(i["L1_ffn_o_w"])
    d["ca_ob"] = c(i["L1_ffn_o_b"]).reshape(1, D)
    d["router_w"] = c(i["L1_ffn_router_w"])
    d["trash_rows"] = (E * CAP + np.arange(2)[None, :, None] * TOK + np.arange(NT)[None, None, :] * P
                       + np.arange(P)[:, None, None]).astype(np.float32)
    d["result_rows"] = (np.arange(2)[None, :, None] * TOK + np.arange(NT)[None, None, :] * P
                        + np.arange(P)[:, None, None]).astype(np.int32)
    d["unused_rows"] = (2 * TOK + np.arange(E * CAP)).reshape(P, E * CAP // P).astype(np.int32)
    d["fc1_w"] = c(i["L1_ffn_fc1_w"])
    d["fc2_w"] = c(i["L1_ffn_fc2_w"].reshape(E, FF // P, P, D).transpose(0, 2, 1, 3))
    d["fc1_b"] = c(i["L1_ffn_fc1_b"].reshape(E, FF // P, P).transpose(2, 0, 1))
    d["fc2_b"] = c(i["L1_ffn_fc2_b"]).reshape(1, E, D)
    return d


def kernel(**inputs):
    import concourse.bacc as _bacc
    from concourse import mybir as _mybir
    from concourse.bass_utils import run_bass_kernel_spmd as _run

    nc = _bacc.Bacc("TRN2", target_bir_lowering=False, num_devices=1)
    arrays = layouts(inputs)
    m = {n: nc.dram_tensor("in_" + n, a.shape, _mybir.dt.from_np(a.dtype), kind="ExternalInput").ap()
         for n, a in arrays.items()}
    m["out"] = nc.dram_tensor("out_x", (B, L, D), F32, kind="ExternalOutput").ap()
    program(nc, m)
    r = _run(nc, [{"in_" + n: a for n, a in arrays.items()}], core_ids=[0])
    return r.results[0]["out_x"]
```
